# Optimizing a Trainium2 kernel written in Bass

```python
import numpy as np
import jax
import jax.numpy as jnp

def _softmax(x, axis=-1):
    return jax.nn.softmax(x, axis=axis)

def _gelu(x):
    return jax.nn.gelu(x, approximate=True)

def _silu(x):
    return jax.nn.silu(x)

def _sigmoid(x):
    return jax.nn.sigmoid(x)

def _layernorm(x, axis=-1, eps=1e-05):
    m = jnp.mean(x, axis=axis, keepdims=True)
    v = jnp.var(x, axis=axis, keepdims=True)
    return (x - m) / jnp.sqrt(v + eps)

def _scatter_add(tgt, idx, src, axis=0):
    return tgt.at[idx].add(src)

def _segment_sum(src, seg, n):
    return jax.ops.segment_sum(src, seg, n)
kernel_name = 'mk_gnn_preln_d2_gnn_r32_03bb27'

def setup_inputs(seed: int=0):
    np.random.seed(seed)
    _w = jnp.asarray

    def _rec_inputs():
        import jax
        import jax.numpy as jnp
        _gk = jax.random.key(seed)
        x = -0.0002117 + 1 * jax.random.normal(jax.random.fold_in(_gk, 1), (3125, 256), jnp.float32)
        src = jax.random.randint(jax.random.fold_in(_gk, 2), (50000,), 0, 3125, jnp.int32)
        dst = jnp.minimum((3125 * jax.random.uniform(jax.random.fold_in(_gk, 3), (50000,)) ** 2.0).astype(jnp.int32), 99999)
        _o = jnp.argsort(dst, stable=True)
        src = src[_o]
        dst = dst[_o]
        edge_weight = jax.random.uniform(jax.random.fold_in(_gk, 13), (50000,), jnp.float32, 0.0, 1)
        return (x, src, dst, edge_weight)
    x, src, dst, edge_weight = _rec_inputs()

    def _L0_gnn_setup():
        import jax, jax.numpy as jnp
        import numpy as np
        N_NODES = 3125
        N_EDGES = 100000
        D_IN = 256
        D_OUT = 256
        key = jax.random.key(seed)
        k1, k2, k3, k4, k5, k6 = jax.random.split(key, 6)
        X = jax.random.normal(k1, (N_NODES, D_IN), dtype=jnp.float32)
        edge_src = jax.random.randint(k2, (N_EDGES,), 0, N_NODES, dtype=jnp.int32)
        edge_dst = jax.random.randint(k3, (N_EDGES,), 0, N_NODES, dtype=jnp.int32)
        edge_val = jax.random.uniform(k4, (N_EDGES,), dtype=jnp.float32)
        stdv = 1.0 / np.sqrt(D_OUT)
        W = jax.random.uniform(k5, (D_IN, D_OUT), minval=-stdv, maxval=stdv, dtype=jnp.float32)
        b = jax.random.uniform(k6, (D_OUT,), minval=-stdv, maxval=stdv, dtype=jnp.float32)
        return {'X': X, 'edge_src': edge_src, 'edge_dst': edge_dst, 'edge_val': edge_val, 'W': W, 'b': b}
    _L0_gnn_all = _L0_gnn_setup()
    _L0_gnn_in = {k: v for k, v in _L0_gnn_all.items() if k in ('W', 'b')}
    del _L0_gnn_all

    def _L1_gnn_setup():
        import jax, jax.numpy as jnp
        import numpy as np
        N, E = (30000, 15000)
        D, H, DFF = (256, 8, 1024)
        HD = D // H

        def _layer_norm(x, g, b, eps=1e-05):
            mu = jnp.mean(x, axis=-1, keepdims=True)
            var = jnp.var(x, axis=-1, keepdims=True)
            return (x - mu) * jax.lax.rsqrt(var + eps) * g + b

        def _transformer_conv(x, src, dst, Wq, bq, Wk, bk, Wv, bv, Wskip, bskip):
            n = x.shape[0]
            q = (x @ Wq + bq).reshape(n, H, HD)
            k = (x @ Wk + bk).reshape(n, H, HD)
            v = (x @ Wv + bv).reshape(n, H, HD)
            qi = q[dst]
            kj = k[src]
            logits = jnp.sum(qi * kj, axis=-1) / np.sqrt(HD)
            m = jax.ops.segment_max(logits, dst, num_segments=n)
            m = jax.lax.stop_gradient(jnp.where(jnp.isfinite(m), m, 0.0))
            ex = jnp.exp(logits - m[dst])
            denom = jax.ops.segment_sum(ex, dst, num_segments=n)
            alpha = ex / (denom[dst] + 1e-16)
            msg = v[src] * alpha[..., None]
            out = jax.ops.segment_sum(msg, dst, num_segments=n).reshape(n, H * HD)
            return out + (x @ Wskip + bskip)
        key = jax.random.key(seed)
        ks = jax.random.split(key, 16)
        s = 0.02
        inp = {'node': jax.random.normal(ks[0], (N, D), dtype=jnp.float32), 'edge_index': jax.random.randint(ks[1], (2, E), 0, N, dtype=jnp.int64), 'Wq': jax.random.normal(ks[2], (D, H * HD), dtype=jnp.float32) * s, 'bq': jnp.zeros((H * HD,), dtype=jnp.float32), 'Wk': jax.random.normal(ks[3], (D, H * HD), dtype=jnp.float32) * s, 'bk': jnp.zeros((H * HD,), dtype=jnp.float32), 'Wv': jax.random.normal(ks[4], (D, H * HD), dtype=jnp.float32) * s, 'bv': jnp.zeros((H * HD,), dtype=jnp.float32), 'Wskip': jax.random.normal(ks[5], (D, H * HD), dtype=jnp.float32) * s, 'bskip': jnp.zeros((H * HD,), dtype=jnp.float32), 'Wo': jax.random.normal(ks[6], (H * HD, D), dtype=jnp.float32) * s, 'bo': jnp.zeros((D,), dtype=jnp.float32), 'W1': jax.random.normal(ks[7], (D, DFF), dtype=jnp.float32) * s, 'b1': jnp.zeros((DFF,), dtype=jnp.float32), 'W2': jax.random.normal(ks[8], (DFF, D), dtype=jnp.float32) * s, 'b2': jnp.zeros((D,), dtype=jnp.float32), 'g1': jnp.ones((D,), dtype=jnp.float32), 'be1': jnp.zeros((D,), dtype=jnp.float32), 'g2': jnp.ones((D,), dtype=jnp.float32), 'be2': jnp.zeros((D,), dtype=jnp.float32)}
        return inp
    _L1_gnn_all = _L1_gnn_setup()
    _L1_gnn_in = {k: v for k, v in _L1_gnn_all.items() if k in ('Wq', 'bq', 'Wk', 'bk', 'Wv', 'bv', 'Wskip', 'bskip', 'Wo', 'bo', 'W1', 'b1', 'W2', 'b2', 'g1', 'be1', 'g2', 'be2')}
    del _L1_gnn_all
    return {'x': x, 'src': src, 'dst': dst, 'edge_weight': edge_weight, 'L0_gnn_W': _L0_gnn_in['W'], 'L0_gnn_b': _L0_gnn_in['b'], 'L1_gnn_Wq': _L1_gnn_in['Wq'], 'L1_gnn_bq': _L1_gnn_in['bq'], 'L1_gnn_Wk': _L1_gnn_in['Wk'], 'L1_gnn_bk': _L1_gnn_in['bk'], 'L1_gnn_Wv': _L1_gnn_in['Wv'], 'L1_gnn_bv': _L1_gnn_in['bv'], 'L1_gnn_Wskip': _L1_gnn_in['Wskip'], 'L1_gnn_bskip': _L1_gnn_in['bskip'], 'L1_gnn_Wo': _L1_gnn_in['Wo'], 'L1_gnn_bo': _L1_gnn_in['bo'], 'L1_gnn_W1': _L1_gnn_in['W1'], 'L1_gnn_b1': _L1_gnn_in['b1'], 'L1_gnn_W2': _L1_gnn_in['W2'], 'L1_gnn_b2': _L1_gnn_in['b2'], 'L1_gnn_g1': _L1_gnn_in['g1'], 'L1_gnn_be1': _L1_gnn_in['be1'], 'L1_gnn_g2': _L1_gnn_in['g2'], 'L1_gnn_be2': _L1_gnn_in['be2']}

def reference(x, src, dst, edge_weight, L0_gnn_W, L0_gnn_b, L1_gnn_Wq, L1_gnn_bq, L1_gnn_Wk, L1_gnn_bk, L1_gnn_Wv, L1_gnn_bv, L1_gnn_Wskip, L1_gnn_bskip, L1_gnn_Wo, L1_gnn_bo, L1_gnn_W1, L1_gnn_b1, L1_gnn_W2, L1_gnn_b2, L1_gnn_g1, L1_gnn_be1, L1_gnn_g2, L1_gnn_be2):
    import jax
    import jax.numpy as jnp

    def _L0_gnn_ref(X, edge_src, edge_dst, edge_val, W, b):
        import jax, jax.numpy as jnp
        import numpy as np
        N_NODES = 3125
        N_EDGES = 100000
        D_IN = 256
        D_OUT = 256
        support = X @ W
        msgs = support[edge_src] * edge_val[:, None]
        out = jax.ops.segment_sum(msgs, edge_dst, num_segments=N_NODES)
        return out + b

    def _L1_gnn_ref(node, edge_index, Wq, bq, Wk, bk, Wv, bv, Wskip, bskip, Wo, bo, W1, b1, W2, b2, g1, be1, g2, be2):
        import jax, jax.numpy as jnp
        import numpy as np
        N, E = (30000, 15000)
        D, H, DFF = (256, 8, 1024)
        HD = D // H

        def _layer_norm(x, g, b, eps=1e-05):
            mu = jnp.mean(x, axis=-1, keepdims=True)
            var = jnp.var(x, axis=-1, keepdims=True)
            return (x - mu) * jax.lax.rsqrt(var + eps) * g + b

        def _transformer_conv(x, src, dst, Wq, bq, Wk, bk, Wv, bv, Wskip, bskip):
            n = x.shape[0]
            q = (x @ Wq + bq).reshape(n, H, HD)
            k = (x @ Wk + bk).reshape(n, H, HD)
            v = (x @ Wv + bv).reshape(n, H, HD)
            qi = q[dst]
            kj = k[src]
            logits = jnp.sum(qi * kj, axis=-1) / np.sqrt(HD)
            m = jax.ops.segment_max(logits, dst, num_segments=n)
            m = jax.lax.stop_gradient(jnp.where(jnp.isfinite(m), m, 0.0))
            ex = jnp.exp(logits - m[dst])
            denom = jax.ops.segment_sum(ex, dst, num_segments=n)
            alpha = ex / (denom[dst] + 1e-16)
            msg = v[src] * alpha[..., None]
            out = jax.ops.segment_sum(msg, dst, num_segments=n).reshape(n, H * HD)
            return out + (x @ Wskip + bskip)
        src, dst = (edge_index[0], edge_index[1])
        sa = _transformer_conv(node, src, dst, Wq, bq, Wk, bk, Wv, bv, Wskip, bskip)
        sa = sa @ Wo + bo
        x = _layer_norm(node + sa, g1, be1)
        ff = jax.nn.relu(x @ W1 + b1) @ W2 + b2
        return _layer_norm(x + ff, g2, be2)
    edge_index = jnp.stack([src, dst])
    h = jnp.maximum(_layernorm(x, axis=-1), 0.0)
    x = x + _L0_gnn_ref(h, src, dst, edge_weight, L0_gnn_W, L0_gnn_b)
    h = jnp.maximum(_layernorm(x, axis=-1), 0.0)
    x = x + _L1_gnn_ref(h, edge_index, L1_gnn_Wq, L1_gnn_bq, L1_gnn_Wk, L1_gnn_bk, L1_gnn_Wv, L1_gnn_bv, L1_gnn_Wskip, L1_gnn_bskip, L1_gnn_Wo, L1_gnn_bo, L1_gnn_W1, L1_gnn_b1, L1_gnn_W2, L1_gnn_b2, L1_gnn_g1, L1_gnn_be1, L1_gnn_g2, L1_gnn_be2)
    return x

_drawn_inputs = setup_inputs


def setup_inputs(seed=0):
    import zlib

    import numpy as np

    out = dict(_drawn_inputs(seed))
    spreads = {'L1_gnn_bq': (0.0, 2.0),
     'L1_gnn_bk': (0.0, 2.0),
     'L1_gnn_bv': (0.0, 0.628),
     'L1_gnn_bskip': (0.0, 0.692),
     'L1_gnn_bo': (0.0, 0.271),
     'L1_gnn_b1': (0.0, 0.741),
     'L1_gnn_b2': (0.0, 0.318),
     'L1_gnn_g1': (1.0, 0.2),
     'L1_gnn_be1': (0.0, 0.356),
     'L1_gnn_g2': (1.0, 0.2),
     'L1_gnn_be2': (0.0, 0.324)}
    factors = {'L0_gnn_b': 4.092, 'L1_gnn_Wq': 57.466, 'L1_gnn_Wk': 53.891, 'L1_gnn_Wv': 2.948}
    for name, (base, spread) in spreads.items():
        noise = np.random.default_rng([zlib.crc32(name.encode()), seed]).standard_normal(out[name].shape)
        drawn = base * np.exp(spread * noise) if base else spread * noise
        out[name] = jnp.asarray(drawn.astype(out[name].dtype))
    for name, factor in factors.items():
        out[name] = (out[name] * factor).astype(out[name].dtype)
    return out
```

```python
import concourse.bass as bass
from concourse import mybir
from concourse.alu_op_type import AluOpType as ALU
from contextlib import ExitStack


def gnn_two_layers(nc, a, out):
    f32, bf16, i32 = mybir.dt.float32, mybir.dt.bfloat16, mybir.dt.int32
    ACT = mybir.ActivationFunctionType
    AX = mybir.AxisListType

    P = 128
    N, D = a["x"].shape
    E = a["src"].shape[0]
    NT = -(-N // P)
    NFULL = N // P
    NREST = N - NFULL * P
    CT = 16
    T = -(-(-(-E // P) + NT) // (2 * CT)) * 2 * CT
    C = T // CT
    CE = CT * P
    G4 = CT // 4
    TG = 4
    TP = T // TG
    H = 8
    HD = D // H
    F = a["L1_gnn_W1"].shape[1]
    FK = F // P
    DK = D // P
    AW = D + H
    EPAD = (-(-E // P) + 2) * P
    BIG = 1.0e38
    EW = 4 * CE + 2 + 4 * D
    EPS = 1e-5
    SCALE = float(HD) ** -0.5
    assert DK == 2 and NT % 2 == 1 and TP <= P and E % 125 == 0 and C >= 6

    def scratch(name, shape, dt):
        return nc.dram_tensor(name, shape, dt, kind="Internal").ap()

    src_pad = scratch("src_pad", (EPAD // P, P), i32)
    dst_pad = scratch("dst_pad", (EPAD // P, P), i32)
    w_pad = scratch("w_pad", (EPAD // P, P), f32)
    key_lin = scratch("key_lin", (T * P + P,), f32)
    brk_lin = scratch("brk_lin", (T * P + P,), f32)
    loc_lin = scratch("loc_lin", (T * P,), bf16)
    nt_lin = scratch("nt_lin", (T,), i32)
    sup_tab = scratch("sup_tab", (NT * P, D), f32)
    kv_tab = scratch("kv_tab", (NT * P, 2 * D), f32)
    x2_tab = scratch("x2_tab", (NT * P, D), f32)

    ctx = ExitStack()
    with ctx:
        def sb(name, shape, dt=f32):
            return ctx.enter_context(nc.sbuf_tensor(name, shape, dt))

        def sem(name):
            return ctx.enter_context(nc.semaphore(name))

        BIGR = sb("big_region", [P, 2 * CT * 2 * D])
        Xs = BIGR[:, 0:NT * D].rearrange("p (n d) -> p n d", d=D)
        o = NT * D
        G0 = BIGR[:, o:o + CT * D].rearrange("p (j d) -> p j d", d=D)
        o += CT * D
        W0 = BIGR[:, o:o + DK * D].rearrange("p (k n) -> p k n", k=DK)
        o += DK * D
        WQKV = BIGR[:, o:o + DK * 3 * D].rearrange("p (k n) -> p k n", k=DK)
        o += DK * 3 * D
        assert o <= 2 * CT * 2 * D
        KV = BIGR[:, :].rearrange("p (j d) -> p j d", d=2 * D)
        o = 0
        WS = BIGR[:, o:o + DK * D].rearrange("p (k n) -> p k n", k=DK)
        o += DK * D
        WO = BIGR[:, o:o + DK * D].rearrange("p (k n) -> p k n", k=DK)
        o += DK * D
        W1 = BIGR[:, o:o + DK * F].rearrange("p (k n) -> p k n", k=DK)
        o += DK * F
        W2 = BIGR[:, o:o + FK * D].rearrange("p (k n) -> p k n", k=FK)
        o += FK * D

        EDG = sb("edge_region", [P, EW])
        at = [0]

        def prep(shape, dt=f32):
            n = 1
            for s in shape:
                n *= s
            v = EDG[:, at[0]:at[0] + n]
            at[0] += n
            if dt is not f32:
                v = v.bitcast(dt)
            if len(shape) == 2:
                v = v.rearrange("p (a b) -> p a b", b=shape[1])
            return v

        dst_r, src_r, w_r = prep([TG, P], i32), prep([TG, P], i32), prep([TG, P])
        live, key1, loc_m, prev, brk, src_f = [prep([TG, P]) for _ in range(6)]
        loc_b = EDG[:, at[0]:at[0] + TG * P // 2].bitcast(bf16).rearrange("p (a b) -> p a b", b=P)
        at[0] += TG * P // 2
        ge_, ge2, ge3 = [prep([TG, NT - 1]) for _ in range(3)]
        dst_i = prep([E // 125], i32)
        junk = prep([E // 125])
        Hn, HT, SO = prep([2, D]), prep([2, D]), prep([2, 2 * D])
        assert at[0] <= EW

        at[0] = 0
        BRK = [prep([CE + 1]) for _ in range(2)]
        FM = prep([CE])
        BM = prep([CE])
        PR = [prep([2, D]) for _ in range(2)]
        assert at[0] <= EW

        at[0] = 0
        fin = {k: prep([2, D]) for k in ("x2", "h", "z", "out")}
        f1 = {k: prep([D]) for k in ("hT", "att", "sa", "saT", "y", "yn", "zT", "y2", "yn2")}
        F1 = prep([FK, P])
        assert at[0] <= EW

        ACC = sb("node_sums", [P, NT, AW])
        Q = sb("queries", [P, NT, D])
        R = sb("edge_rows", [P, 2, 4, AW])
        A = sb("edge_to_node", [P, 2, 4, P])
        OT = sb("node_to_edge", [P, 2, 4, P])
        LB = sb("loc_rows", [P, 2, CE], bf16)
        L = sb("logits", [P, 2, CT, H])
        DF = sb("logit_minus_max", [P, CT, H])
        EX = sb("exps", [P, 2, CT, H])
        src_e = sb("src_e", [P, T], i32)
        loc_e = sb("loc_e", [P, T])
        w_e = sb("w_e", [P, T])
        SRC = sb("chunk_src", [P, 2, CT], i32)
        LOC = sb("chunk_loc", [P, 2, CT])
        WGT = sb("chunk_w", [P, 2, CT])
        nt_row = sb("nt_row", [1, T], i32)
        ident = sb("ident", [P, P])
        iota_j = sb("iota_j", [P, P])
        iota_p = sb("iota_p", [P, 1])
        iota_t = sb("iota_t", [P, TG])
        ones = sb("ones", [P, P])
        zpad = sb("zpad", [1, EPAD - E], i32)
        epsc = sb("epsc", [P, 1])
        cnt_p = sb("cnt_p", [P, NT])
        OFF = sb("OFF", [P, NT + 1])
        nb = sb("nb", [P, NT])
        nti = sb("nti", [P, NT], i32)
        ntf = sb("ntf", [P, NT])
        TB = sb("TB", [P, NT + 1])
        Dd = sb("Dd", [P, NT])
        dD = sb("dD", [P, NT])
        s4 = {k: sb("s4_" + k, [P, TG]) for k in ("DD", "EE", "BK", "E0", "LEN", "B1", "E0c")}
        e0_i = sb("e0_i", [P, TG], i32)
        bk_i = sb("bk_i", [P, TG], i32)
        ST = sb("ln_stats", [P, NT, 6])
        MV = sb("ln_mv", [P, NT, 2])
        RS = sb("ln_rs", [P, NT])
        SD = sb("ln_sd", [P, NT])
        NM = sb("ln_nm", [P, NT])
        row = {k: sb("row_" + k, [P, D]) for k in ("b0", "bq", "bs", "bo", "b2", "g1", "be1", "g2", "be2")}
        row_kv = sb("row_kv", [P, 2 * D])
        b1c = sb("b1c", [P, FK])
        m_last = sb("m_last", [H, 1])
        c_d = sb("c_d", [H, 4])
        c_s = sb("c_s", [H, 2])
        c_sel = sb("c_sel", [H, 2, P])
        c_diag = sb("c_diag", [H, 2, H])

        ps = [ctx.enter_context(nc.psum_tensor(f"ps{i}", [P, 512], f32)) for i in range(8)]

        def ge(eng, s, v):
            if not (isinstance(v, int) and v <= 0):
                eng.wait_ge(s, v)

        spare = {}

        def ge_alone(eng, s, v):
            if isinstance(v, int):
                ge(eng, s, v)
                return
            if eng.engine not in spare:
                spare[eng.engine] = eng.alloc_register(f"spare{len(spare)}")
            eng.reg_mov(spare[eng.engine], v)
            eng.wait_ge(S["consts"], 10)
            eng.wait_ge(s, spare[eng.engine])

        def held(eng, v):
            return v if isinstance(v, int) else eng.snap(v)

        def each_node_tile(eng, step):
            step(0, 0, 0)
            step(1, 1, 0)
            with eng.Fori(1, NT // 2) as i:
                step(2 * i, 0, i)
                step(2 * i + 1, 1, i)
            step(NT - 1, 0, NT // 2)

        def each_final_tile(eng, part_a, part_b):
            part_a(0, 0, 0)
            part_a(1, 1, 0)
            part_b(0, 0, 0)
            with eng.Fori(1, NT // 2) as i:
                part_a(2 * i, 0, i)
                part_b(2 * i - 1, 1, i - 1)
                part_a(2 * i + 1, 1, i)
                part_b(2 * i, 0, i)
            part_a(NT - 1, 0, NT // 2)
            part_b(NT - 2, 1, NT // 2 - 1)
            part_b(NT - 1, 0, NT // 2)

        def each_chunk(eng, step):
            step(0, 0)
            step(0, 1)
            with eng.Fori(1, C // 2) as i:
                step(i, 0)
                step(i, 1)

        def node(t, n):
            return t[:, bass.ds(n, 1), :].rearrange("p a d -> p (a d)")

        def dma_load(eng, dst, src, s):
            eng.dma_start(dst, src).then_inc(s, 16)

        def flat(t):
            return t.rearrange("a b -> (a b)")

        def w_view(w):
            return w.rearrange("(k p) n -> p k n", p=P)

        def tiles_of(lin, first):
            return lin[first:first + T * P].rearrange("(g p j) -> p g j", g=TG, j=P)

        names = """consts zeroed x_in dst_in w0_in rows_in pads_in counts total chain rows_gathered e0_ready
            keys_ready key_stored prev_in loc_stored brk_ready brk_stored tr_in tr_out edges_ready
            nt_stored nt_in x2_ready x2_stored acc_clear stat stats_a sd_a ln_a stats_b sd_b ln_b a_h
            a_pt a_ht a_mm a_so b_h b_pt b_ht b_mm b_q b_so staged0 onehot0 l0_mm l0_added staged_src
            staged_loc ot_ready qe_done prod_done logit_pairs lt_ready scan_f scan_b mt_ready df_ready
            ex_ready c_diff c_exp c_sel_r cs_ready acc_scaled a1_ready r_ready rden_ready ag_done
            ag_added cs_done fin_w f_h f_pt f_hT f_skip f_att f_sa f_sapt f_saT f_wo f_y f_st f_sd
            f_rs f_yn f_z f_zpt f_zT f_ff1 f_relu f_ff2 f_y2 f_st2 f_sd2 f_rs2 f_yn2 f_out fr
            """.split()
        S = {n: sem(n) for n in names}
        so_stored = [sem(f"so_stored{k}") for k in range(2)]
        kv_stored = [sem(f"kv_stored{k}") for k in range(2)]
        landed = [sem(f"rows_in{j}") for j in range(2 * CT)]
        landed_before = [16 * C] * CT + [0] * CT
        lb_in = [sem(f"loc_rows_in{k}") for k in range(2)]
        brk_in = [sem(f"breaks_in{k}") for k in range(2)]
        x2_in = [sem(f"x2_in{k}") for k in range(2)]
        out_stored = [sem(f"out_stored{k}") for k in range(2)]

        fs = {k: sb("fs_" + k, [P, H]) for k in ("d", "r")}
        fst = sb("fst", [P, 2, 6])
        fmv = sb("fmv", [P, 2, 2])
        fsd, frs, fnm = sb("fsd", [P, 2]), sb("frs", [P, 2]), sb("fnm", [P, 2])
        edge_c = sb("edge_c", [1, 2])

        block = ctx.enter_context(nc.Block())

        @block.sync
        def _(sp):
            load = lambda dst, src, s: dma_load(sp, dst, src, s)
            load(dst_i[0:125, :], a["dst"].rearrange("(p n) -> p n", p=125), S["dst_in"])
            sp.wait_ge(S["zeroed"], 1)
            load(Xs[:, 0:NFULL, :], a["x"][0:NFULL * P, :].rearrange("(n p) d -> p n d", p=P), S["x_in"])
            load(Xs[0:NREST, NFULL, :], a["x"][NFULL * P:N, :], S["x_in"])
            load(W0, w_view(a["L0_gnn_W"]), S["w0_in"])
            load(WQKV[:, :, 0:D], w_view(a["L1_gnn_Wq"]), S["rows_in"])
            load(WQKV[:, :, D:2 * D], w_view(a["L1_gnn_Wk"]), S["rows_in"])
            load(WQKV[:, :, 2 * D:3 * D], w_view(a["L1_gnn_Wv"]), S["rows_in"])
            load(row["b0"][:, :], a["L0_gnn_b"].partition_broadcast(P), S["rows_in"])
            load(row["bq"][:, :], a["L1_gnn_bq"].partition_broadcast(P), S["rows_in"])
            load(row_kv[:, 0:D], a["L1_gnn_bk"].partition_broadcast(P), S["rows_in"])
            load(row_kv[:, D:2 * D], a["L1_gnn_bv"].partition_broadcast(P), S["rows_in"])
            for k, n in (("bs", "bskip"), ("bo", "bo"), ("b2", "b2"), ("g1", "g1"), ("be1", "be1"),
                         ("g2", "g2"), ("be2", "be2")):
                load(row[k][:, :], a["L1_gnn_" + n].partition_broadcast(P), S["fin_w"])
            with nc.allow_non_contiguous_dma(reason="one column per 128 biases, 4 KiB in all"):
                load(b1c[:, :], a["L1_gnn_b1"].rearrange("(m p) -> p m", p=P), S["fin_w"])

            def store_support(n, par, i):
                first = held(sp, n * P)
                sp.wait_ge(S["a_so"], n + 1)
                sp.dma_start(sup_tab[bass.ds(first, P), :], SO[:, par, 0:D]).then_inc(so_stored[par], 16)

            each_node_tile(sp, store_support)

            sp.wait_ge(S["x2_ready"], 2)
            sp.dma_start(x2_tab.rearrange("(n p) d -> p n d", p=P), Xs).then_inc(S["x2_stored"], 16)

            def store_kv(n, par, i):
                first = held(sp, n * P)
                sp.wait_ge(S["b_so"], n + 1)
                sp.dma_start(kv_tab[bass.ds(first, P), :], SO[:, par, :]).then_inc(kv_stored[par], 16)

            each_node_tile(sp, store_kv)

            sp.wait_ge(S["loc_stored"], 16)
            sp.wait_ge(S["brk_stored"], 32)
            sp.wait_ge(kv_stored[0], 16 * (NT // 2 + 1))
            sp.wait_ge(kv_stored[1], 16 * (NT // 2))

            def load_chunk(i, par):
                c = 2 * i + par
                first = held(sp, c * CE)
                ge(sp, S["ot_ready"], G4 * (c - 1))
                ge(sp, S["c_sel_r"], c - 1)
                sp.dma_start(LB[:, par, :], loc_lin[bass.ds(first, CE)].partition_broadcast(P)
                             ).then_inc(lb_in[par], 16)
                ge_alone(sp, S["scan_b"], c - 1)
                ge_alone(sp, S["c_diff"], 3 * (c - 1))
                sp.dma_start(BRK[par][0:H, :], brk_lin[bass.ds(first, CE + 1)].partition_broadcast(H)
                             ).then_inc(brk_in[par], 16)

            each_chunk(sp, load_chunk)

            sp.wait_ge(S["r_ready"], G4 * C)
            sp.wait_ge(S["logit_pairs"], 2 * G4 * C)
            sp.wait_ge(S["scan_b"], C)
            load(WS, w_view(a["L1_gnn_Wskip"]), S["fin_w"])
            load(WO, w_view(a["L1_gnn_Wo"]), S["fin_w"])
            load(W1, w_view(a["L1_gnn_W1"]), S["fin_w"])
            load(W2, w_view(a["L1_gnn_W2"]), S["fin_w"])

            def load_x2(n, par, i):
                first = held(sp, n * P)
                ge(sp, S["f_out"], 3 * (n - 1))
                sp.dma_start(fin["x2"][:, par, :], x2_tab[bass.ds(first, P), :]).then_inc(x2_in[par], 16)

            def store_out(n, par, i):
                first = held(sp, n * P)
                sp.wait_ge(S["f_out"], 3 * (n + 1))
                sp.dma_start(out[bass.ds(first, P), :], fin["out"][:, par, :]).then_inc(out_stored[par], 16)

            load_x2(0, 0, 0)
            load_x2(1, 1, 0)
            store_out(0, 0, 0)
            load_x2(2, 0, 1)
            with sp.Fori(1, NT // 2) as i:
                store_out(2 * i - 1, 1, i - 1)
                load_x2(2 * i + 1, 1, i)
                store_out(2 * i, 0, i)
                load_x2(2 * i + 2, 0, i + 1)
            store_out(NT - 2, 1, NT // 2 - 1)
            sp.wait_ge(S["f_out"], 3 * NT)
            sp.dma_start(out[NFULL * P:N, :], fin["out"][0:NREST, 0, :]).then_inc(out_stored[0], 16)
            sp.wait_ge(out_stored[0], 16 * (NT // 2 + 1))
            sp.wait_ge(out_stored[1], 16 * (NT // 2))

        @block.gpsimd
        def _(pool):
            g = nc.gpsimd
            g.memset(Xs[:, NFULL, :], 0.0).then_inc(S["zeroed"], 1)
            g.memset(zpad[:, :], 0).then_inc(S["consts"], 1)
            g.memset(ident[:, :], 0.0).then_inc(S["consts"], 1)
            g.iota(iota_j[:, :], [[1, P]], base=0, channel_multiplier=0,
                   allow_small_or_imprecise_dtypes=True).then_inc(S["consts"], 1)
            g.iota(iota_p[:, :], [[0, 1]], base=0, channel_multiplier=1,
                   allow_small_or_imprecise_dtypes=True).then_inc(S["consts"], 1)
            g.iota(iota_t[:, :], [[TP, TG]], base=0, channel_multiplier=1,
                   allow_small_or_imprecise_dtypes=True).then_inc(S["consts"], 1)
            g.memset(ones[:, :], 1.0).then_inc(S["consts"], 1)
            g.memset(epsc[:, :], EPS).then_inc(S["consts"], 1)
            g.memset(edge_c[:, 0:1], -1.0).then_inc(S["consts"], 1)
            g.memset(edge_c[:, 1:2], -BIG).then_inc(S["consts"], 1)
            pool.wait_ge(S["consts"], 2)
            g.affine_select(out=ident[:, :], in_=ident[:, :], compare_op=ALU.not_equal, fill=1.0, base=0,
                            pattern=[[-1, P]], channel_multiplier=1).then_inc(S["consts"], 1)
            pool.wait_ge(S["consts"], 10)

            for dst, src, z in ((src_pad, a["src"], zpad[:, :]), (dst_pad, a["dst"], zpad[:, :]),
                                (w_pad, a["edge_weight"], zpad[:, :].bitcast(f32))):
                pool.dma_start(flat(dst)[0:E].rearrange("(p n) -> p n", p=125),
                               src.rearrange("(p n) -> p n", p=125)).then_inc(S["pads_in"], 16)
                pool.dma_start(flat(dst)[E:EPAD].rearrange("(p n) -> p n", p=1), z).then_inc(S["pads_in"], 16)
            g.memset(ACC[:, :, :], 0.0).then_inc(S["acc_clear"], 1)
            pool.wait_ge(S["pads_in"], 6 * 16)
            pool.wait_ge(S["e0_ready"], 1)
            for dst, src in ((dst_r, dst_pad), (src_r, src_pad), (w_r, w_pad)):
                for k in range(TG):
                    pool.indirect_dma_start(dst[0:TP, k, :], None, src,
                                            bass.IndirectOffsetOnAxis(e0_i[0:TP, k:k + 1], 1)
                                            ).then_inc(S["rows_gathered"], 16)
            for k in range(TG):
                with nc.allow_non_contiguous_dma(reason="one number per edge tile"):
                    pool.dma_start(nt_lin[k * TP:(k + 1) * TP].rearrange("(p n) -> p n", n=1),
                                   bk_i[0:TP, k:k + 1]).then_inc(S["nt_stored"], 16)
            pool.wait_ge(S["nt_stored"], TG * 16)
            pool.dma_start(nt_row[:, :], nt_lin.rearrange("(a n) -> a n", a=1)).then_inc(S["nt_in"], 16)
            pool.wait_ge(S["keys_ready"], 1)
            pool.dma_start(tiles_of(key_lin, 1), key1[0:TP]).then_inc(S["key_stored"], 16)
            pool.dma_start(key_lin[0:1].rearrange("(a n) -> a n", a=1), edge_c[:, 0:1]).then_inc(S["key_stored"], 16)
            pool.wait_ge(S["key_stored"], 32)
            pool.dma_start(prev[0:TP], tiles_of(key_lin, 0)).then_inc(S["prev_in"], 16)
            pool.wait_ge(S["keys_ready"], 2)
            pool.dma_start(tiles_of(loc_lin, 0), loc_b[0:TP]).then_inc(S["loc_stored"], 16)
            pool.wait_ge(S["brk_ready"], 1)
            pool.dma_start(tiles_of(brk_lin, 0), brk[0:TP]).then_inc(S["brk_stored"], 16)
            pool.dma_start(brk_lin[T * P:T * P + 1].rearrange("(a n) -> a n", a=1), edge_c[:, 1:2]
                           ).then_inc(S["brk_stored"], 16)

            pool.wait_ge(so_stored[0], 16 * (NT // 2 + 1))
            pool.wait_ge(so_stored[1], 16 * (NT // 2))

            def gather_support(i, par):
                c = 2 * i + par
                pool.wait_ge(S["staged0"], 3 * c + 1)
                for j in range(CT):
                    ge_alone(pool, S["l0_mm"], CT * (c - 1) + j + 1)
                    pool.indirect_dma_start(G0[:, j, :], None, sup_tab,
                                            bass.IndirectOffsetOnAxis(SRC[:, par, j:j + 1], 0)
                                            ).then_inc(landed[j], 16)

            each_chunk(pool, gather_support)

            pool.wait_ge(S["x2_ready"], 2)
            g.memset(ACC[:, :, :], 0.0).then_inc(S["acc_clear"], 1)

            pool.wait_ge(kv_stored[0], 16 * (NT // 2 + 1))
            pool.wait_ge(kv_stored[1], 16 * (NT // 2))
            pool.wait_ge(S["x2_stored"], 16)

            def gather_kv(i, par):
                c = 2 * i + par
                pool.wait_ge(S["staged_src"], c + 1)
                for j in range(CT):
                    if j % 4 == 0:
                        ge_alone(pool, S["r_ready"], G4 * (c - 2) + j // 4 + 1)
                    pool.indirect_dma_start(KV[:, par * CT + j, :], None, kv_tab,
                                            bass.IndirectOffsetOnAxis(SRC[:, par, j:j + 1], 0)
                                            ).then_inc(landed[par * CT + j], 16)

            each_chunk(pool, gather_kv)

        @block.scalar
        def _(act):
            A_ = nc.scalar.activation

            def node_acts(p_, ln, copy_out):
                h, pt, ht, mm, so = (S[p_ + k] for k in ("h", "pt", "ht", "mm", "so"))

                def norm(n, par):
                    ge(act, pt, n - 1)
                    A_(Hn[:, par, :], node(Xs, n), ACT.Relu, bias=NM[:, bass.ds(n, 1)],
                       scale=RS[:, bass.ds(n, 1)]).then_inc(h, 1)

                def evac(m, par, i):
                    act.wait_ge(mm, m + 1)
                    ge(act, so_stored[par], 16 * i)
                    A_(SO[:, par, 0:D], ps[2 + par][:, 0:D], ACT.Copy).then_inc(so, 1)

                def step(n, par, i):
                    if not (isinstance(n, int) and n == NT - 1):
                        norm(n + 1, 1 - par)
                    act.wait_ge(pt, n + 1)
                    ge(act, mm, n - 1)
                    A_(HT[:, par, :], ps[par][:, 0:D], ACT.Copy).then_inc(ht, 1)
                    if copy_out and not (isinstance(n, int) and n == 0):
                        evac(n - 1, 1 - par, i if par else i - 1)

                act.wait_ge(ln, 2)
                norm(0, 0)
                each_node_tile(act, step)
                if copy_out:
                    evac(NT - 1, 0, NT // 2)

            act.wait_ge(S["consts"], 10)
            act.wait_ge(S["stats_a"], 1)
            A_(SD[:, :], MV[:, :, 1], ACT.Sqrt, bias=epsc[:, :]).then_inc(S["sd_a"], 1)
            node_acts("a_", S["ln_a"], True)
            act.wait_ge(S["stats_b"], 1)
            A_(SD[:, :], MV[:, :, 1], ACT.Sqrt, bias=epsc[:, :]).then_inc(S["sd_b"], 1)
            node_acts("b_", S["ln_b"], False)

            def denominators(i, par, k):
                c = 2 * i + par
                G = G4 * c + k
                act.wait_ge(S["ex_ready"], c + 1)
                ge(act, S["ag_done"], 4 * (G - 1))
                A_(R[:, k % 2, :, D:AW], EX[:, par, 4 * k:4 * k + 4, :], ACT.Copy).then_inc(S["rden_ready"], 1)

            def chunk(i, par, carried):
                c = 2 * i + par
                pi, pp = (i, 0) if par else (i - 1, 1)
                if carried:
                    denominators(pi, pp, 0)
                    denominators(pi, pp, 1)
                    act.wait_ge(S["c_diff"], 3 * c)
                    ge(act, S["cs_ready"], c - 2)
                    A_(c_s[:, par:par + 1], c_d[:, 2:3], ACT.Exp, scale=SCALE).then_inc(S["c_exp"], 1)
                act.wait_ge(S["df_ready"], c + 1)
                ge(act, S["r_ready"], G4 * (c - 1))
                A_(EX[:, par], DF[:, :, :], ACT.Exp, scale=SCALE).then_inc(S["ex_ready"], 1)
                if carried:
                    denominators(pi, pp, 2)
                    denominators(pi, pp, 3)

            chunk(0, 0, False)
            chunk(0, 1, True)
            chunk(1, 0, True)
            with act.Fori(1, C // 2 - 1) as i:
                chunk(i, 1, True)
                chunk(i + 1, 0, True)
            chunk(C // 2 - 1, 1, True)
            for k in range(G4):
                denominators(C // 2 - 1, 1, k)

            def relus(n, part):
                for m in range(4 * part, 4 * part + 4):
                    act.wait_ge(S["f_ff1"], 2 * n + part + 1)
                    ge(act, S["f_ff2"], n)
                    A_(F1[:, m, :], ps[5 + m // 4][:, m % 4 * P:(m % 4 + 1) * P], ACT.Relu, bias=b1c[:, m:m + 1]
                       ).then_inc(S["f_relu"], 1)

            def part_a(n, par, i):
                first = isinstance(n, int) and n == 0
                act.wait_ge(x2_in[par], 16 * (i + 1))
                ge(act, S["f_z"], 2 * (n - 1))
                A_(fin["h"][:, par, :], fin["x2"][:, par, :], ACT.Relu, bias=NM[:, bass.ds(n, 1)],
                   scale=RS[:, bass.ds(n, 1)]).then_inc(S["f_h"], 1)
                act.wait_ge(S["f_pt"], n + 1)
                ge(act, S["f_skip"], n)
                A_(f1["hT"][:, :], ps[0][:, 0:D], ACT.Copy).then_inc(S["f_hT"], 1)
                if not first:
                    relus(n - 1, 0)
                act.wait_ge(S["f_sapt"], n + 1)
                ge(act, S["f_wo"], n)
                A_(f1["saT"][:, :], ps[2][:, 0:D], ACT.Copy).then_inc(S["f_saT"], 1)
                if not first:
                    relus(n - 1, 1)
                act.wait_ge(S["f_st"], 2 * (n + 1))
                A_(fsd[:, 0:1], fmv[:, 0, 1:2], ACT.Sqrt, bias=epsc[:, :]).then_inc(S["f_sd"], 1)
                act.wait_ge(S["f_rs"], 2 * (n + 1))
                A_(f1["yn"][:, :], f1["y"][:, :], ACT.Identity, bias=fnm[:, 0:1], scale=frs[:, 0:1]
                   ).then_inc(S["f_yn"], 1)
                act.wait_ge(S["f_zpt"], n + 1)
                ge(act, S["f_ff1"], 2 * n)
                A_(f1["zT"][:, :], ps[4][:, 0:D], ACT.Copy).then_inc(S["f_zT"], 1)

            def part_b(n, par, i):
                if isinstance(n, int) and n == NT - 1:
                    relus(n, 0)
                    relus(n, 1)
                act.wait_ge(S["f_st2"], 2 * (n + 1))
                A_(fsd[:, 1:2], fmv[:, 1, 1:2], ACT.Sqrt, bias=epsc[:, :]).then_inc(S["f_sd2"], 1)
                act.wait_ge(S["f_rs2"], 2 * (n + 1))
                A_(f1["yn2"][:, :], f1["y2"][:, :], ACT.Identity, bias=fnm[:, 1:2], scale=frs[:, 1:2]
                   ).then_inc(S["f_yn2"], 1)

            act.wait_ge(S["fin_w"], 12 * 16)
            each_final_tile(act, part_a, part_b)

        @block.vector
        def _(dve):
            V = nc.vector
            chained = [0]

            def link(ins):
                chained[0] += 1
                ins.then_inc(S["chain"], 1)
                dve.wait_ge(S["chain"], chained[0])

            def layer_norm_stats(first, st, sd, ln):
                def stat(n):
                    V.bn_stats(node(ST, n), node(Xs, n)).then_inc(S["stat"], 1)
                with dve.Fori(0, NT) as n:
                    stat(n)
                dve.wait_ge(S["stat"], first + NT)
                for n in range(NT):
                    last = V.bn_aggr(MV[:, n, :], ST[:, n, :])
                last.then_inc(st, 1)
                dve.wait_ge(sd, 1)
                dve.wait_ge(st, 1)
                V.reciprocal(RS[:, :], SD[:, :]).then_inc(ln, 1)
                dve.wait_ge(ln, 1)
                V.scalar_tensor_tensor(NM[:, :], MV[:, :, 0], -1.0, RS[:, :], ALU.mult, ALU.mult).then_inc(ln, 1)

            dve.wait_ge(S["x_in"], 32)
            dve.wait_ge(S["consts"], 10)
            layer_norm_stats(0, S["stats_a"], S["sd_a"], S["ln_a"])

            dve.wait_ge(S["dst_in"], 16)
            for b in range(NT):
                link(V.tensor_scalar(junk[0:125, :], dst_i[0:125, :], float(P * (b + 1)), None, ALU.is_lt,
                                     ALU.add, accum_out=cnt_p[0:125, b:b + 1]))
            V.memset(TB[:, 0:1], 0.0)
            V.memset(OFF[:, 0:1], 0.0)
            dve.wait_ge(S["total"], 1)
            link(V.tensor_copy(OFF[:, 1:NT + 1], ps[4][:, 0:NT]))
            link(V.tensor_tensor(nb[:, :], OFF[:, 1:NT + 1], OFF[:, 0:NT], ALU.subtract))
            link(V.tensor_scalar(nti[:, :], nb[:, :], 1.0 / P, (P - 1.0) / P - 0.5 + 1.0 / 512, ALU.mult, ALU.add))
            link(V.tensor_copy(ntf[:, :], nti[:, :]))
            link(V.tensor_tensor_scan(TB[:, 1:NT + 1], ones[:, 0:NT], ntf[:, :], 0.0, ALU.mult, ALU.add))
            link(V.scalar_tensor_tensor(Dd[:, :], TB[:, 0:NT], -float(P), OFF[:, 0:NT], ALU.mult, ALU.add))
            link(V.tensor_tensor(dD[:, 0:NT - 1], Dd[:, 1:NT], Dd[:, 0:NT - 1], ALU.subtract))
            B = [P, TG, NT - 1]

            def over_tiles(v):
                return v.unsqueeze(1).to_broadcast(B)

            link(V.tensor_tensor(ge_, iota_t[:, :].unsqueeze(2).to_broadcast(B), over_tiles(TB[:, 1:NT]), ALU.is_ge))
            link(V.tensor_tensor(ge2, ge_, over_tiles(dD[:, 0:NT - 1]), ALU.mult))
            link(V.tensor_tensor(ge3, ge_, over_tiles(nb[:, 1:NT]), ALU.mult))
            link(V.tensor_reduce(s4["BK"][:, :], ge_, AX.X, ALU.add))
            link(V.tensor_reduce(s4["DD"][:, :], ge2, AX.X, ALU.add))
            link(V.tensor_reduce(s4["EE"][:, :], ge3, AX.X, ALU.add))
            link(V.scalar_tensor_tensor(s4["E0"][:, :], iota_t[:, :], float(P), s4["DD"][:, :], ALU.mult, ALU.add))
            link(V.scalar_tensor_tensor(s4["LEN"][:, :], s4["EE"][:, :], OFF[:, 1:2], s4["E0"][:, :],
                                        ALU.add, ALU.subtract))
            link(V.tensor_scalar(bk_i[:, :], s4["BK"][:, :], 1.0, None, ALU.mult))
            link(V.tensor_scalar(s4["B1"][:, :], s4["BK"][:, :], float(P), 1.0, ALU.mult, ALU.add))
            link(V.tensor_scalar(e0_i[:, :], s4["E0"][:, :], float(E), None, ALU.min))
            V.memset(junk[:, 0:1], 0.0).then_inc(S["e0_ready"], 1)

            def over_edges(v):
                return v[0:TP, :].unsqueeze(2).to_broadcast([TP, TG, P])

            link(V.tensor_tensor(live[0:TP], iota_j[0:TP, :].unsqueeze(1).to_broadcast([TP, TG, P]),
                                 over_edges(s4["LEN"]), ALU.is_lt))
            dve.wait_ge(S["rows_gathered"], 3 * TG * 16)
            V.scalar_tensor_tensor(key1[0:TP], dst_r[0:TP], 1.0, live[0:TP], ALU.add, ALU.mult
                                   ).then_inc(S["keys_ready"], 1)
            dve.wait_ge(S["keys_ready"], 1)
            link(V.tensor_tensor(loc_m[0:TP], key1[0:TP], over_edges(s4["B1"]), ALU.subtract))
            V.tensor_copy(loc_b[0:TP], loc_m[0:TP]).then_inc(S["keys_ready"], 1)
            V.tensor_copy(src_f[0:TP], src_r[0:TP]).then_inc(S["tr_in"], 1)
            dve.wait_ge(S["prev_in"], 16)
            link(V.tensor_tensor(brk[0:TP], key1[0:TP], prev[0:TP], ALU.not_equal))
            V.tensor_scalar(brk[0:TP], brk[0:TP], -BIG, None, ALU.mult).then_inc(S["brk_ready"], 1)
            dve.wait_ge(S["tr_out"], 1)
            V.tensor_copy(loc_e[:, :], ps[5][:, 0:T])
            V.tensor_copy(src_e[:, :], ps[6][:, 0:T])
            V.tensor_copy(w_e[:, :], ps[7][:, 0:T]).then_inc(S["edges_ready"], 1)
            dve.wait_ge(S["edges_ready"], 1)
            dve.wait_ge(S["acc_clear"], 1)
            dve.wait_ge(S["nt_in"], 16)

            regs = [dve.alloc_register(f"dve_nt{k}") for k in range(4)]

            def node_tiles(first):
                dve.load(regs, nt_row[0:1, bass.ds(first, 4)])
                return [dve.snap(r, min_val=0, max_val=NT - 1) for r in regs]

            def stage0(i, par):
                c = 2 * i + par
                cols = bass.ds(c * CT, CT)
                V.tensor_copy(SRC[:, par, :], src_e[:, cols]).then_inc(S["staged0"], 1)
                V.tensor_copy(LOC[:, par, :], loc_e[:, cols]).then_inc(S["staged0"], 1)
                V.tensor_copy(WGT[:, par, :], w_e[:, cols]).then_inc(S["staged0"], 1)

            def weights(i, par, k):
                c = 2 * i + par
                ge(dve, S["l0_mm"], CT * c + 4 * (k - 1))
                for t in range(4):
                    j = 4 * k + t
                    last = V.tensor_scalar(A[:, k % 2, t, :], iota_j[:, :], LOC[:, par, j:j + 1],
                                           WGT[:, par, j:j + 1], ALU.is_equal, ALU.mult)
                last.then_inc(S["onehot0"], 1)

            def sums0(i, par):
                c = 2 * i + par
                dve.wait_ge(S["staged0"], 3 * c + 3)
                if not (isinstance(i, int) and i == C // 2 - 1 and par):
                    stage0(i + par, 1 - par)
                weights(i, par, 0)
                for k in range(G4):
                    if k + 1 < G4:
                        weights(i, par, k + 1)
                    nt = node_tiles(c * CT + 4 * k)
                    for t in range(4):
                        n = c * CT + 4 * k + t
                        dve.wait_ge(S["l0_mm"], n + 1)
                        ge(dve, S["l0_added"], n)
                        s_ = ACC[:, bass.ds(nt[t], 1), 0:D].rearrange("p a d -> p (a d)")
                        V.tensor_tensor(s_, ps[t][:, 0:D], s_, ALU.add).then_inc(S["l0_added"], 1)

            stage0(0, 0)
            sums0(0, 0)
            sums0(0, 1)
            with dve.Fori(1, C // 2 - 1) as i:
                sums0(i, 0)
                sums0(i, 1)
            sums0(C // 2 - 1, 0)
            sums0(C // 2 - 1, 1)

            dve.wait_ge(S["l0_added"], T)
            V.tensor_tensor(Xs, Xs, ACC[:, :, 0:D], ALU.add).then_inc(S["x2_ready"], 1)
            dve.wait_ge(S["x2_ready"], 1)
            dve.wait_ge(S["rows_in"], 7 * 16)
            V.tensor_tensor(Xs, Xs, row["b0"][:, :].unsqueeze(1).to_broadcast([P, NT, D]), ALU.add
                            ).then_inc(S["x2_ready"], 1)
            dve.wait_ge(S["x2_ready"], 2)
            layer_norm_stats(NT, S["stats_b"], S["sd_b"], S["ln_b"])

            def biases(n, par, i):
                dve.wait_ge(S["b_mm"], n + 1)
                V.tensor_tensor(node(Q, n), ps[2 + par][:, 0:D], row["bq"][:, :], ALU.add).then_inc(S["b_q"], 1)
                ge(dve, kv_stored[par], 16 * i)
                V.tensor_tensor(SO[:, par, :], ps[4 + par][:, :], row_kv[:, :], ALU.add).then_inc(S["b_so"], 1)

            each_node_tile(dve, biases)

            def stage_src(i, par):
                V.tensor_copy(SRC[:, par, :], src_e[:, bass.ds((2 * i + par) * CT, CT)]).then_inc(S["staged_src"], 1)

            def front(i, par, carried):
                c = 2 * i + par
                last_chunk = isinstance(i, int) and i == C // 2 - 1 and par == 1
                V.tensor_copy(LOC[:, par, :], loc_e[:, bass.ds(c * CT, CT)]).then_inc(S["staged_loc"], 1)
                if not last_chunk:
                    stage_src(i + par, 1 - par)
                dve.wait_ge(lb_in[par], 16 * (i + 1))
                dve.wait_ge(brk_in[par], 16 * (i + 1))
                if carried:
                    ge(dve, S["c_diff"], 3 * c - 3)
                    V.tensor_copy(m_last[:, :], FM[0:H, CE - 1:CE]).then_inc(S["c_diff"], 1)

                def onehots(k):
                    G = G4 * c + k
                    ge(dve, S["qe_done"], 2 * (G - 1))
                    V.tensor_scalar(OT[:, k % 2].rearrange("p t e -> p (t e)"), LB[:, par, 512 * k:512 * (k + 1)],
                                    iota_p[:, :], None, ALU.is_equal).then_inc(S["ot_ready"], 1)

                def logits(k):
                    for u in (2 * k, 2 * k + 1):
                        U = 2 * G4 * c + u
                        dve.wait_ge(S["qe_done"], U + 1)
                        for t in (2 * u, 2 * u + 1):
                            dve.wait_ge(landed[par * CT + t], landed_before[par * CT] + 16 * (i + 1))
                        V.tensor_tensor(PR[u % 2], KV[:, par * CT + 2 * u:par * CT + 2 * u + 2, 0:D],
                                        ps[u % 2][:, :].rearrange("p (t d) -> p t d", d=D), ALU.mult
                                        ).then_inc(S["prod_done"], 1)
                        dve.wait_ge(S["prod_done"], U + 1)
                        V.tensor_reduce(L[:, par, 2 * u:2 * u + 2, :], PR[u % 2].rearrange(
                            "p t (h d) -> p t h d", d=HD), AX.X, ALU.add).then_inc(S["logit_pairs"], 1)

                def scan_forward(k):
                    G = G4 * c + k
                    dve.wait_ge(S["lt_ready"], G + 1)
                    if k:
                        first = FM[0:H, 512 * k - 1:512 * k]
                    else:
                        first = m_last[:, :] if carried else -BIG
                    if carried and k == 0:
                        dve.wait_ge(S["c_diff"], 3 * c - 2)
                    ge(dve, S["scan_f"], G)
                    V.tensor_tensor_scan(FM[0:H, 512 * k:512 * (k + 1)], BRK[par][0:H, 512 * k:512 * (k + 1)],
                                         ps[2 + k % 2][0:H, :], first, ALU.add, ALU.max).then_inc(S["scan_f"], 1)

                onehots(0)
                for k in range(G4):
                    if k + 1 < G4:
                        onehots(k + 1)
                    logits(k)
                    if k:
                        scan_forward(k - 1)
                scan_forward(G4 - 1)
                dve.wait_ge(S["scan_f"], G4 * (c + 1))
                ge(dve, S["mt_ready"], c)
                V.tensor_tensor_scan(BM[0:H, ::-1], BRK[par][0:H, 1:CE + 1][:, ::-1], FM[0:H, ::-1], -BIG,
                                     ALU.add, ALU.max).then_inc(S["scan_b"], 1)

            def carry(i, par):
                c = 2 * i + par
                dve.wait_ge(S["scan_b"], c + 1)
                ge(dve, S["c_exp"], c - 1)
                V.tensor_tensor(c_d[:, 0:1], m_last[:, :], BM[0:H, 0:1], ALU.subtract).then_inc(S["c_diff"], 1)
                V.tensor_scalar(c_sel[:, par, :], iota_j[0:H, :], LB[0:H, par, 0:1], None, ALU.is_equal
                                ).then_inc(S["c_sel_r"], 1)
                dve.wait_ge(S["c_diff"], 3 * c - 1)
                V.scalar_tensor_tensor(c_d[:, 2:3], BRK[par][0:H, 0:1], 0.0, c_d[:, 0:1], ALU.is_equal, ALU.mult
                                       ).then_inc(S["c_diff"], 1)

            def carry_diag(i, par):
                c = 2 * i + par
                dve.wait_ge(S["c_exp"], c)
                V.scalar_tensor_tensor(c_diag[:, par, :], ident[0:H, 0:H], c_s[:, par:par + 1], ident[0:H, 0:H],
                                       ALU.mult, ALU.subtract).then_inc(S["cs_ready"], 1)

            def minus_max(i, par):
                c = 2 * i + par
                dve.wait_ge(S["mt_ready"], c + 1)
                ge(dve, S["ex_ready"], c)
                V.tensor_tensor(DF[:, :, :], L[:, par], ps[4][:, 0:CT * H].rearrange("p (t h) -> p t h", h=H),
                                ALU.subtract).then_inc(S["df_ready"], 1)

            def rows(i, par, k):
                c = 2 * i + par
                G = G4 * c + k
                ge(dve, S["ag_done"], 4 * (G - 1))
                for t in range(4):
                    last = V.tensor_scalar(A[:, k % 2, t, :], iota_j[:, :], LOC[:, par, 4 * k + t:4 * k + t + 1],
                                           None, ALU.is_equal)
                last.then_inc(S["a1_ready"], 1)
                dve.wait_ge(S["ex_ready"], c + 1)
                j = par * CT + 4 * k
                V.tensor_tensor(R[:, k % 2, :, 0:D].rearrange("p t (h d) -> p t h d", d=HD),
                                KV[:, j:j + 4, D:2 * D].rearrange("p t (h d) -> p t h d", d=HD),
                                EX[:, par, 4 * k:4 * k + 4, :].unsqueeze(3).to_broadcast([P, 4, H, HD]),
                                ALU.mult).then_inc(S["r_ready"], 1)

            def rescale(i, par):
                c = 2 * i + par
                nt = node_tiles(c * CT)[0]
                dve.wait_ge(S["cs_done"], c)
                dve.wait_ge(S["ag_added"], CT * c)
                s_ = ACC[:, bass.ds(nt, 1), 0:D].rearrange("p a (h d) -> p (a h) d", d=HD)
                V.scalar_tensor_tensor(s_, ps[5][:, 0:H].unsqueeze(2).to_broadcast([P, H, HD]), 1.0, s_,
                                       ALU.add, ALU.mult).then_inc(S["acc_scaled"], 1)
                d_ = ACC[:, bass.ds(nt, 1), D:AW].rearrange("p a h -> p (a h)")
                V.scalar_tensor_tensor(d_, ps[5][:, 0:H], 1.0, d_, ALU.add, ALU.mult).then_inc(S["acc_scaled"], 1)

            def add(i, par, k):
                c = 2 * i + par
                nt = node_tiles(c * CT + 4 * k)
                if k == 0:
                    ge(dve, S["acc_scaled"], 2 * c)
                for t in range(4):
                    n = c * CT + 4 * k + t
                    dve.wait_ge(S["ag_done"], n + 1)
                    ge(dve, S["ag_added"], n)
                    s_ = ACC[:, bass.ds(nt[t], 1), :].rearrange("p a d -> p (a d)")
                    V.tensor_tensor(s_, ps[6 + t % 2][:, 0:AW], s_, ALU.add).then_inc(S["ag_added"], 1)

            def chunk(i, par, carried, last=False):
                front(i, par, carried)
                pi, pp = (i, 0) if par else (i - 1, 1)
                before = carried
                if carried:
                    carry(i, par)
                    rows(pi, pp, 0)
                    rows(pi, pp, 1)
                    if not (isinstance(pi, int) and pi == 0 and pp == 0):
                        rescale(pi, pp)
                    add(pi, pp, 0)
                    carry_diag(i, par)
                minus_max(i, par)
                if before:
                    rows(pi, pp, 2)
                    add(pi, pp, 1)
                    rows(pi, pp, 3)
                    add(pi, pp, 2)
                    add(pi, pp, 3)

            dve.wait_ge(S["acc_clear"], 2)
            stage_src(0, 0)
            chunk(0, 0, False)
            chunk(0, 1, True)
            chunk(1, 0, True)
            with dve.Fori(1, C // 2 - 1) as i:
                chunk(i, 1, True)
                chunk(i + 1, 0, True)
            chunk(C // 2 - 1, 1, True)
            li = C // 2 - 1
            rows(li, 1, 0)
            rows(li, 1, 1)
            rescale(li, 1)
            add(li, 1, 0)
            rows(li, 1, 2)
            add(li, 1, 1)
            rows(li, 1, 3)
            add(li, 1, 2)
            add(li, 1, 3)

            def norm(n, y, s_st, s_sd, s_rs, k):
                V.bn_stats(fst[:, k, :], y).then_inc(s_st, 1)
                ge_alone(dve, s_st, 2 * n + 1)
                V.bn_aggr(fmv[:, k, :], fst[:, k, :]).then_inc(s_st, 1)
                dve.wait_ge(s_sd, n + 1)
                V.reciprocal(frs[:, k:k + 1], fsd[:, k:k + 1]).then_inc(s_rs, 1)
                dve.wait_ge(s_rs, 2 * n + 1)
                dve.wait_ge(s_st, 2 * n + 2)
                V.scalar_tensor_tensor(fnm[:, k:k + 1], fmv[:, k, 0:1], -1.0, frs[:, k:k + 1], ALU.mult, ALU.mult
                                       ).then_inc(s_rs, 1)

            def part_a(n, par, i):
                ge(dve, S["f_att"], 3 * n)
                V.tensor_scalar(fs["d"][:, :], ACC[:, bass.ds(n, 1), D:AW].rearrange("p a h -> p (a h)"), 1e-16,
                                None, ALU.add).then_inc(S["f_att"], 1)
                dve.wait_ge(S["f_att"], 3 * n + 1)
                V.reciprocal(fs["r"][:, :], fs["d"][:, :]).then_inc(S["f_att"], 1)
                dve.wait_ge(S["f_att"], 3 * n + 2)
                V.tensor_tensor(f1["att"][:, :].rearrange("p (h d) -> p h d", d=HD),
                                ACC[:, bass.ds(n, 1), 0:D].rearrange("p a (h d) -> p (a h) d", d=HD),
                                fs["r"][:, :].unsqueeze(2).to_broadcast([P, H, HD]), ALU.mult
                                ).then_inc(S["f_att"], 1)
                dve.wait_ge(S["f_att"], 3 * n + 3)
                V.tensor_tensor(f1["att"][:, :], f1["att"][:, :], row["bs"][:, :], ALU.add).then_inc(S["fr"], 1)
                dve.wait_ge(S["f_skip"], n + 1)
                dve.wait_ge(S["fr"], n + 1)
                ge(dve, S["f_sapt"], n)
                V.tensor_tensor(f1["sa"][:, :], ps[1][:, 0:D], f1["att"][:, :], ALU.add).then_inc(S["f_sa"], 1)
                dve.wait_ge(S["f_wo"], n + 1)
                ge(dve, S["f_yn"], n)
                V.tensor_tensor(f1["y"][:, :], ps[3][:, 0:D], row["bo"][:, :], ALU.add).then_inc(S["f_y"], 1)
                dve.wait_ge(S["f_y"], 2 * n + 1)
                V.tensor_tensor(f1["y"][:, :], f1["y"][:, :], fin["h"][:, par, :], ALU.add).then_inc(S["f_y"], 1)
                dve.wait_ge(S["f_y"], 2 * n + 2)
                norm(n, f1["y"][:, :], S["f_st"], S["f_sd"], S["f_rs"], 0)
                dve.wait_ge(S["f_yn"], n + 1)
                V.tensor_tensor(fin["z"][:, par, :], f1["yn"][:, :], row["g1"][:, :], ALU.mult).then_inc(S["f_z"], 1)
                dve.wait_ge(S["f_z"], 2 * n + 1)
                V.tensor_tensor(fin["z"][:, par, :], fin["z"][:, par, :], row["be1"][:, :], ALU.add
                                ).then_inc(S["f_z"], 1)

            def part_b(n, par, i):
                dve.wait_ge(S["f_ff2"], n + 1)
                ge(dve, S["f_yn2"], n)
                V.tensor_tensor(f1["y2"][:, :], ps[7][:, 0:D], row["b2"][:, :], ALU.add).then_inc(S["f_y2"], 1)
                dve.wait_ge(S["f_y2"], 2 * n + 1)
                V.tensor_tensor(f1["y2"][:, :], f1["y2"][:, :], fin["z"][:, par, :], ALU.add).then_inc(S["f_y2"], 1)
                dve.wait_ge(S["f_y2"], 2 * n + 2)
                norm(n, f1["y2"][:, :], S["f_st2"], S["f_sd2"], S["f_rs2"], 1)
                dve.wait_ge(S["f_yn2"], n + 1)
                ge(dve, out_stored[par], 16 * i)
                V.tensor_tensor(fin["out"][:, par, :], f1["yn2"][:, :], row["g2"][:, :], ALU.mult
                                ).then_inc(S["f_out"], 1)
                dve.wait_ge(S["f_out"], 3 * n + 1)
                V.tensor_tensor(fin["out"][:, par, :], fin["out"][:, par, :], row["be2"][:, :], ALU.add
                                ).then_inc(S["f_out"], 1)
                dve.wait_ge(S["f_out"], 3 * n + 2)
                V.tensor_tensor(fin["out"][:, par, :], fin["out"][:, par, :], fin["x2"][:, par, :], ALU.add
                                ).then_inc(S["f_out"], 1)

            dve.wait_ge(S["ag_added"], T)
            dve.wait_ge(S["fin_w"], 12 * 16)
            each_final_tile(dve, part_a, part_b)

        @block.tensor
        def _(pe):
            mm, tr = nc.tensor.matmul, nc.tensor.transpose
            pe.wait_ge(S["consts"], 10)
            pe.wait_ge(S["chain"], NT)
            mm(ps[4][:, 0:NT], ones[0:125, :], cnt_p[0:125, :], start=True, stop=True).then_inc(S["total"], 1)

            def node_products(p_, products, s_out):
                h, pt, ht, done = (S[p_ + k] for k in ("h", "pt", "ht", "mm"))

                def product(m, par):
                    pe.wait_ge(ht, m + 1)
                    ge(pe, s_out, m - 1)
                    for bank, w, width in products:
                        for k in range(DK):
                            last = mm(ps[bank + par][:, 0:width], HT[:, par, k * P:(k + 1) * P], w[:, k, :],
                                      start=(k == 0), stop=(k == DK - 1))
                    last.then_inc(done, 1)

                def step(n, par, i):
                    pe.wait_ge(h, n + 1)
                    ge(pe, ht, n - 1)
                    for k in range(DK):
                        last = tr(ps[par][:, k * P:(k + 1) * P], Hn[:, par, k * P:(k + 1) * P], ident[:, :])
                    last.then_inc(pt, 1)
                    if not (isinstance(n, int) and n == 0):
                        product(n - 1, 1 - par)

                each_node_tile(pe, step)
                product(NT - 1, 0)

            pe.wait_ge(S["w0_in"], 16)
            node_products("a_", [(2, W0, D)], S["a_so"])

            pe.wait_ge(S["tr_in"], 1)
            for bank, t_ in ((5, loc_m), (6, src_f), (7, w_r.bitcast(f32))):
                for k in range(TG):
                    last = tr(ps[bank][:, k * TP:(k + 1) * TP], t_[0:TP, k, :], ident[0:TP, 0:TP])
            last.then_inc(S["tr_out"], 1)

            pe.wait_ge(S["a_so"], NT)

            def sums0(i, par):
                c = 2 * i + par
                for j in range(CT):
                    n = CT * c + j
                    if j % 4 == 0:
                        pe.wait_ge(S["onehot0"], G4 * c + j // 4 + 1)
                    pe.wait_ge(landed[j], 16 * (c + 1))
                    ge(pe, S["l0_added"], n - 3)
                    mm(ps[j % 4][:, 0:D], A[:, j // 4 % 2, j % 4, :], G0[:, j, :], start=True, stop=True
                       ).then_inc(S["l0_mm"], 1)

            each_chunk(pe, sums0)

            pe.wait_ge(S["rows_in"], 7 * 16)
            pe.wait_ge(S["l0_added"], T)
            node_products("b_", [(2, WQKV[:, :, 0:D], D), (4, WQKV[:, :, D:3 * D], 2 * D)], S["b_so"])
            pe.wait_ge(S["b_so"], NT)

            regs = [pe.alloc_register(f"pe_nt{k}") for k in range(4)]

            def front(i, par, carried):
                c = 2 * i + par

                def queries(k):
                    G = G4 * c + k
                    pe.load(regs, nt_row[0:1, bass.ds(c * CT + 4 * k, 4)])
                    nt = [pe.snap(r, min_val=0, max_val=NT - 1) for r in regs]
                    pe.wait_ge(S["ot_ready"], G + 1)
                    for u in (2 * k, 2 * k + 1):
                        ge(pe, S["prod_done"], 2 * G4 * c + u - 1)
                        for t in range(2):
                            e = 2 * (u % 2) + t
                            last = mm(ps[u % 2][:, t * D:(t + 1) * D], OT[:, k % 2, e, :], node(Q, nt[e]),
                                      start=True, stop=True)
                        last.then_inc(S["qe_done"], 1)

                def by_head(k):
                    G = G4 * c + k
                    pe.wait_ge(S["logit_pairs"], 2 * G + 2)
                    ge(pe, S["scan_f"], G - 1)
                    for t in range(4):
                        last = tr(ps[2 + k % 2][0:H, t * P:(t + 1) * P], L[:, par, 4 * k + t, :], ident[:, :])
                    last.then_inc(S["lt_ready"], 1)

                queries(0)
                for k in range(G4):
                    if k + 1 < G4:
                        queries(k + 1)
                    by_head(k)

            def max_by_edge(i, par):
                c = 2 * i + par
                ge_alone(pe, S["scan_b"], c + 1)
                ge(pe, S["df_ready"], c)
                for t in range(CT):
                    last = tr(ps[4][:, t * H:(t + 1) * H], BM[0:H, t * P:(t + 1) * P], ident[0:H, 0:H])
                last.then_inc(S["mt_ready"], 1)

            def carry(i, par):
                c = 2 * i + par
                pe.wait_ge(S["cs_ready"], c)
                pe.wait_ge(S["c_sel_r"], c)
                ge(pe, S["acc_scaled"], 2 * (c - 1))
                mm(ps[5][:, 0:H], c_sel[:, par, :], c_diag[:, par, :], start=True, stop=True
                   ).then_inc(S["cs_done"], 1)

            def sums(i, par, k):
                c = 2 * i + par
                G = G4 * c + k
                pe.wait_ge(S["a1_ready"], G + 1)
                pe.wait_ge(S["r_ready"], G + 1)
                pe.wait_ge(S["rden_ready"], G + 1)
                for t in range(4):
                    ge(pe, S["ag_added"], 4 * G + t - 1)
                    mm(ps[6 + t % 2][:, 0:AW], A[:, k % 2, t, :], R[:, k % 2, t, :], start=True, stop=True
                       ).then_inc(S["ag_done"], 1)

            def chunk(i, par, carried):
                front(i, par, carried)
                pi, pp = (i, 0) if par else (i - 1, 1)
                if carried:
                    if not (isinstance(pi, int) and pi == 0 and pp == 0):
                        carry(pi, pp)
                    sums(pi, pp, 0)
                max_by_edge(i, par)
                if carried:
                    for k in range(1, G4):
                        sums(pi, pp, k)

            chunk(0, 0, False)
            chunk(0, 1, True)
            chunk(1, 0, True)
            with pe.Fori(1, C // 2 - 1) as i:
                chunk(i, 1, True)
                chunk(i + 1, 0, True)
            chunk(C // 2 - 1, 1, True)
            carry(C // 2 - 1, 1)
            for k in range(G4):
                sums(C // 2 - 1, 1, k)

            def across(bank, t_, s_):
                for k in range(DK):
                    last = tr(ps[bank][:, k * P:(k + 1) * P], t_[:, k * P:(k + 1) * P], ident[:, :])
                last.then_inc(s_, 1)

            def times(bank, tT, w, s_):
                for k in range(DK):
                    last = mm(ps[bank][:, 0:D], tT[:, k * P:(k + 1) * P], w[:, k, :], start=(k == 0), stop=(k == DK - 1))
                last.then_inc(s_, 1)

            def a_rows(n, par):
                pe.wait_ge(S["f_h"], n + 1)
                ge(pe, S["f_hT"], n)
                across(0, fin["h"][:, par, :], S["f_pt"])
                pe.wait_ge(S["f_hT"], n + 1)
                ge(pe, S["f_sa"], n)
                times(1, f1["hT"][:, :], WS, S["f_skip"])

            def a_attention(n, par):
                pe.wait_ge(S["f_sa"], n + 1)
                ge(pe, S["f_saT"], n)
                across(2, f1["sa"][:, :], S["f_sapt"])

            def a_output(n, par):
                pe.wait_ge(S["f_saT"], n + 1)
                ge(pe, S["f_y"], 2 * n)
                times(3, f1["saT"][:, :], WO, S["f_wo"])

            def a_z(n, par):
                pe.wait_ge(S["f_z"], 2 * (n + 1))
                ge(pe, S["f_zT"], n)
                across(4, fin["z"][:, par, :], S["f_zpt"])

            def b_up(n, part):
                pe.wait_ge(S["f_zT"], n + 1)
                ge(pe, S["f_relu"], FK * (n - 1) + 4 * (part + 1))
                for m in range(4 * part, 4 * part + 4):
                    for k in range(DK):
                        last = mm(ps[5 + part][:, m % 4 * P:(m % 4 + 1) * P], W1[:, k, m * P:(m + 1) * P],
                                  f1["zT"][:, k * P:(k + 1) * P], start=(k == 0), stop=(k == DK - 1))
                last.then_inc(S["f_ff1"], 1)

            def b_down(n, part):
                if part == 0:
                    ge(pe, S["f_y2"], 2 * n)
                for m in range(4 * part, 4 * part + 4):
                    pe.wait_ge(S["f_relu"], FK * n + m + 1)
                    last = mm(ps[7][:, 0:D], F1[:, m, :], W2[:, m, :], start=(m == 0), stop=(m == FK - 1))
                if part:
                    last.then_inc(S["f_ff2"], 1)

            pe.wait_ge(S["fin_w"], 12 * 16)
            pe.wait_ge(S["ag_added"], T)

            def step(n, par, i):
                more = not (isinstance(n, int) and n == NT - 1)
                if more:
                    a_rows(n + 1, 1 - par)
                b_up(n, 0)
                if more:
                    a_attention(n + 1, 1 - par)
                b_up(n, 1)
                if more:
                    a_output(n + 1, 1 - par)
                b_down(n, 0)
                b_down(n, 1)
                if more:
                    a_z(n + 1, 1 - par)

            a_rows(0, 0)
            a_attention(0, 0)
            a_output(0, 0)
            a_z(0, 0)
            each_node_tile(pe, step)


def kernel(**inputs):
    import numpy as _np
    import concourse.bacc as _bacc
    from concourse import mybir as _mybir
    from concourse.bass_utils import run_bass_kernel_spmd as _run

    nc = _bacc.Bacc("TRN2", target_bir_lowering=False, num_devices=1)
    arrays, args = {}, {}
    for name, value in inputs.items():
        v = _np.ascontiguousarray(value)
        arrays[f"in_{name}"] = v
        args[name] = nc.dram_tensor(f"in_{name}", v.shape, _mybir.dt.from_np(v.dtype), kind="ExternalInput").ap()
    x = args["x"]
    out = nc.dram_tensor("out_x", x.shape, _mybir.dt.float32, kind="ExternalOutput").ap()
    gnn_two_layers(nc, args, out)
    r = _run(nc, [arrays], core_ids=[0])
    return r.results[0]["out_x"]
```

```python
import concourse.bass as bass
from concourse import mybir
from concourse.alu_op_type import AluOpType as ALU
from contextlib import ExitStack


def gnn_two_layers(nc, a, out):
    f32, bf16, i32 = mybir.dt.float32, mybir.dt.bfloat16, mybir.dt.int32
    ACT = mybir.ActivationFunctionType
    AX = mybir.AxisListType

    P = 128
    N, D = a["x"].shape
    E = a["src"].shape[0]
    NT = -(-N // P)
    NFULL = N // P
    NREST = N - NFULL * P
    CT = 16
    T = -(-(-(-E // P) + NT) // (2 * CT)) * 2 * CT
    C = T // CT
    CE = CT * P
    G4 = CT // 4
    TG = 4
    TP = T // TG
    H = 8
    HD = D // H
    F = a["L1_gnn_W1"].shape[1]
    FK = F // P
    DK = D // P
    AW = D + H
    EPAD = (-(-E // P) + 2) * P
    BIG = 1.0e38
    EW = 8704
    EPS = 1e-5
    SCALE = float(HD) ** -0.5
    assert DK == 2 and NT % 2 == 1 and TP <= P and E % 125 == 0 and C >= 6

    def scratch(name, shape, dt):
        return nc.dram_tensor(name, shape, dt, kind="Internal").ap()

    src_pad = scratch("src_pad", (EPAD // P, P), i32)
    dst_pad = scratch("dst_pad", (EPAD // P, P), i32)
    w_pad = scratch("w_pad", (EPAD // P, P), f32)
    brk_rep = scratch("brk_rep", (T, H, 2 * P), f32)
    run_lin = scratch("run_lin", (2, T), f32)
    key_lin = scratch("key_lin", (T * P + P,), f32)
    brk_lin = scratch("brk_lin", (T * P + P,), f32)
    loc_lin = scratch("loc_lin", (T * P,), bf16)
    nt_lin = scratch("nt_lin", (T,), i32)
    sup_tab = scratch("sup_tab", (NT * P, D), f32)
    kv_tab = scratch("kv_tab", (NT * P, 2 * D), f32)
    x2_tab = scratch("x2_tab", (NT * P, D), f32)

    ctx = ExitStack()
    with ctx:
        def sb(name, shape, dt=f32):
            return ctx.enter_context(nc.sbuf_tensor(name, shape, dt))

        def sem(name):
            return ctx.enter_context(nc.semaphore(name))

        BIGR = sb("big_region", [P, 2 * CT * 2 * D])
        Xs = BIGR[:, 0:NT * D].rearrange("p (n d) -> p n d", d=D)
        o = NT * D
        G0 = BIGR[:, o:o + CT * D].rearrange("p (j d) -> p j d", d=D)
        o += CT * D
        W0 = BIGR[:, o:o + DK * D].rearrange("p (k n) -> p k n", k=DK)
        o += DK * D
        WQKV = BIGR[:, o:o + DK * 3 * D].rearrange("p (k n) -> p k n", k=DK)
        o += DK * 3 * D
        assert o <= 2 * CT * 2 * D
        KV = BIGR[:, :].rearrange("p (j d) -> p j d", d=2 * D)
        o = 0
        WS = BIGR[:, o:o + DK * D].rearrange("p (k n) -> p k n", k=DK)
        o += DK * D
        WO = BIGR[:, o:o + DK * D].rearrange("p (k n) -> p k n", k=DK)
        o += DK * D
        W1 = BIGR[:, o:o + DK * F].rearrange("p (k n) -> p k n", k=DK)
        o += DK * F
        W2 = BIGR[:, o:o + FK * D].rearrange("p (k n) -> p k n", k=FK)
        o += FK * D

        EDG = sb("edge_region", [P, EW])
        at = [0]

        def prep(shape, dt=f32):
            n = 1
            for s in shape:
                n *= s
            v = EDG[:, at[0]:at[0] + n]
            at[0] += n
            if dt is not f32:
                v = v.bitcast(dt)
            if len(shape) == 2:
                v = v.rearrange("p (a b) -> p a b", b=shape[1])
            return v

        dst_r, src_r, w_r = prep([TG, P], i32), prep([TG, P], i32), prep([TG, P])
        live, key1, loc_m, prev, src_f = [prep([TG, P]) for _ in range(5)]
        brk2 = prep([TG, 2 * P])
        brk, brk_next = brk2[:, :, 0:P], brk2[:, :, P:2 * P]
        loc_b = EDG[:, at[0]:at[0] + TG * P // 2].bitcast(bf16).rearrange("p (a b) -> p a b", b=P)
        at[0] += TG * P // 2
        ge_, ge2, ge3 = [prep([TG, NT - 1]) for _ in range(3)]
        dst_i = prep([E // 125], i32)
        junk = prep([E // 125])
        Hn, HT, SO = prep([2, D]), prep([2, D]), prep([2, 2 * D])
        assert at[0] <= EW

        at[0] = 0
        PR = [prep([2, D]) for _ in range(2)]
        AB = prep([4, P])
        BRK = prep([2, 2 * P])
        F1s, F2s, B1s, B2s = [prep([P]) for _ in range(4)]
        assert at[0] <= EW

        at[0] = 0
        fin = {k: prep([2, D]) for k in ("x2", "h", "hb", "att", "y", "zT", "zb", "y2", "xo", "out")}
        f1 = {k: prep([D]) for k in ("hT", "sa", "saT", "t", "z", "t2")}
        F1 = prep([FK, P])
        assert at[0] <= EW

        ACC = sb("node_sums", [P, NT, AW])
        Q = sb("queries", [P, NT, D])
        R = sb("edge_rows", [P, 2, 4, AW])
        A = sb("edge_to_node", [P, 2, 4, P])
        OT = sb("node_to_edge", [P, 2, 4, P])
        LB = sb("loc_rows", [P, 2, CE], bf16)
        L = sb("logits", [P, 2, CT, H])
        DF = sb("logit_minus_max", [P, CT, H])
        EX = sb("exps", [P, 2, CT, H])
        src_e = sb("src_e", [P, T], i32)
        loc_e = sb("loc_e", [P, T])
        w_e = sb("w_e", [P, T])
        SRC = sb("chunk_src", [P, 2, CT], i32)
        LOC = sb("chunk_loc", [P, 2, CT])
        WGT = sb("chunk_w", [P, 2, CT])
        sel_t = sb("sel_t", [P, CT])
        sel_h = sb("sel_h", [P, H])
        sel_hT = sb("sel_hT", [H, CT, H])
        run_f = sb("run_f", [H, T])
        run_b = sb("run_b", [H, T])
        run_br = sb("run_br", [H, T])
        run2 = sb("run2", [P, 2, TG])
        ends = sb("ends", [P, 2, CT])
        cf = sb("cf", [H, 2, CT])
        cb = sb("cb", [H, 2, CT + 1])
        start = sb("start", [P, 2])
        pick = sb("pick", [P, 2, CT])
        nt_row = sb("nt_row", [1, T], i32)
        ident = sb("ident", [P, P])
        iota_j = sb("iota_j", [P, P])
        iota_p = sb("iota_p", [P, 1])
        iota_t = sb("iota_t", [P, TG])
        ones = sb("ones", [P, P])
        zpad = sb("zpad", [1, EPAD - E], i32)
        epsc = sb("epsc", [P, 1])
        cnt_p = sb("cnt_p", [P, NT])
        OFF = sb("OFF", [P, NT + 1])
        nb = sb("nb", [P, NT])
        nti = sb("nti", [P, NT], i32)
        ntf = sb("ntf", [P, NT])
        TB = sb("TB", [P, NT + 1])
        Dd = sb("Dd", [P, NT])
        dD = sb("dD", [P, NT])
        s4 = {k: sb("s4_" + k, [P, TG]) for k in ("DD", "EE", "BK", "E0", "LEN", "B1", "E0c")}
        e0_i = sb("e0_i", [P, TG], i32)
        bk_i = sb("bk_i", [P, TG], i32)
        ST = sb("ln_stats", [P, NT, 6])
        MV = sb("ln_mv", [P, NT, 2])
        RS = sb("ln_rs", [P, NT])
        SD = sb("ln_sd", [P, NT])
        NM = sb("ln_nm", [P, NT])
        row = {k: sb("row_" + k, [P, D]) for k in ("b0", "bq", "bs", "bo", "b2", "g1", "be1", "g2", "be2")}
        row_kv = sb("row_kv", [P, 2 * D])
        b1c = sb("b1c", [P, FK])
        c_d = sb("c_d", [H, 4])
        c_s = sb("c_s", [H, 2])
        c_sel = sb("c_sel", [H, 2, P])
        c_diag = sb("c_diag", [H, 2, H])

        ps = [ctx.enter_context(nc.psum_tensor(f"ps{i}", [P, 512], f32)) for i in range(8)]

        def ge(eng, s, v):
            if not (isinstance(v, int) and v <= 0):
                eng.wait_ge(s, v)

        spare = {}

        def ge_alone(eng, s, v):
            if isinstance(v, int):
                ge(eng, s, v)
                return
            if eng.engine not in spare:
                spare[eng.engine] = eng.alloc_register(f"spare{len(spare)}")
            eng.reg_mov(spare[eng.engine], v)
            eng.wait_ge(S["consts"], 11)
            eng.wait_ge(s, spare[eng.engine])

        def held(eng, v):
            return v if isinstance(v, int) else eng.snap(v)

        def each_node_tile(eng, step):
            step(0, 0, 0)
            step(1, 1, 0)
            with eng.Fori(1, NT // 2) as i:
                step(2 * i, 0, i)
                step(2 * i + 1, 1, i)
            step(NT - 1, 0, NT // 2)

        def each_chunk(eng, step):
            step(0, 0)
            step(0, 1)
            with eng.Fori(1, C // 2) as i:
                step(i, 0)
                step(i, 1)

        def each_step(eng, parts):
            least, most = min(l for l, _ in parts), max(l for l, _ in parts)
            first, last = 3, NT - 1 - most
            last -= (last - first + 1) % 2

            def fixed(n):
                for lead, part in parts:
                    m = n + lead
                    if 0 <= m < NT:
                        part(m, m % 2, m // 2)

            for n in range(-most, first):
                fixed(n)
            with eng.Fori(first // 2, (last + 1) // 2) as i:
                for u in range(2):
                    for lead, part in parts:
                        k = first % 2 + u + lead
                        part(2 * i + k, k % 2, i + k // 2)
            for n in range(last + 1, NT - least):
                fixed(n)

        def node(t, n):
            return t[:, bass.ds(n, 1), :].rearrange("p a d -> p (a d)")

        def dma_load(eng, dst, src, s):
            eng.dma_start(dst, src).then_inc(s, 16)

        def flat(t):
            return t.rearrange("a b -> (a b)")

        def w_view(w):
            return w.rearrange("(k p) n -> p k n", p=P)

        def tiles_of(lin, first):
            return lin[first:first + T * P].rearrange("(g p j) -> p g j", g=TG, j=P)

        names = """consts zeroed x_in dst_in w0_in rows_in pads_in total chain rows_gathered
            e0_ready keys_ready prepared breaks brk_ready next_ready sel_ready
            tr_in tr_out edges_ready x2_ready x2_stored acc_clear
            stat stats_ready sd_ready ln_ready ln_h ln_pt ln_ht ln_mm ln_so
            staged0 onehot0 l0_mm l0_added
            staged_src staged_loc ot_ready qe_done prod_done logit_pairs
            max_moved last_f carry_f max_f carry_b max_b
            df_ready ex_ready c_diff c_exp c_sel_r cs_ready acc_scaled
            ab_ready a1_ready r_ready rden_ready ag_done ag_added cs_done
            fin_w den_ready f_h f_hb f_att f_pt f_hT f_skip f_sa f_sapt f_saT f_wo f_y f_st f_sd f_t
            f_z f_zb f_zpt f_zT f_ff1 f_relu f_ff2 f_y2 f_st2 f_sd2 f_t2 f_xb f_out
            """.split()
        S = {n: sem(n) for n in names}
        so_stored = [sem(f"so_stored{k}") for k in range(2)]
        kv_stored = [sem(f"kv_stored{k}") for k in range(2)]
        landed = [sem(f"pair_in{j}") for j in range(CT)]
        landed_before = [32 * C, 0]
        NT_STORED = TG * 16
        NT_IN = NT_STORED + 16
        KEY_STORED = NT_IN + 32
        PREV_IN = KEY_STORED + 16
        LOC_STORED = PREV_IN + 16
        BRK_STORED = 32
        NEXT_IN = BRK_STORED + 16
        REP_STORED = NEXT_IN + H * 16
        RUN_STORED = REP_STORED + 2 * TG * 16
        RUN_IN = RUN_STORED + 32
        lb_in = [sem(f"loc_rows_in{k}") for k in range(2)]
        brk_in = [sem(f"breaks_in{k}") for k in range(2)]
        x2_in = [sem(f"x2_in{k}") for k in range(2)]
        xo_in = [sem(f"xo_in{k}") for k in range(2)]
        out_stored = [sem(f"out_stored{k}") for k in range(2)]

        RD = sb("inv_den", [P, NT, H])
        fst = sb("fst", [P, 2, 6])
        fmv = sb("fmv", [P, 2, 2])
        fsd, frs = sb("fsd", [P, 2]), sb("frs", [P, 2])
        edge_c = sb("edge_c", [1, 2])
        below = sb("below", [H, 1])

        block = ctx.enter_context(nc.Block())

        @block.sync
        def _(sp):
            load = lambda dst, src, s: dma_load(sp, dst, src, s)
            load(dst_i[0:125, :], a["dst"].rearrange("(p n) -> p n", p=125), S["dst_in"])
            sp.wait_ge(S["zeroed"], 1)
            load(Xs[:, 0:NFULL, :], a["x"][0:NFULL * P, :].rearrange("(n p) d -> p n d", p=P), S["x_in"])
            load(Xs[0:NREST, NFULL, :], a["x"][NFULL * P:N, :], S["x_in"])
            load(W0, w_view(a["L0_gnn_W"]), S["w0_in"])
            load(WQKV[:, :, 0:D], w_view(a["L1_gnn_Wq"]), S["rows_in"])
            load(WQKV[:, :, D:2 * D], w_view(a["L1_gnn_Wk"]), S["rows_in"])
            load(WQKV[:, :, 2 * D:3 * D], w_view(a["L1_gnn_Wv"]), S["rows_in"])
            load(row["b0"][:, :], a["L0_gnn_b"].partition_broadcast(P), S["rows_in"])
            load(row["bq"][:, :], a["L1_gnn_bq"].partition_broadcast(P), S["rows_in"])
            load(row_kv[:, 0:D], a["L1_gnn_bk"].partition_broadcast(P), S["rows_in"])
            load(row_kv[:, D:2 * D], a["L1_gnn_bv"].partition_broadcast(P), S["rows_in"])
            for k, n in (("bs", "bskip"), ("bo", "bo"), ("b2", "b2"), ("g1", "g1"), ("be1", "be1"),
                         ("g2", "g2"), ("be2", "be2")):
                load(row[k][:, :], a["L1_gnn_" + n].partition_broadcast(P), S["fin_w"])
            with nc.allow_non_contiguous_dma(reason="one column per 128 biases, 4 KiB in all"):
                load(b1c[:, :], a["L1_gnn_b1"].rearrange("(m p) -> p m", p=P), S["fin_w"])

            def store_support(n, par, i):
                first = held(sp, n * P)
                sp.wait_ge(S["ln_so"], n + 1)
                sp.dma_start(sup_tab[bass.ds(first, P), :], SO[:, par, 0:D]).then_inc(so_stored[par], 16)

            each_node_tile(sp, store_support)

            sp.wait_ge(S["prepared"], LOC_STORED)
            sp.wait_ge(S["brk_ready"], 1)
            sp.dma_start(tiles_of(brk_lin, 0), brk[0:TP]).then_inc(S["breaks"], 16)
            sp.dma_start(brk_lin[T * P:T * P + 1].rearrange("(a n) -> a n", a=1), edge_c[:, 1:2]
                           ).then_inc(S["breaks"], 16)
            sp.wait_ge(S["breaks"], BRK_STORED)
            sp.dma_start(brk_next[0:TP], tiles_of(brk_lin, 1)).then_inc(S["breaks"], 16)
            sp.wait_ge(S["breaks"], NEXT_IN)
            for h in range(H):
                sp.dma_start(brk_rep[:, h, :].rearrange("(g p) j -> p g j", g=TG), brk2[0:TP]
                               ).then_inc(S["breaks"], 16)
            sp.wait_ge(S["breaks"], REP_STORED)
            sp.wait_ge(S["next_ready"], 1)
            for v in range(2):
                for k in range(TG):
                    with nc.allow_non_contiguous_dma(reason="one number per edge tile"):
                        sp.dma_start(run_lin[v, k * TP:(k + 1) * TP].rearrange("(p n) -> p n", n=1),
                                       run2[0:TP, v, k:k + 1]).then_inc(S["breaks"], 16)
            sp.wait_ge(S["breaks"], RUN_STORED)
            sp.dma_start(run_f[:, :], run_lin[0, :].partition_broadcast(H)).then_inc(S["breaks"], 16)
            sp.dma_start(run_b[:, :], run_lin[1, :].partition_broadcast(H)).then_inc(S["breaks"], 16)

            sp.wait_ge(S["x2_ready"], 2)
            sp.dma_start(x2_tab.rearrange("(n p) d -> p n d", p=P), Xs).then_inc(S["x2_stored"], 16)

            def store_kv(n, par, i):
                first = held(sp, n * P)
                sp.wait_ge(S["ln_so"], NT + n + 1)
                sp.dma_start(kv_tab[bass.ds(first, P), :], SO[:, par, :]).then_inc(kv_stored[par], 16)

            each_node_tile(sp, store_kv)

            sp.wait_ge(S["breaks"], REP_STORED)
            sp.wait_ge(kv_stored[0], 16 * (NT // 2 + 1))
            sp.wait_ge(kv_stored[1], 16 * (NT // 2))

            def load_chunk(i, par):
                c = 2 * i + par
                first = held(sp, c * CE)
                ge(sp, S["ot_ready"], G4 * (c - 1))
                ge(sp, S["c_sel_r"], c - 1)
                sp.dma_start(LB[:, par, :], loc_lin[bass.ds(first, CE)].partition_broadcast(P)
                             ).then_inc(lb_in[par], 16)
                first = held(sp, c * CT * H)
                ge_alone(sp, S["max_b"], 3 * (c - 1))
                ge_alone(sp, S["c_diff"], 2 * (c - 1))
                sp.dma_start(BRK[:, par, :], brk_rep.rearrange("t h j -> (t h) j")[bass.ds(first, P), :]
                             ).then_inc(brk_in[par], 16)

            each_chunk(sp, load_chunk)

            sp.wait_ge(S["r_ready"], G4 * C)
            sp.wait_ge(S["logit_pairs"], 2 * G4 * C)
            sp.wait_ge(S["max_b"], 3 * C)
            load(WS, w_view(a["L1_gnn_Wskip"]), S["fin_w"])
            load(WO, w_view(a["L1_gnn_Wo"]), S["fin_w"])
            load(W1, w_view(a["L1_gnn_W1"]), S["fin_w"])
            load(W2, w_view(a["L1_gnn_W2"]), S["fin_w"])

            def load_x2(n, par, i):
                first = held(sp, n * P)
                ge(sp, S["f_h"], n - 1)
                sp.dma_start(fin["x2"][:, par, :], x2_tab[bass.ds(first, P), :]).then_inc(x2_in[par], 16)

            def load_xo(n, par, i):
                first = held(sp, n * P)
                ge(sp, S["f_out"], n - 1)
                sp.dma_start(fin["xo"][:, par, :], x2_tab[bass.ds(first, P), :]).then_inc(xo_in[par], 16)

            def store_out(n, par, i):
                first = held(sp, n * P)
                sp.wait_ge(S["f_out"], n + 1)
                if isinstance(n, int) and n == NT - 1:
                    sp.dma_start(out[NFULL * P:N, :], fin["out"][0:NREST, par, :]).then_inc(out_stored[par], 16)
                else:
                    sp.dma_start(out[bass.ds(first, P), :], fin["out"][:, par, :]).then_inc(out_stored[par], 16)

            each_step(sp, [(3, load_x2), (0, load_xo), (-2, store_out)])
            sp.wait_ge(out_stored[0], 16 * (NT // 2 + 1))
            sp.wait_ge(out_stored[1], 16 * (NT // 2))

        @block.gpsimd
        def _(pool):
            g = nc.gpsimd
            g.memset(Xs[:, NFULL, :], 0.0).then_inc(S["zeroed"], 1)
            g.memset(zpad[:, :], 0).then_inc(S["consts"], 1)
            g.memset(ident[:, :], 0.0).then_inc(S["consts"], 1)
            g.iota(iota_j[:, :], [[1, P]], base=0, channel_multiplier=0,
                   allow_small_or_imprecise_dtypes=True).then_inc(S["consts"], 1)
            g.iota(iota_p[:, :], [[0, 1]], base=0, channel_multiplier=1,
                   allow_small_or_imprecise_dtypes=True).then_inc(S["consts"], 1)
            g.iota(iota_t[:, :], [[TP, TG]], base=0, channel_multiplier=1,
                   allow_small_or_imprecise_dtypes=True).then_inc(S["consts"], 1)
            g.memset(ones[:, :], 1.0).then_inc(S["consts"], 1)
            g.memset(epsc[:, :], EPS).then_inc(S["consts"], 1)
            g.memset(edge_c[:, 0:1], -1.0).then_inc(S["consts"], 1)
            g.memset(edge_c[:, 1:2], -BIG).then_inc(S["consts"], 1)
            g.memset(below[:, :], -BIG).then_inc(S["consts"], 1)
            pool.wait_ge(S["consts"], 2)
            g.affine_select(out=ident[:, :], in_=ident[:, :], compare_op=ALU.not_equal, fill=1.0, base=0,
                            pattern=[[-1, P]], channel_multiplier=1).then_inc(S["consts"], 1)
            pool.wait_ge(S["consts"], 11)

            for dst, src, z in ((src_pad, a["src"], zpad[:, :]), (dst_pad, a["dst"], zpad[:, :]),
                                (w_pad, a["edge_weight"], zpad[:, :].bitcast(f32))):
                pool.dma_start(flat(dst)[0:E].rearrange("(p n) -> p n", p=125),
                               src.rearrange("(p n) -> p n", p=125)).then_inc(S["pads_in"], 16)
                pool.dma_start(flat(dst)[E:EPAD].rearrange("(p n) -> p n", p=1), z).then_inc(S["pads_in"], 16)
            g.memset(ACC[:, :, :], 0.0).then_inc(S["acc_clear"], 1)
            pool.wait_ge(S["pads_in"], 6 * 16)
            pool.wait_ge(S["e0_ready"], 1)
            for dst, src in ((dst_r, dst_pad), (src_r, src_pad), (w_r, w_pad)):
                for k in range(TG):
                    pool.indirect_dma_start(dst[0:TP, k, :], None, src,
                                            bass.IndirectOffsetOnAxis(e0_i[0:TP, k:k + 1], 1)
                                            ).then_inc(S["rows_gathered"], 16)
            for k in range(TG):
                with nc.allow_non_contiguous_dma(reason="one number per edge tile"):
                    pool.dma_start(nt_lin[k * TP:(k + 1) * TP].rearrange("(p n) -> p n", n=1),
                                   bk_i[0:TP, k:k + 1]).then_inc(S["prepared"], 16)
            pool.wait_ge(S["prepared"], NT_STORED)
            pool.dma_start(nt_row[:, :], nt_lin.rearrange("(a n) -> a n", a=1)).then_inc(S["prepared"], 16)
            pool.wait_ge(S["prepared"], NT_IN)
            pool.wait_ge(S["keys_ready"], 1)
            pool.dma_start(tiles_of(key_lin, 1), key1[0:TP]).then_inc(S["prepared"], 16)
            pool.dma_start(key_lin[0:1].rearrange("(a n) -> a n", a=1), edge_c[:, 0:1]).then_inc(S["prepared"], 16)
            pool.wait_ge(S["prepared"], KEY_STORED)
            pool.dma_start(prev[0:TP], tiles_of(key_lin, 0)).then_inc(S["prepared"], 16)
            pool.wait_ge(S["keys_ready"], 2)
            pool.wait_ge(S["prepared"], PREV_IN)
            pool.dma_start(tiles_of(loc_lin, 0), loc_b[0:TP]).then_inc(S["prepared"], 16)

            pool.wait_ge(so_stored[0], 16 * (NT // 2 + 1))
            pool.wait_ge(so_stored[1], 16 * (NT // 2))

            def gather_support(i, par):
                c = 2 * i + par
                pool.wait_ge(S["staged0"], 3 * c + 1)
                for j in range(CT):
                    ge_alone(pool, S["l0_mm"], CT * (c - 1) + j + 1)
                    pool.indirect_dma_start(G0[:, j, :], None, sup_tab,
                                            bass.IndirectOffsetOnAxis(SRC[:, par, j:j + 1], 0)
                                            ).then_inc(landed[j // 2], 16)

            each_chunk(pool, gather_support)

            pool.wait_ge(S["x2_ready"], 2)
            g.memset(ACC[:, :, :], 0.0).then_inc(S["acc_clear"], 1)

            pool.wait_ge(kv_stored[0], 16 * (NT // 2 + 1))
            pool.wait_ge(kv_stored[1], 16 * (NT // 2))
            pool.wait_ge(S["x2_stored"], 16)

            def gather_kv(i, par):
                c = 2 * i + par
                pool.wait_ge(S["staged_src"], c + 1)
                for j in range(CT):
                    if j % 4 == 0:
                        ge_alone(pool, S["r_ready"], G4 * (c - 2) + j // 4 + 1)
                    pool.indirect_dma_start(KV[:, par * CT + j, :], None, kv_tab,
                                            bass.IndirectOffsetOnAxis(SRC[:, par, j:j + 1], 0)
                                            ).then_inc(landed[(par * CT + j) // 2], 16)

            each_chunk(pool, gather_kv)

            pool.wait_ge(S["fin_w"], 12 * 16)
            pool.wait_ge(S["den_ready"], 2)

            def attention(n, par, i):
                ge(pool, S["f_sa"], n - 1)
                g.tensor_tensor(fin["att"][:, par, :].rearrange("p (h d) -> p h d", d=HD),
                                ACC[:, bass.ds(n, 1), 0:D].rearrange("p a (h d) -> p (a h) d", d=HD),
                                RD[:, bass.ds(n, 1), :].rearrange("p a h -> p (a h)").unsqueeze(2)
                                .to_broadcast([P, H, HD]), ALU.mult).then_inc(S["f_att"], 1)
                pool.wait_ge(S["f_att"], 2 * n + 1)
                g.tensor_tensor(fin["att"][:, par, :], fin["att"][:, par, :], row["bs"][:, :], ALU.add
                                ).then_inc(S["f_att"], 1)

            def rows_and_bias(n, par, i):
                pool.wait_ge(S["f_h"], n + 1)
                ge(pool, S["f_y"], n - 1)
                g.tensor_tensor(fin["hb"][:, par, :], fin["h"][:, par, :], row["bo"][:, :], ALU.add
                                ).then_inc(S["f_hb"], 1)

            def z_and_bias(n, par, i):
                pool.wait_ge(S["f_z"], n + 1)
                ge(pool, S["f_y2"], n - 1)
                g.tensor_tensor(fin["zb"][:, par, :], f1["z"][:, :], row["b2"][:, :], ALU.add
                                ).then_inc(S["f_zb"], 1)

            def x_and_bias(n, par, i):
                pool.wait_ge(xo_in[par], 16 * (i + 1))
                g.tensor_tensor(fin["xo"][:, par, :], fin["xo"][:, par, :], row["be2"][:, :], ALU.add
                                ).then_inc(S["f_xb"], 1)

            each_step(pool, [(2, attention), (-1, x_and_bias), (2, rows_and_bias), (1, z_and_bias)])

        @block.scalar
        def _(act):
            A_ = nc.scalar.activation

            def node_acts(before, copy_out):
                def norm(n, par):
                    ge(act, S["ln_pt"], before + n - 1)
                    A_(Hn[:, par, :], node(Xs, n), ACT.Relu, bias=NM[:, bass.ds(n, 1)],
                       scale=RS[:, bass.ds(n, 1)]).then_inc(S["ln_h"], 1)

                def evac(m, par, i):
                    act.wait_ge(S["ln_mm"], m + 1)
                    ge(act, so_stored[par], 16 * i)
                    A_(SO[:, par, 0:D], ps[2 + par][:, 0:D], ACT.Copy).then_inc(S["ln_so"], 1)

                def step(n, par, i):
                    if not (isinstance(n, int) and n == NT - 1):
                        norm(n + 1, 1 - par)
                    act.wait_ge(S["ln_pt"], before + n + 1)
                    ge(act, S["ln_mm"], before + n - 1)
                    A_(HT[:, par, :], ps[par][:, 0:D], ACT.Copy).then_inc(S["ln_ht"], 1)
                    if copy_out and not (isinstance(n, int) and n == 0):
                        evac(n - 1, 1 - par, i if par else i - 1)

                norm(0, 0)
                each_node_tile(act, step)
                if copy_out:
                    evac(NT - 1, 0, NT // 2)

            act.wait_ge(S["consts"], 11)
            act.wait_ge(S["stats_ready"], 1)
            A_(SD[:, :], MV[:, :, 1], ACT.Sqrt, bias=epsc[:, :]).then_inc(S["sd_ready"], 1)
            act.wait_ge(S["ln_ready"], 2)
            node_acts(0, True)
            act.wait_ge(S["stats_ready"], 2)
            A_(SD[:, :], MV[:, :, 1], ACT.Sqrt, bias=epsc[:, :]).then_inc(S["sd_ready"], 1)
            act.wait_ge(S["ln_ready"], 4)
            node_acts(NT, False)

            def edge_to_node(i, par, k):
                G = G4 * (2 * i + par) + k
                ge(act, S["a1_ready"], G)
                if k == 0:
                    act.wait_ge(S["staged_loc"], 2 * i + par + 1)
                for t in range(4):
                    last = A_(AB[:, t, :], iota_j[:, :], ACT.Abs, bias=LOC[:, par, 4 * k + t:4 * k + t + 1])
                last.then_inc(S["ab_ready"], 1)
                act.wait_ge(S["ab_ready"], G + 1)
                ge(act, S["ag_done"], 4 * (G - 1))
                A_(A[:, k % 2], AB[:, :, :], ACT.Relu, bias=1.0, scale=-1.0).then_inc(S["a1_ready"], 1)

            def denominators(i, par, k):
                c = 2 * i + par
                G = G4 * c + k
                act.wait_ge(S["ex_ready"], c + 1)
                ge(act, S["ag_done"], 4 * (G - 1))
                A_(R[:, k % 2, :, D:AW], EX[:, par, 4 * k:4 * k + 4, :], ACT.Copy).then_inc(S["rden_ready"], 1)

            def chunk(i, par, carried):
                c = 2 * i + par
                pi, pp = (i, 0) if par else (i - 1, 1)
                if carried:
                    for k in range(G4):
                        edge_to_node(pi, pp, k)
                        denominators(pi, pp, k)
                    act.wait_ge(S["c_diff"], 2 * c)
                    ge(act, S["cs_ready"], c - 2)
                    A_(c_s[:, par:par + 1], c_d[:, 2:3], ACT.Exp, scale=SCALE).then_inc(S["c_exp"], 1)
                act.wait_ge(S["df_ready"], c + 1)
                ge(act, S["r_ready"], G4 * (c - 1))
                A_(EX[:, par], DF[:, :, :], ACT.Exp, scale=SCALE).then_inc(S["ex_ready"], 1)

            chunk(0, 0, False)
            chunk(0, 1, True)
            chunk(1, 0, True)
            with act.Fori(1, C // 2 - 1) as i:
                chunk(i, 1, True)
                chunk(i + 1, 0, True)
            chunk(C // 2 - 1, 1, True)
            for k in range(G4):
                edge_to_node(C // 2 - 1, 1, k)
                denominators(C // 2 - 1, 1, k)

            def rows_of(n, par, i):
                act.wait_ge(x2_in[par], 16 * (i + 1))
                ge(act, S["f_pt"], n - 1)
                ge(act, S["f_hb"], n - 1)
                A_(fin["h"][:, par, :], fin["x2"][:, par, :], ACT.Relu, bias=NM[:, bass.ds(n, 1)],
                   scale=RS[:, bass.ds(n, 1)]).then_inc(S["f_h"], 1)

            def rows_across(n, par, i):
                act.wait_ge(S["f_pt"], n + 1)
                ge(act, S["f_skip"], n)
                A_(f1["hT"][:, :], ps[0][:, 0:D], ACT.Copy).then_inc(S["f_hT"], 1)

            def attention_across(n, par, i):
                act.wait_ge(S["f_sapt"], n + 1)
                ge(act, S["f_wo"], n)
                A_(f1["saT"][:, :], ps[2][:, 0:D], ACT.Copy).then_inc(S["f_saT"], 1)

            def deviation(n, par, i):
                act.wait_ge(S["f_st"], 2 * (n + 1))
                ge(act, S["f_t"], 2 * n)
                A_(fsd[:, 0:1], fmv[:, 0, 1:2], ACT.Sqrt, bias=epsc[:, :]).then_inc(S["f_sd"], 1)

            def z_across(n, par, i):
                act.wait_ge(S["f_zpt"], n + 1)
                ge(act, S["f_ff1"], 2 * (n - 1))
                A_(fin["zT"][:, par, :], ps[4][:, 0:D], ACT.Copy).then_inc(S["f_zT"], 1)

            def relus(part):
                def half(n, par, i):
                    act.wait_ge(S["f_ff1"], 2 * n + part + 1)
                    ge(act, S["f_ff2"], n)
                    for m in range(4 * part, 4 * part + 4):
                        last = A_(F1[:, m, :], ps[5 + part][:, m % 4 * P:(m % 4 + 1) * P], ACT.Relu,
                                  bias=b1c[:, m:m + 1])
                    last.then_inc(S["f_relu"], 1)
                return half

            def deviation2(n, par, i):
                act.wait_ge(S["f_st2"], 2 * (n + 1))
                ge(act, S["f_t2"], 2 * n)
                A_(fsd[:, 1:2], fmv[:, 1, 1:2], ACT.Sqrt, bias=epsc[:, :]).then_inc(S["f_sd2"], 1)

            act.wait_ge(S["fin_w"], 12 * 16)
            act.wait_ge(S["r_ready"], G4 * C)
            each_step(act, [(2, rows_of), (-1, deviation2), (2, rows_across), (0, relus(0)), (1, deviation),
                            (2, attention_across), (0, relus(1)), (1, z_across)])

        @block.vector
        def _(dve):
            V = nc.vector
            chained = [0]

            def link(ins):
                chained[0] += 1
                ins.then_inc(S["chain"], 1)
                dve.wait_ge(S["chain"], chained[0])

            def layer_norm_stats(before):
                with dve.Fori(0, NT) as n:
                    V.bn_stats(node(ST, n), node(Xs, n)).then_inc(S["stat"], 1)
                dve.wait_ge(S["stat"], (before + 1) * NT)
                for n in range(NT):
                    last = V.bn_aggr(MV[:, n, :], ST[:, n, :])
                last.then_inc(S["stats_ready"], 1)
                dve.wait_ge(S["sd_ready"], before + 1)
                dve.wait_ge(S["stats_ready"], before + 1)
                V.reciprocal(RS[:, :], SD[:, :]).then_inc(S["ln_ready"], 1)
                dve.wait_ge(S["ln_ready"], 2 * before + 1)
                V.scalar_tensor_tensor(NM[:, :], MV[:, :, 0], -1.0, RS[:, :], ALU.mult, ALU.mult
                                       ).then_inc(S["ln_ready"], 1)

            dve.wait_ge(S["consts"], 11)
            dve.wait_ge(S["dst_in"], 16)
            for b in range(NT):
                link(V.tensor_scalar(junk[0:125, :], dst_i[0:125, :], float(P * (b + 1)), None, ALU.is_lt,
                                     ALU.add, accum_out=cnt_p[0:125, b:b + 1]))
            V.memset(TB[:, 0:1], 0.0)
            V.memset(OFF[:, 0:1], 0.0)
            V.tensor_reduce(sel_t[:, :], ident[:, :].rearrange("p (t h) -> p t h", h=H), AX.X, ALU.add
                            ).then_inc(S["sel_ready"], 1)
            V.tensor_reduce(sel_h[:, :], ident[:, :].rearrange("p (t h) -> p h t", h=H), AX.X, ALU.add
                            ).then_inc(S["sel_ready"], 1)
            V.tensor_copy(sel_hT[:, :, :], ident[0:H, 0:H].unsqueeze(1).to_broadcast([H, CT, H])
                          ).then_inc(S["sel_ready"], 1)
            dve.wait_ge(S["total"], 1)
            link(V.tensor_copy(OFF[:, 1:NT + 1], ps[4][:, 0:NT]))
            link(V.tensor_tensor(nb[:, :], OFF[:, 1:NT + 1], OFF[:, 0:NT], ALU.subtract))
            link(V.tensor_scalar(nti[:, :], nb[:, :], 1.0 / P, (P - 1.0) / P - 0.5 + 1.0 / 512, ALU.mult, ALU.add))
            link(V.tensor_copy(ntf[:, :], nti[:, :]))
            link(V.tensor_tensor_scan(TB[:, 1:NT + 1], ones[:, 0:NT], ntf[:, :], 0.0, ALU.mult, ALU.add))
            link(V.scalar_tensor_tensor(Dd[:, :], TB[:, 0:NT], -float(P), OFF[:, 0:NT], ALU.mult, ALU.add))
            link(V.tensor_tensor(dD[:, 0:NT - 1], Dd[:, 1:NT], Dd[:, 0:NT - 1], ALU.subtract))
            B = [P, TG, NT - 1]

            def over_tiles(v):
                return v.unsqueeze(1).to_broadcast(B)

            link(V.tensor_tensor(ge_, iota_t[:, :].unsqueeze(2).to_broadcast(B), over_tiles(TB[:, 1:NT]), ALU.is_ge))
            link(V.tensor_tensor(ge2, ge_, over_tiles(dD[:, 0:NT - 1]), ALU.mult))
            link(V.tensor_tensor(ge3, ge_, over_tiles(nb[:, 1:NT]), ALU.mult))
            link(V.tensor_reduce(s4["BK"][:, :], ge_, AX.X, ALU.add))
            link(V.tensor_reduce(s4["DD"][:, :], ge2, AX.X, ALU.add))
            link(V.tensor_reduce(s4["EE"][:, :], ge3, AX.X, ALU.add))
            link(V.scalar_tensor_tensor(s4["E0"][:, :], iota_t[:, :], float(P), s4["DD"][:, :], ALU.mult, ALU.add))
            link(V.scalar_tensor_tensor(s4["LEN"][:, :], s4["EE"][:, :], OFF[:, 1:2], s4["E0"][:, :],
                                        ALU.add, ALU.subtract))
            link(V.tensor_scalar(bk_i[:, :], s4["BK"][:, :], 1.0, None, ALU.mult))
            link(V.tensor_scalar(s4["B1"][:, :], s4["BK"][:, :], float(P), 1.0, ALU.mult, ALU.add))
            link(V.tensor_scalar(e0_i[:, :], s4["E0"][:, :], float(E), None, ALU.min))
            V.memset(junk[:, 0:1], 0.0).then_inc(S["e0_ready"], 1)
            dve.wait_ge(S["x_in"], 32)
            layer_norm_stats(0)

            def over_edges(v):
                return v[0:TP, :].unsqueeze(2).to_broadcast([TP, TG, P])

            link(V.tensor_tensor(live[0:TP], iota_j[0:TP, :].unsqueeze(1).to_broadcast([TP, TG, P]),
                                 over_edges(s4["LEN"]), ALU.is_lt))
            dve.wait_ge(S["rows_gathered"], 3 * TG * 16)
            V.scalar_tensor_tensor(key1[0:TP], dst_r[0:TP], 1.0, live[0:TP], ALU.add, ALU.mult
                                   ).then_inc(S["keys_ready"], 1)
            dve.wait_ge(S["keys_ready"], 1)
            link(V.tensor_tensor(loc_m[0:TP], key1[0:TP], over_edges(s4["B1"]), ALU.subtract))
            V.tensor_copy(loc_b[0:TP], loc_m[0:TP]).then_inc(S["keys_ready"], 1)
            V.tensor_copy(src_f[0:TP], src_r[0:TP]).then_inc(S["tr_in"], 1)
            dve.wait_ge(S["tr_out"], 1)
            V.tensor_copy(loc_e[:, :], ps[5][:, 0:T])
            V.tensor_copy(src_e[:, :], ps[6][:, 0:T])
            V.tensor_copy(w_e[:, :], ps[7][:, 0:T]).then_inc(S["edges_ready"], 1)
            dve.wait_ge(S["edges_ready"], 1)
            dve.wait_ge(S["acc_clear"], 1)
            dve.wait_ge(S["prepared"], NT_IN)

            regs = [dve.alloc_register(f"dve_nt{k}") for k in range(4)]

            def node_tiles(first):
                dve.load(regs, nt_row[0:1, bass.ds(first, 4)])
                return [dve.snap(r, min_val=0, max_val=NT - 1) for r in regs]

            def stage0(i, par):
                c = 2 * i + par
                cols = bass.ds(c * CT, CT)
                V.tensor_copy(SRC[:, par, :], src_e[:, cols]).then_inc(S["staged0"], 1)
                V.tensor_copy(LOC[:, par, :], loc_e[:, cols]).then_inc(S["staged0"], 1)
                V.tensor_copy(WGT[:, par, :], w_e[:, cols]).then_inc(S["staged0"], 1)

            def weights(i, par, k):
                c = 2 * i + par
                ge(dve, S["l0_mm"], CT * c + 4 * (k - 1))
                for t in range(4):
                    j = 4 * k + t
                    last = V.tensor_scalar(A[:, k % 2, t, :], iota_j[:, :], LOC[:, par, j:j + 1],
                                           WGT[:, par, j:j + 1], ALU.is_equal, ALU.mult)
                last.then_inc(S["onehot0"], 1)

            def sums0(i, par):
                c = 2 * i + par
                dve.wait_ge(S["staged0"], 3 * c + 3)
                if not (isinstance(i, int) and i == C // 2 - 1 and par):
                    stage0(i + par, 1 - par)
                weights(i, par, 0)
                for k in range(G4):
                    if k + 1 < G4:
                        weights(i, par, k + 1)
                    nt = node_tiles(c * CT + 4 * k)
                    for t in range(4):
                        n = c * CT + 4 * k + t
                        dve.wait_ge(S["l0_mm"], n + 1)
                        ge(dve, S["l0_added"], n)
                        s_ = ACC[:, bass.ds(nt[t], 1), 0:D].rearrange("p a d -> p (a d)")
                        V.tensor_tensor(s_, ps[t][:, 0:D], s_, ALU.add).then_inc(S["l0_added"], 1)

            stage0(0, 0)
            sums0(0, 0)
            dve.wait_ge(S["prepared"], PREV_IN)
            link(V.tensor_tensor(brk[0:TP], key1[0:TP], prev[0:TP], ALU.not_equal))
            V.tensor_scalar(brk[0:TP], brk[0:TP], -BIG, None, ALU.mult).then_inc(S["brk_ready"], 1)
            sums0(0, 1)
            dve.wait_ge(S["brk_ready"], 1)
            dve.wait_ge(S["breaks"], NEXT_IN)
            V.tensor_reduce(run2[0:TP, 0, :], brk[0:TP], AX.X, ALU.min)
            V.tensor_reduce(run2[0:TP, 1, :], brk_next[0:TP], AX.X, ALU.min).then_inc(S["next_ready"], 1)
            with dve.Fori(1, C // 2 - 1) as i:
                sums0(i, 0)
                sums0(i, 1)
            sums0(C // 2 - 1, 0)
            sums0(C // 2 - 1, 1)

            dve.wait_ge(S["l0_added"], T)
            V.tensor_tensor(Xs, Xs, ACC[:, :, 0:D], ALU.add).then_inc(S["x2_ready"], 1)
            dve.wait_ge(S["x2_ready"], 1)
            dve.wait_ge(S["rows_in"], 7 * 16)
            V.tensor_tensor(Xs, Xs, row["b0"][:, :].unsqueeze(1).to_broadcast([P, NT, D]), ALU.add
                            ).then_inc(S["x2_ready"], 1)
            dve.wait_ge(S["x2_ready"], 2)
            layer_norm_stats(1)

            def biases(n, par, i):
                dve.wait_ge(S["ln_mm"], NT + n + 1)
                V.tensor_tensor(node(Q, n), ps[2 + par][:, 0:D], row["bq"][:, :], ALU.add)
                ge(dve, kv_stored[par], 16 * i)
                V.tensor_tensor(SO[:, par, :], ps[4 + par][:, :], row_kv[:, :], ALU.add).then_inc(S["ln_so"], 1)

            each_node_tile(dve, biases)

            def stage_src(i, par):
                V.tensor_copy(SRC[:, par, :], src_e[:, bass.ds((2 * i + par) * CT, CT)]).then_inc(S["staged_src"], 1)

            def front(i, par, carried):
                c = 2 * i + par
                last_chunk = isinstance(i, int) and i == C // 2 - 1 and par == 1
                V.tensor_scalar(LOC[:, par, :], loc_e[:, bass.ds(c * CT, CT)], -1.0, None, ALU.mult
                                ).then_inc(S["staged_loc"], 1)
                if not last_chunk:
                    stage_src(i + par, 1 - par)
                dve.wait_ge(lb_in[par], 16 * (i + 1))
                dve.wait_ge(brk_in[par], 16 * (i + 1))
                def onehots(k):
                    G = G4 * c + k
                    ge(dve, S["qe_done"], 2 * (G - 1))
                    V.tensor_scalar(OT[:, k % 2].rearrange("p t e -> p (t e)"), LB[:, par, 512 * k:512 * (k + 1)],
                                    iota_p[:, :], None, ALU.is_equal).then_inc(S["ot_ready"], 1)

                def logits(k):
                    for u in (2 * k, 2 * k + 1):
                        U = 2 * G4 * c + u
                        dve.wait_ge(S["qe_done"], U + 1)
                        dve.wait_ge(landed[par * CT // 2 + u], landed_before[par] + 32 * (i + 1))
                        V.tensor_tensor(PR[u % 2], KV[:, par * CT + 2 * u:par * CT + 2 * u + 2, 0:D],
                                        ps[u % 2][:, :].rearrange("p (t d) -> p t d", d=D), ALU.mult
                                        ).then_inc(S["prod_done"], 1)
                        dve.wait_ge(S["prod_done"], U + 1)
                        V.tensor_reduce(L[:, par, 2 * u:2 * u + 2, :], PR[u % 2].rearrange(
                            "p t (h d) -> p t h d", d=HD), AX.X, ALU.add).then_inc(S["logit_pairs"], 1)

                onehots(0)
                for k in range(G4):
                    if k + 1 < G4:
                        onehots(k + 1)
                    logits(k)

            def scan(out, breaks, values, initial, back):
                if back:
                    out, breaks, values = out[:, ::-1], breaks[:, ::-1], values[:, ::-1]
                return V.tensor_tensor_scan(out, breaks, values, initial, ALU.add, ALU.max)

            def forward_1(i, par):
                c = 2 * i + par
                dve.wait_ge(S["max_moved"], 6 * c + 1)
                scan(F1s, BRK[:, par, 0:P], ps[2][:, 0:P], -BIG, False).then_inc(S["last_f"], 1)
                dve.wait_ge(S["last_f"], 2 * c + 1)
                V.tensor_scalar(ends[:, 0, :], sel_t[:, :], F1s[:, P - 1:P], None, ALU.mult
                                ).then_inc(S["last_f"], 1)

            def forward_2(i, par, carried):
                c = 2 * i + par
                dve.wait_ge(S["max_moved"], 6 * c + 2)
                first = cf[:, 1 - par, CT - 1:CT] if carried else -BIG
                V.tensor_tensor_scan(cf[:, par, :], run_f[:, bass.ds(c * CT, CT)], ps[3][0:H, 128:128 + CT],
                                     first, ALU.add, ALU.max).then_inc(S["carry_f"], 1)

            def pick_start(k, at_, done, before):
                V.tensor_tensor(pick[:, k, :], ps[3][:, at_:at_ + CT], sel_t[:, :], ALU.mult).then_inc(done, 1)
                dve.wait_ge(done, before + 1)
                V.tensor_reduce(start[:, k:k + 1], pick[:, k, :], AX.X, ALU.add).then_inc(done, 1)
                dve.wait_ge(done, before + 2)

            def forward_3(i, par):
                c = 2 * i + par
                dve.wait_ge(S["max_moved"], 6 * c + 3)
                pick_start(0, 160, S["max_f"], 5 * c)
                scan(F2s, BRK[:, par, 0:P], ps[2][:, 0:P], start[:, 0:1], False).then_inc(S["max_f"], 1)
                dve.wait_ge(S["max_f"], 5 * c + 3)
                scan(B1s, BRK[:, par, P:2 * P], F2s, -BIG, True).then_inc(S["max_f"], 1)
                dve.wait_ge(S["max_f"], 5 * c + 4)
                V.tensor_scalar(ends[:, 1, :], sel_t[:, :], B1s[:, 0:1], None, ALU.mult).then_inc(S["max_f"], 1)

            def backward_2(i, par):
                c = 2 * i + par
                dve.wait_ge(S["max_moved"], 6 * c + 4)
                V.memset(cb[:, par, CT:CT + 1], -BIG)
                V.tensor_tensor_scan(cb[:, par, 0:CT][:, ::-1], run_br[:, bass.ds(T - (c + 1) * CT, CT)],
                                     ps[3][0:H, 192:192 + CT][:, ::-1], -BIG, ALU.add, ALU.max
                                     ).then_inc(S["carry_b"], 1)

            def backward_3(i, par):
                c = 2 * i + par
                dve.wait_ge(S["max_moved"], 6 * c + 5)
                pick_start(1, 224, S["max_b"], 3 * c)
                scan(B2s, BRK[:, par, P:2 * P], F2s, start[:, 1:2], True).then_inc(S["max_b"], 1)

            def carry(i, par):
                c = 2 * i + par
                dve.wait_ge(S["carry_b"], c + 1)
                dve.wait_ge(S["carry_f"], c)
                V.tensor_tensor(c_d[:, 0:1], cf[:, 1 - par, CT - 1:CT], cb[:, par, 0:1], ALU.subtract
                                ).then_inc(S["c_diff"], 1)
                V.tensor_scalar(c_sel[:, par, :], iota_j[0:H, :], LB[0:H, par, 0:1], None, ALU.is_equal
                                ).then_inc(S["c_sel_r"], 1)
                dve.wait_ge(S["c_diff"], 2 * c - 1)
                ge(dve, S["c_exp"], c - 1)
                V.scalar_tensor_tensor(c_d[:, 2:3], BRK[0:H, par, 0:1], 0.0, c_d[:, 0:1], ALU.is_equal, ALU.mult
                                       ).then_inc(S["c_diff"], 1)

            def carry_diag(i, par):
                c = 2 * i + par
                dve.wait_ge(S["c_exp"], c)
                V.scalar_tensor_tensor(c_diag[:, par, :], ident[0:H, 0:H], c_s[:, par:par + 1], ident[0:H, 0:H],
                                       ALU.mult, ALU.subtract).then_inc(S["cs_ready"], 1)

            def minus_max(i, par):
                c = 2 * i + par
                dve.wait_ge(S["max_moved"], 6 * c + 6)
                ge(dve, S["ex_ready"], c)
                V.tensor_tensor(DF[:, :, :], L[:, par], ps[3][:, 0:P].rearrange("p (t h) -> p t h", h=H),
                                ALU.subtract).then_inc(S["df_ready"], 1)

            def rows(i, par, k):
                c = 2 * i + par
                ge(dve, S["ag_done"], 4 * (G4 * c + k - 1))
                dve.wait_ge(S["ex_ready"], c + 1)
                j = par * CT + 4 * k
                V.tensor_tensor(R[:, k % 2, :, 0:D].rearrange("p t (h d) -> p t h d", d=HD),
                                KV[:, j:j + 4, D:2 * D].rearrange("p t (h d) -> p t h d", d=HD),
                                EX[:, par, 4 * k:4 * k + 4, :].unsqueeze(3).to_broadcast([P, 4, H, HD]),
                                ALU.mult).then_inc(S["r_ready"], 1)

            def rescale(i, par):
                c = 2 * i + par
                nt = node_tiles(c * CT)[0]
                dve.wait_ge(S["cs_done"], c)
                dve.wait_ge(S["ag_added"], CT * c)
                s_ = ACC[:, bass.ds(nt, 1), 0:D].rearrange("p a (h d) -> p (a h) d", d=HD)
                V.scalar_tensor_tensor(s_, ps[2][:, 256:256 + H].unsqueeze(2).to_broadcast([P, H, HD]), 1.0, s_,
                                       ALU.add, ALU.mult).then_inc(S["acc_scaled"], 1)
                d_ = ACC[:, bass.ds(nt, 1), D:AW].rearrange("p a h -> p (a h)")
                V.scalar_tensor_tensor(d_, ps[2][:, 256:256 + H], 1.0, d_, ALU.add, ALU.mult).then_inc(S["acc_scaled"], 1)

            def add(i, par, k):
                c = 2 * i + par
                nt = node_tiles(c * CT + 4 * k)
                if k == 0:
                    ge(dve, S["acc_scaled"], 2 * c)
                for t in range(4):
                    n = c * CT + 4 * k + t
                    dve.wait_ge(S["ag_done"], n + 1)
                    ge(dve, S["ag_added"], n)
                    s_ = ACC[:, bass.ds(nt[t], 1), :].rearrange("p a d -> p (a d)")
                    V.tensor_tensor(s_, ps[4 + t][:, 0:AW], s_, ALU.add).then_inc(S["ag_added"], 1)

            def chunk(i, par, carried):
                front(i, par, carried)
                pi, pp = (i, 0) if par else (i - 1, 1)
                if carried:
                    rows(pi, pp, 0)
                forward_1(i, par)
                if carried:
                    if not (isinstance(pi, int) and pi == 0 and pp == 0):
                        carry_diag(pi, pp)
                    rows(pi, pp, 1)
                forward_2(i, par, carried)
                if carried:
                    if not (isinstance(pi, int) and pi == 0 and pp == 0):
                        rescale(pi, pp)
                    add(pi, pp, 0)
                forward_3(i, par)
                if carried:
                    rows(pi, pp, 2)
                backward_2(i, par)
                if carried:
                    add(pi, pp, 1)
                backward_3(i, par)
                if carried:
                    carry(i, par)
                    rows(pi, pp, 3)
                    add(pi, pp, 2)
                minus_max(i, par)
                if carried:
                    add(pi, pp, 3)

            dve.wait_ge(S["acc_clear"], 2)
            dve.wait_ge(S["breaks"], RUN_IN)
            V.tensor_copy(run_br[:, :], run_b[:, ::-1]).then_inc(S["sel_ready"], 1)
            dve.wait_ge(S["sel_ready"], 4)
            stage_src(0, 0)
            chunk(0, 0, False)
            chunk(0, 1, True)
            chunk(1, 0, True)
            with dve.Fori(1, C // 2 - 1) as i:
                chunk(i, 1, True)
                chunk(i + 1, 0, True)
            chunk(C // 2 - 1, 1, True)
            li = C // 2 - 1
            rows(li, 1, 0)
            carry_diag(li, 1)
            rows(li, 1, 1)
            rescale(li, 1)
            add(li, 1, 0)
            rows(li, 1, 2)
            add(li, 1, 1)
            rows(li, 1, 3)
            add(li, 1, 2)
            add(li, 1, 3)

            def stats(k, src, ready, st, sd_used):
                def part(n, par, i):
                    dve.wait_ge(ready, n + 1)
                    ge(dve, sd_used, n)
                    V.bn_stats(fst[:, k, :], fin[src][:, par, :]).then_inc(st, 1)
                    ge_alone(dve, st, 2 * n + 1)
                    V.bn_aggr(fmv[:, k, :], fst[:, k, :]).then_inc(st, 1)
                return part

            def attention_sum(n, par, i):
                dve.wait_ge(S["f_skip"], n + 1)
                dve.wait_ge(S["f_att"], 2 * (n + 1))
                ge(dve, S["f_sapt"], n)
                V.tensor_tensor(f1["sa"][:, :], ps[1][:, 0:D], fin["att"][:, par, :], ALU.add
                                ).then_inc(S["f_sa"], 1)

            def residual(n, par, i):
                dve.wait_ge(S["f_wo"], n + 1)
                dve.wait_ge(S["f_hb"], n + 1)
                V.tensor_tensor(fin["y"][:, par, :], ps[3][:, 0:D], fin["hb"][:, par, :], ALU.add
                                ).then_inc(S["f_y"], 1)

            def residual2(n, par, i):
                dve.wait_ge(S["f_ff2"], n + 1)
                dve.wait_ge(S["f_zb"], n + 1)
                V.tensor_tensor(fin["y2"][:, par, :], ps[7][:, 0:D], fin["zb"][:, par, :], ALU.add
                                ).then_inc(S["f_y2"], 1)

            def norm1(n, par, i):
                dve.wait_ge(S["f_sd"], n + 1)
                V.reciprocal(frs[:, 0:1], fsd[:, 0:1]).then_inc(S["f_t"], 1)
                V.scalar_tensor_tensor(f1["t"][:, :], fin["y"][:, par, :], fmv[:, 0, 0:1], row["g1"][:, :],
                                       ALU.subtract, ALU.mult).then_inc(S["f_t"], 1)
                dve.wait_ge(S["f_t"], 2 * (n + 1))
                ge(dve, S["f_zpt"], n)
                ge(dve, S["f_zb"], n)
                V.scalar_tensor_tensor(f1["z"][:, :], f1["t"][:, :], frs[:, 0:1], row["be1"][:, :],
                                       ALU.mult, ALU.add).then_inc(S["f_z"], 1)

            def norm2(n, par, i):
                dve.wait_ge(S["f_sd2"], n + 1)
                V.reciprocal(frs[:, 1:2], fsd[:, 1:2]).then_inc(S["f_t2"], 1)
                V.scalar_tensor_tensor(f1["t2"][:, :], fin["y2"][:, par, :], fmv[:, 1, 0:1], row["g2"][:, :],
                                       ALU.subtract, ALU.mult).then_inc(S["f_t2"], 1)
                dve.wait_ge(S["f_t2"], 2 * (n + 1))
                dve.wait_ge(S["f_xb"], n + 1)
                ge(dve, out_stored[par], 16 * i)
                V.scalar_tensor_tensor(fin["out"][:, par, :], f1["t2"][:, :], frs[:, 1:2], fin["xo"][:, par, :],
                                       ALU.mult, ALU.add).then_inc(S["f_out"], 1)

            dve.wait_ge(S["ag_added"], T)
            V.tensor_scalar(RD[:, :, :], ACC[:, :, D:AW], 1e-16, None, ALU.add).then_inc(S["den_ready"], 1)
            dve.wait_ge(S["den_ready"], 1)
            V.reciprocal(RD[:, :, :], RD[:, :, :]).then_inc(S["den_ready"], 1)
            dve.wait_ge(S["fin_w"], 12 * 16)
            each_step(dve, [(-1, stats(1, "y2", S["f_y2"], S["f_st2"], S["f_sd2"])), (1, stats(0, "y", S["f_y"], S["f_st"], S["f_sd"])),
                            (2, attention_sum), (-1, norm2), (1, norm1), (2, residual), (0, residual2)])

        @block.tensor
        def _(pe):
            mm, tr = nc.tensor.matmul, nc.tensor.transpose
            pe.wait_ge(S["consts"], 11)
            pe.wait_ge(S["chain"], NT)
            mm(ps[4][:, 0:NT], ones[0:125, :], cnt_p[0:125, :], start=True, stop=True).then_inc(S["total"], 1)

            def node_products(before, products):
                def product(m, par):
                    pe.wait_ge(S["ln_ht"], before + m + 1)
                    ge(pe, S["ln_so"], before + m - 1)
                    for bank, w, width in products:
                        for k in range(DK):
                            last = mm(ps[bank + par][:, 0:width], HT[:, par, k * P:(k + 1) * P], w[:, k, :],
                                      start=(k == 0), stop=(k == DK - 1))
                    last.then_inc(S["ln_mm"], 1)

                def step(n, par, i):
                    pe.wait_ge(S["ln_h"], before + n + 1)
                    ge(pe, S["ln_ht"], before + n - 1)
                    for k in range(DK):
                        last = tr(ps[par][:, k * P:(k + 1) * P], Hn[:, par, k * P:(k + 1) * P], ident[:, :])
                    last.then_inc(S["ln_pt"], 1)
                    if not (isinstance(n, int) and n == 0):
                        product(n - 1, 1 - par)

                each_node_tile(pe, step)
                product(NT - 1, 0)

            pe.wait_ge(S["w0_in"], 16)
            node_products(0, [(2, W0, D)])

            pe.wait_ge(S["tr_in"], 1)
            for bank, t_ in ((5, loc_m), (6, src_f), (7, w_r.bitcast(f32))):
                for k in range(TG):
                    last = tr(ps[bank][:, k * TP:(k + 1) * TP], t_[0:TP, k, :], ident[0:TP, 0:TP])
            last.then_inc(S["tr_out"], 1)

            pe.wait_ge(S["ln_so"], NT)

            def sums0(i, par):
                c = 2 * i + par
                for j in range(CT):
                    n = CT * c + j
                    if j % 4 == 0:
                        pe.wait_ge(S["onehot0"], G4 * c + j // 4 + 1)
                    if j % 2 == 0:
                        pe.wait_ge(landed[j // 2], 32 * (c + 1))
                    ge(pe, S["l0_added"], n - 3)
                    mm(ps[j % 4][:, 0:D], A[:, j // 4 % 2, j % 4, :], G0[:, j, :], start=True, stop=True
                       ).then_inc(S["l0_mm"], 1)

            each_chunk(pe, sums0)

            pe.wait_ge(S["rows_in"], 7 * 16)
            pe.wait_ge(S["l0_added"], T)
            node_products(NT, [(2, WQKV[:, :, 0:D], D), (4, WQKV[:, :, D:3 * D], 2 * D)])
            pe.wait_ge(S["ln_so"], 2 * NT)

            regs = [pe.alloc_register(f"pe_nt{k}") for k in range(4)]

            def front(i, par, carried):
                c = 2 * i + par

                def queries(k):
                    G = G4 * c + k
                    pe.load(regs, nt_row[0:1, bass.ds(c * CT + 4 * k, 4)])
                    nt = [pe.snap(r, min_val=0, max_val=NT - 1) for r in regs]
                    pe.wait_ge(S["ot_ready"], G + 1)
                    for u in (2 * k, 2 * k + 1):
                        ge(pe, S["prod_done"], 2 * G4 * c + u - 1)
                        for t in range(2):
                            e = 2 * (u % 2) + t
                            last = mm(ps[u % 2][:, t * D:(t + 1) * D], OT[:, k % 2, e, :], node(Q, nt[e]),
                                      start=True, stop=True)
                        last.then_inc(S["qe_done"], 1)

                for k in range(G4):
                    queries(k)
                pe.wait_ge(S["logit_pairs"], 2 * G4 * (c + 1))
                ge(pe, S["max_f"], 5 * c - 2)
                tr(ps[2][:, 0:P], L[:, par].rearrange("p t h -> p (t h)"), ident[:, :]).then_inc(S["max_moved"], 1)

            def to_heads(k, ready, count):
                pe.wait_ge(ready, count)
                mm(ps[3][0:H, 128 + 64 * k:128 + 64 * k + CT], sel_h[:, :], ends[:, k, :], start=True, stop=True
                   ).then_inc(S["max_moved"], 1)

            def to_tiles(par, k, ready, count, carried):
                pe.wait_ge(ready, count)
                o_ = 160 + 64 * k
                sel = sel_hT[:, :, :].rearrange("a t h -> a (t h)")
                if k == 0:
                    mm(ps[3][:, o_ + 1:o_ + CT], sel, cf[:, par, 0:CT - 1], start=True, stop=True)
                    first = cf[:, 1 - par, CT - 1:CT] if carried else below[:, :]
                    mm(ps[3][:, o_:o_ + 1], sel, first, start=True, stop=True).then_inc(S["max_moved"], 1)
                else:
                    mm(ps[3][:, o_:o_ + CT], sel, cb[:, par, 1:CT + 1], start=True, stop=True).then_inc(S["max_moved"], 1)

            def max_by_edge(i, par):
                c = 2 * i + par
                pe.wait_ge(S["max_b"], 3 * c + 3)
                ge(pe, S["df_ready"], c)
                tr(ps[3][:, 0:P], B2s, ident[:, :]).then_inc(S["max_moved"], 1)

            def carry(i, par):
                c = 2 * i + par
                pe.wait_ge(S["cs_ready"], c)
                pe.wait_ge(S["c_sel_r"], c)
                ge(pe, S["acc_scaled"], 2 * (c - 1))
                mm(ps[2][:, 256:256 + H], c_sel[:, par, :], c_diag[:, par, :], start=True, stop=True
                   ).then_inc(S["cs_done"], 1)

            def sums(i, par, k):
                c = 2 * i + par
                G = G4 * c + k
                pe.wait_ge(S["a1_ready"], G + 1)
                pe.wait_ge(S["r_ready"], G + 1)
                pe.wait_ge(S["rden_ready"], G + 1)
                for t in range(4):
                    ge(pe, S["ag_added"], 4 * G + t - 3)
                    mm(ps[4 + t][:, 0:AW], A[:, k % 2, t, :], R[:, k % 2, t, :], start=True, stop=True
                       ).then_inc(S["ag_done"], 1)

            def chunk(i, par, carried):
                c = 2 * i + par
                front(i, par, carried)
                pi, pp = (i, 0) if par else (i - 1, 1)
                if carried:
                    sums(pi, pp, 0)
                to_heads(0, S["last_f"], 2 * c + 2)
                if carried and not (isinstance(pi, int) and pi == 0 and pp == 0):
                    carry(pi, pp)
                to_tiles(par, 0, S["carry_f"], c + 1, carried)
                if carried:
                    sums(pi, pp, 1)
                to_heads(1, S["max_f"], 5 * c + 5)
                to_tiles(par, 1, S["carry_b"], c + 1, carried)
                if carried:
                    sums(pi, pp, 2)
                max_by_edge(i, par)
                if carried:
                    sums(pi, pp, 3)

            chunk(0, 0, False)
            chunk(0, 1, True)
            chunk(1, 0, True)
            with pe.Fori(1, C // 2 - 1) as i:
                chunk(i, 1, True)
                chunk(i + 1, 0, True)
            chunk(C // 2 - 1, 1, True)
            carry(C // 2 - 1, 1)
            for k in range(G4):
                sums(C // 2 - 1, 1, k)

            def across(bank, t_, s_):
                for k in range(DK):
                    last = tr(ps[bank][:, k * P:(k + 1) * P], t_[:, k * P:(k + 1) * P], ident[:, :])
                last.then_inc(s_, 1)

            def times(bank, tT, w, s_):
                for k in range(DK):
                    last = mm(ps[bank][:, 0:D], tT[:, k * P:(k + 1) * P], w[:, k, :], start=(k == 0), stop=(k == DK - 1))
                last.then_inc(s_, 1)

            def rows_across(n, par, i):
                pe.wait_ge(S["f_h"], n + 1)
                ge(pe, S["f_hT"], n)
                across(0, fin["h"][:, par, :], S["f_pt"])

            def skip(n, par, i):
                pe.wait_ge(S["f_hT"], n + 1)
                ge(pe, S["f_sa"], n)
                times(1, f1["hT"][:, :], WS, S["f_skip"])

            def attention_across(n, par, i):
                pe.wait_ge(S["f_sa"], n + 1)
                ge(pe, S["f_saT"], n)
                across(2, f1["sa"][:, :], S["f_sapt"])

            def output(n, par, i):
                pe.wait_ge(S["f_saT"], n + 1)
                ge(pe, S["f_y"], n)
                times(3, f1["saT"][:, :], WO, S["f_wo"])

            def z_across(n, par, i):
                pe.wait_ge(S["f_z"], n + 1)
                ge(pe, S["f_zT"], n)
                across(4, f1["z"][:, :], S["f_zpt"])

            def up(part):
                def half(n, par, i):
                    pe.wait_ge(S["f_zT"], n + 1)
                    ge(pe, S["f_relu"], 2 * (n - 1) + part + 1)
                    for m in range(4 * part, 4 * part + 4):
                        for k in range(DK):
                            last = mm(ps[5 + part][:, m % 4 * P:(m % 4 + 1) * P], W1[:, k, m * P:(m + 1) * P],
                                      fin["zT"][:, par, k * P:(k + 1) * P], start=(k == 0), stop=(k == DK - 1))
                    last.then_inc(S["f_ff1"], 1)
                return half

            def down(part):
                def half(n, par, i):
                    if part == 0:
                        ge(pe, S["f_y2"], n)
                    pe.wait_ge(S["f_relu"], 2 * n + part + 1)
                    for m in range(4 * part, 4 * part + 4):
                        last = mm(ps[7][:, 0:D], F1[:, m, :], W2[:, m, :], start=(m == 0), stop=(m == FK - 1))
                    if part:
                        last.then_inc(S["f_ff2"], 1)
                return half

            pe.wait_ge(S["fin_w"], 12 * 16)
            pe.wait_ge(S["ag_added"], T)
            each_step(pe, [(2, rows_across), (0, up(0)), (2, skip), (0, up(1)), (2, attention_across),
                           (1, z_across), (0, down(0)), (2, output), (0, down(1))])


def kernel(**inputs):
    import numpy as _np
    import concourse.bacc as _bacc
    from concourse import mybir as _mybir
    from concourse.bass_utils import run_bass_kernel_spmd as _run

    nc = _bacc.Bacc("TRN2", target_bir_lowering=False, num_devices=1)
    arrays, args = {}, {}
    for name, value in inputs.items():
        v = _np.ascontiguousarray(value)
        arrays[f"in_{name}"] = v
        args[name] = nc.dram_tensor(f"in_{name}", v.shape, _mybir.dt.from_np(v.dtype), kind="ExternalInput").ap()
    x = args["x"]
    out = nc.dram_tensor("out_x", x.shape, _mybir.dt.float32, kind="ExternalOutput").ap()
    gnn_two_layers(nc, args, out)
    r = _run(nc, [arrays], core_ids=[0])
    return r.results[0]["out_x"]
```

```python
import concourse.bass as bass
from concourse import mybir
from concourse.alu_op_type import AluOpType as ALU
from contextlib import ExitStack


def gnn_two_layers(nc, a, out):
    f32, bf16, i32 = mybir.dt.float32, mybir.dt.bfloat16, mybir.dt.int32
    ACT = mybir.ActivationFunctionType
    AX = mybir.AxisListType

    P = 128
    N, D = a["x"].shape
    E = a["src"].shape[0]
    NT = -(-N // P)
    NFULL = N // P
    NREST = N - NFULL * P
    CT = 16
    T = -(-(-(-E // P) + NT) // (2 * CT)) * 2 * CT
    C = T // CT
    CE = CT * P
    G4 = CT // 4
    TG = 4
    TP = T // TG
    H = 8
    HD = D // H
    F = a["L1_gnn_W1"].shape[1]
    FK = F // P
    DK = D // P
    AW = D + H
    EPAD = (-(-E // P) + 2) * P
    BIG = 1.0e38
    EW = 8704
    EPS = 1e-5
    SCALE = float(HD) ** -0.5
    assert DK == 2 and NT % 2 == 1 and TP <= P and E % 125 == 0 and C >= 6

    def scratch(name, shape, dt):
        return nc.dram_tensor(name, shape, dt, kind="Internal").ap()

    src_pad = scratch("src_pad", (EPAD // P, P), i32)
    dst_pad = scratch("dst_pad", (EPAD // P, P), i32)
    w_pad = scratch("w_pad", (EPAD // P, P), f32)
    brk_rep = scratch("brk_rep", (T, H, 2 * P), f32)
    run_lin = scratch("run_lin", (2, T), f32)
    key_lin = scratch("key_lin", (T * P + P,), f32)
    brk_lin = scratch("brk_lin", (T * P + P,), f32)
    loc_lin = scratch("loc_lin", (T * P,), bf16)
    nt_lin = scratch("nt_lin", (T,), i32)
    sup_tab = scratch("sup_tab", (NT * P, D), f32)
    kv_tab = scratch("kv_tab", (NT * P, 2 * D), f32)
    x2_tab = scratch("x2_tab", (NT * P, D), f32)

    ctx = ExitStack()
    with ctx:
        def sb(name, shape, dt=f32):
            return ctx.enter_context(nc.sbuf_tensor(name, shape, dt))

        def sem(name):
            return ctx.enter_context(nc.semaphore(name))

        BIGR = sb("big_region", [P, 2 * CT * 2 * D])
        Xs = BIGR[:, 0:NT * D].rearrange("p (n d) -> p n d", d=D)
        o = NT * D
        G0 = BIGR[:, o:o + CT * D].rearrange("p (j d) -> p j d", d=D)
        o += CT * D
        W0 = BIGR[:, o:o + DK * D].rearrange("p (k n) -> p k n", k=DK)
        o += DK * D
        WKV = BIGR[:, o:o + DK * 2 * D].rearrange("p (k n) -> p k n", k=DK)
        o += DK * 2 * D
        assert o <= 2 * CT * 2 * D
        KV = BIGR[:, :].rearrange("p (j d) -> p j d", d=2 * D)
        o = 0
        WS = BIGR[:, o:o + DK * D].rearrange("p (k n) -> p k n", k=DK)
        o += DK * D
        WO = BIGR[:, o:o + DK * D].rearrange("p (k n) -> p k n", k=DK)
        o += DK * D
        W1 = BIGR[:, o:o + DK * F].rearrange("p (k n) -> p k n", k=DK)
        o += DK * F
        W2 = BIGR[:, o:o + FK * D].rearrange("p (k n) -> p k n", k=FK)
        o += FK * D
        row = {}
        for k in ("bs", "bo", "b2", "g1", "be1", "g2", "be2"):
            row[k] = BIGR[:, o:o + D]
            o += D
        assert o <= CT * 2 * D

        EDG = sb("edge_region", [P, EW])
        at = [0]

        def prep(shape, dt=f32):
            n = 1
            for s in shape:
                n *= s
            v = EDG[:, at[0]:at[0] + n]
            at[0] += n
            if dt is not f32:
                v = v.bitcast(dt)
            if len(shape) == 2:
                v = v.rearrange("p (a b) -> p a b", b=shape[1])
            return v

        dst_r, src_r, w_r = prep([TG, P], i32), prep([TG, P], i32), prep([TG, P])
        live, key1, loc_m, prev, src_f = [prep([TG, P]) for _ in range(5)]
        brk2 = prep([TG, 2 * P])
        brk, brk_next = brk2[:, :, 0:P], brk2[:, :, P:2 * P]
        loc_b = EDG[:, at[0]:at[0] + TG * P // 2].bitcast(bf16).rearrange("p (a b) -> p a b", b=P)
        at[0] += TG * P // 2
        ge_, ge2, ge3 = [prep([TG, NT - 1]) for _ in range(3)]
        dst_i = prep([E // 125], i32)
        junk = prep([E // 125])
        lns_at = at[0]
        Hn, HT, SO = prep([2, D]), prep([2, D]), prep([2, 2 * D])
        SUP = SO.rearrange("p a (c d) -> p (a c) d", c=2)
        assert at[0] <= EW

        at[0] = 0
        PR = [prep([2, D]) for _ in range(2)]
        AB = prep([4, P])
        WQ = EDG[:, at[0]:at[0] + DK * D].rearrange("p (k n) -> p k n", k=DK)
        OB = prep([4, P])
        BRK = prep([2, 2 * P])
        F1s, F2s, B1s, B2s = [prep([P]) for _ in range(4)]
        QLO = EDG[:, at[0]:at[0] + NT * D // 2].bitcast(bf16).rearrange("p (n d) -> p n d", d=D)
        QF, QR = [EDG[:, k * 2 * D:(k + 1) * 2 * D].rearrange("p (a d) -> p a d", d=D) for k in range(2)]
        assert at[0] + NT * D // 2 <= lns_at

        at[0] = 0
        fin = {k: prep([2, D]) for k in ("x2", "h", "hb", "att", "y", "zT", "zb", "y2", "xo", "out")}
        f1 = {k: prep([D]) for k in ("hT", "sa", "saT", "t", "z", "t2")}
        F1 = prep([FK, P])
        assert at[0] <= EW

        ACC = sb("node_sums", [P, NT, AW])
        QHM = sb("queries", [P, NT, 2 * D], bf16)
        R = sb("edge_rows", [P, G4, 4, AW])
        A = sb("edge_to_node", [P, 2, 4, P])
        OT = sb("node_to_edge", [P, 2, 4, P], bf16)
        LB = sb("loc_rows", [P, 2, CE], bf16)
        L = sb("logits", [P, 2, CT, H])
        DF = sb("logit_minus_max", [P, CT, H])
        EX = sb("exps", [P, 2, CT, H])
        src_e = sb("src_e", [P, T], i32)
        loc_e = sb("loc_e", [P, T])
        w_e = sb("w_e", [P, T])
        SRC = sb("chunk_src", [P, 2, CT], i32)
        LOC = sb("chunk_loc", [P, 2, CT])
        WGT = sb("chunk_w", [P, 2, CT])
        sel_t = sb("sel_t", [P, CT])
        sel_h = sb("sel_h", [P, H])
        sel_hT = sb("sel_hT", [H, CT, H])
        run_f = sb("run_f", [H, T])
        run_b = sb("run_b", [H, T])
        run_br = sb("run_br", [H, T])
        run2 = sb("run2", [P, 2, TG])
        ends = sb("ends", [P, 2, CT])
        cf = sb("cf", [H, 2, CT])
        cb = sb("cb", [H, 2, CT + 1])
        start = sb("start", [P, 2])
        pick = sb("pick", [P, 2, CT])
        nt_row = sb("nt_row", [1, T], i32)
        ident = sb("ident", [P, P])
        iota_j = sb("iota_j", [P, P])
        iota_p = sb("iota_p", [P, 1])
        minus_p = sb("minus_p", [P, 1])
        iota_t = sb("iota_t", [P, TG])
        ones = sb("ones", [P, P])
        zpad = sb("zpad", [1, EPAD - E], i32)
        epsc = sb("epsc", [P, 1])
        cnt_p = sb("cnt_p", [P, NT])
        OFF = sb("OFF", [P, NT + 1])
        nb = sb("nb", [P, NT])
        nti = sb("nti", [P, NT], i32)
        ntf = sb("ntf", [P, NT])
        TB = sb("TB", [P, NT + 1])
        Dd = sb("Dd", [P, NT])
        dD = sb("dD", [P, NT])
        s4 = {k: sb("s4_" + k, [P, TG]) for k in ("DD", "EE", "BK", "E0", "LEN", "B1", "E0c")}
        e0_i = sb("e0_i", [P, TG], i32)
        bk_i = sb("bk_i", [P, TG], i32)
        ST = sb("ln_stats", [P, NT, 6])
        MV = sb("ln_mv", [P, NT, 2])
        RS = sb("ln_rs", [P, NT])
        SD = sb("ln_sd", [P, NT])
        NM = sb("ln_nm", [P, NT])
        row["b0"], row["bq"] = sb("row_b0", [P, D]), sb("row_bq", [P, D])
        row_kv = sb("row_kv", [P, 2 * D])
        b1c = sb("b1c", [P, FK])
        c_d = sb("c_d", [H, 4])
        c_s = sb("c_s", [H, 2])
        c_sel = sb("c_sel", [H, 2, P])
        c_diag = sb("c_diag", [H, 2, H])

        LN_PARTS = (slice(0, 5), slice(5, NT))

        ps = [ctx.enter_context(nc.psum_tensor(f"ps{i}", [P, 512], f32)) for i in range(8)]

        def ge(eng, s, v):
            if not (isinstance(v, int) and v <= 0):
                eng.wait_ge(s, v)

        spare = {}

        def ge_alone(eng, s, v):
            if isinstance(v, int):
                ge(eng, s, v)
                return
            if eng.engine not in spare:
                spare[eng.engine] = eng.alloc_register(f"spare{len(spare)}")
            eng.reg_mov(spare[eng.engine], v)
            eng.wait_ge(S["consts"], 11)
            eng.wait_ge(s, spare[eng.engine])

        def held(eng, v):
            return v if isinstance(v, int) else eng.snap(v)

        def each_node_tile(eng, step):
            step(0, 0, 0)
            step(1, 1, 0)
            step(2, 0, 1)
            step(3, 1, 1)
            with eng.Fori(2, NT // 2) as i:
                step(2 * i, 0, i)
                step(2 * i + 1, 1, i)
            step(NT - 1, 0, NT // 2)

        def each_node_tile_in_fours(eng, step):
            for k in range(4):
                step(k, k, 0)
            with eng.Fori(1, NT // 4) as i:
                for k in range(4):
                    step(4 * i + k, k, i)
            for k in range(NT % 4):
                step(NT // 4 * 4 + k, k, NT // 4)

        def each_chunk(eng, step):
            step(0, 0)
            step(0, 1)
            with eng.Fori(1, C // 2) as i:
                step(i, 0)
                step(i, 1)

        def rows_done(eng, c, k):
            ge_alone(eng, S["r_ready" if k < 2 else "r_ready_2"], 2 * c + k % 2 + 1)

        def each_l1_step(eng, step):
            step(0, 0, True, 0)
            step(0, 1, True, 1)
            step(1, 0, True, 2)
            with eng.Fori(1, C // 2 - 1) as i:
                step(i, 1, True, 3)
                step(i + 1, 0, True, 3)
            step(C // 2 - 1, 1, True, 3)
            step(C // 2, 0, False, 3)

        def before(i, par):
            return (i, 0) if par else (i - 1, 1)

        def each_step(eng, parts):
            least, most = min(l for l, _ in parts), max(l for l, _ in parts)
            first, last = 3, NT - 1 - most
            last -= (last - first + 1) % 2

            def fixed(n):
                for lead, part in parts:
                    m = n + lead
                    if 0 <= m < NT:
                        part(m, m % 2, m // 2)

            for n in range(-most, first):
                fixed(n)
            with eng.Fori(first // 2, (last + 1) // 2) as i:
                for u in range(2):
                    for lead, part in parts:
                        k = first % 2 + u + lead
                        part(2 * i + k, k % 2, i + k // 2)
            for n in range(last + 1, NT - least):
                fixed(n)

        def node(t, n):
            return t[:, bass.ds(n, 1), :].rearrange("p a d -> p (a d)")

        def dma_load(eng, dst, src, s):
            eng.dma_start(dst, src).then_inc(s, 16)

        def flat(t):
            return t.rearrange("a b -> (a b)")

        def w_view(w):
            return w.rearrange("(k p) n -> p k n", p=P)

        def tiles_of(lin, first):
            return lin[first:first + T * P].rearrange("(g p j) -> p g j", g=TG, j=P)

        names = """consts zeroed x_in dst_in w0_in b0_in rows_in pads_in total chain rows_gathered
            e0_ready keys_ready prepared breaks brk_ready next_ready sel_ready
            tr_in tr_out edges_ready acc_set x2_stored acc_clear
            stat stats_ready sd_ready ln_ready ln_h ln_pt ln_ht ln_mm ln_so
            q_left q_first q_second q_ready staged0 onehot0 l0_mm l0_added
            staged_src staged_loc ot_ready qe_done prod_done logit_pairs
            max_moved last_f carry_f max_f carry_b max_b
            df_ready ex_ready c_diff c_exp c_sel_r cs_ready acc_scaled
            ob_ready ab_ready a1_ready r_ready r_ready_2 rden_ready ag_done ag_added cs_done
            fin_w den_ready f_h f_hb f_att f_pt f_hT f_skip f_sa f_sapt f_saT f_wo f_y f_st f_sd f_t
            f_z f_zb f_zpt f_zT f_ff1 f_relu f_ff2 f_y2 f_st2 f_sd2 f_t2 f_xb f_out
            """.split()
        S = {n: sem(n) for n in names}
        so_stored = [sem(f"so_stored{k}") for k in range(4)]
        kv_stored = [sem(f"kv_stored{k}") for k in range(2)]
        landed = [sem(f"pair_in{j}") for j in range(CT)]
        landed_before = [32 * C, 0]
        NT_STORED = TG * 16
        NT_IN = NT_STORED + 16
        KEY_STORED = NT_IN + 32
        PREV_IN = KEY_STORED + 16
        LOC_STORED = PREV_IN + 16
        BRK_STORED = 32
        NEXT_IN = BRK_STORED + 16
        REP_STORED = NEXT_IN + H * 16
        RUN_STORED = REP_STORED + 2 * TG * 16
        RUN_IN = RUN_STORED + 32
        lb_in = [sem(f"loc_rows_in{k}") for k in range(2)]
        brk_in = [sem(f"breaks_in{k}") for k in range(2)]
        x2_in = [sem(f"x2_in{k}") for k in range(2)]
        xo_in = [sem(f"xo_in{k}") for k in range(2)]
        out_stored = [sem(f"out_stored{k}") for k in range(2)]

        RD = sb("inv_den", [P, NT, H])
        fst = sb("fst", [P, 2, 6])
        fmv = sb("fmv", [P, 2, 2])
        fsd, frs = sb("fsd", [P, 2]), sb("frs", [P, 2])
        edge_c = sb("edge_c", [1, 2])
        below = sb("below", [H, 1])

        block = ctx.enter_context(nc.Block())

        @block.sync
        def _(sp):
            load = lambda dst, src, s: dma_load(sp, dst, src, s)
            load(dst_i[0:125, :], a["dst"].rearrange("(p n) -> p n", p=125), S["dst_in"])
            sp.wait_ge(S["zeroed"], 1)
            load(Xs[:, 0:NFULL, :], a["x"][0:NFULL * P, :].rearrange("(n p) d -> p n d", p=P), S["x_in"])
            load(Xs[0:NREST, NFULL, :], a["x"][NFULL * P:N, :], S["x_in"])
            load(W0, w_view(a["L0_gnn_W"]), S["w0_in"])
            load(row["b0"][:, :], a["L0_gnn_b"].partition_broadcast(P), S["b0_in"])
            load(WKV[:, :, 0:D], w_view(a["L1_gnn_Wk"]), S["rows_in"])
            load(WKV[:, :, D:2 * D], w_view(a["L1_gnn_Wv"]), S["rows_in"])
            load(row["bq"][:, :], a["L1_gnn_bq"].partition_broadcast(P), S["rows_in"])
            load(row_kv[:, 0:D], a["L1_gnn_bk"].partition_broadcast(P), S["rows_in"])
            load(row_kv[:, D:2 * D], a["L1_gnn_bv"].partition_broadcast(P), S["rows_in"])
            with nc.allow_non_contiguous_dma(reason="one column per 128 biases, 4 KiB in all"):
                load(b1c[:, :], a["L1_gnn_b1"].rearrange("(m p) -> p m", p=P), S["fin_w"])

            def store_support(n, slot, i):
                first = held(sp, n * P)
                sp.wait_ge(S["ln_so"], n + 1)
                sp.dma_start(sup_tab[bass.ds(first, P), :], SUP[:, slot, :]).then_inc(so_stored[slot], 16)

            each_node_tile_in_fours(sp, store_support)

            sp.wait_ge(S["prepared"], LOC_STORED)
            sp.wait_ge(S["brk_ready"], 1)
            sp.dma_start(tiles_of(brk_lin, 0), brk[0:TP]).then_inc(S["breaks"], 16)
            sp.dma_start(brk_lin[T * P:T * P + 1].rearrange("(a n) -> a n", a=1), edge_c[:, 1:2]
                           ).then_inc(S["breaks"], 16)
            sp.wait_ge(S["breaks"], BRK_STORED)
            sp.dma_start(brk_next[0:TP], tiles_of(brk_lin, 1)).then_inc(S["breaks"], 16)
            sp.wait_ge(S["breaks"], NEXT_IN)
            for h in range(H):
                sp.dma_start(brk_rep[:, h, :].rearrange("(g p) j -> p g j", g=TG), brk2[0:TP]
                               ).then_inc(S["breaks"], 16)
            sp.wait_ge(S["breaks"], REP_STORED)
            sp.wait_ge(S["next_ready"], 1)
            for v in range(2):
                for k in range(TG):
                    with nc.allow_non_contiguous_dma(reason="one number per edge tile"):
                        sp.dma_start(run_lin[v, k * TP:(k + 1) * TP].rearrange("(p n) -> p n", n=1),
                                       run2[0:TP, v, k:k + 1]).then_inc(S["breaks"], 16)
            sp.wait_ge(S["breaks"], RUN_STORED)
            sp.dma_start(run_f[:, :], run_lin[0, :].partition_broadcast(H)).then_inc(S["breaks"], 16)
            sp.dma_start(run_b[:, :], run_lin[1, :].partition_broadcast(H)).then_inc(S["breaks"], 16)

            sp.wait_ge(S["breaks"], RUN_IN)
            load(WQ, w_view(a["L1_gnn_Wq"]), S["rows_in"])
            sp.wait_ge(S["l0_added"], T)
            sp.dma_start(x2_tab.rearrange("(n p) d -> p n d", p=P), ACC[:, :, 0:D]).then_inc(S["x2_stored"], 16)

            def store_kv(n, par, i):
                first = held(sp, n * P)
                sp.wait_ge(S["ln_so"], NT + n + 1)
                sp.dma_start(kv_tab[bass.ds(first, P), :], SO[:, par, :]).then_inc(kv_stored[par], 16)

            each_node_tile(sp, store_kv)

            sp.wait_ge(S["breaks"], REP_STORED)
            sp.wait_ge(kv_stored[0], 16 * (NT // 2 + 1))
            sp.wait_ge(kv_stored[1], 16 * (NT // 2))

            def load_chunk(i, par):
                c = 2 * i + par
                first, used = held(sp, c * CE), held(sp, c - 1)
                ge(sp, S["ot_ready"], G4 * (c - 1))
                ge(sp, S["c_sel_r"], used)
                sp.dma_start(LB[:, par, :], loc_lin[bass.ds(first, CE)].partition_broadcast(P)
                             ).then_inc(lb_in[par], 16)
                first = held(sp, c * CT * H)
                ge_alone(sp, S["max_b"], 3 * (c - 1))
                ge_alone(sp, S["c_diff"], 2 * (c - 1))
                sp.dma_start(BRK[:, par, :], brk_rep.rearrange("t h j -> (t h) j")[bass.ds(first, P), :]
                             ).then_inc(brk_in[par], 16)

            each_chunk(sp, load_chunk)

            sp.wait_ge(S["r_ready"], 2 * (C - 1))
            sp.wait_ge(S["r_ready_2"], 2 * (C - 1))
            sp.wait_ge(S["logit_pairs"], 2 * G4 * (C - 1))
            for k, n in (("bs", "bskip"), ("bo", "bo"), ("b2", "b2"), ("g1", "g1"), ("be1", "be1"),
                         ("g2", "g2"), ("be2", "be2")):
                load(row[k][:, :], a["L1_gnn_" + n].partition_broadcast(P), S["fin_w"])
            load(WS, w_view(a["L1_gnn_Wskip"]), S["fin_w"])
            load(WO, w_view(a["L1_gnn_Wo"]), S["fin_w"])
            load(W1, w_view(a["L1_gnn_W1"]), S["fin_w"])
            load(W2, w_view(a["L1_gnn_W2"]), S["fin_w"])

            sp.wait_ge(S["max_b"], 3 * C)
            sp.wait_ge(S["logit_pairs"], 2 * G4 * C)
            sp.wait_ge(S["a1_ready"], G4 * C)

            def load_x2(n, par, i):
                first = held(sp, n * P)
                ge(sp, S["f_h"], n - 1)
                sp.dma_start(fin["x2"][:, par, :], x2_tab[bass.ds(first, P), :]).then_inc(x2_in[par], 16)

            def load_xo(n, par, i):
                first = held(sp, n * P)
                ge(sp, S["f_out"], n - 1)
                sp.dma_start(fin["xo"][:, par, :], x2_tab[bass.ds(first, P), :]).then_inc(xo_in[par], 16)

            def store_out(n, par, i):
                first = held(sp, n * P)
                sp.wait_ge(S["f_out"], n + 1)
                if isinstance(n, int) and n == NT - 1:
                    sp.dma_start(out[NFULL * P:N, :], fin["out"][0:NREST, par, :]).then_inc(out_stored[par], 16)
                else:
                    sp.dma_start(out[bass.ds(first, P), :], fin["out"][:, par, :]).then_inc(out_stored[par], 16)

            each_step(sp, [(4, load_x2), (0, load_xo), (-2, store_out)])
            sp.wait_ge(out_stored[0], 16 * (NT // 2 + 1))
            sp.wait_ge(out_stored[1], 16 * (NT // 2))

        @block.gpsimd
        def _(pool):
            g = nc.gpsimd
            g.memset(Xs[:, NFULL, :], 0.0).then_inc(S["zeroed"], 1)
            g.memset(zpad[:, :], 0).then_inc(S["consts"], 1)
            g.memset(ident[:, :], 0.0).then_inc(S["consts"], 1)
            g.iota(iota_j[:, :], [[1, P]], base=0, channel_multiplier=0,
                   allow_small_or_imprecise_dtypes=True).then_inc(S["consts"], 1)
            g.iota(iota_p[:, :], [[0, 1]], base=0, channel_multiplier=1,
                   allow_small_or_imprecise_dtypes=True).then_inc(S["consts"], 1)
            g.iota(iota_t[:, :], [[TP, TG]], base=0, channel_multiplier=1,
                   allow_small_or_imprecise_dtypes=True).then_inc(S["consts"], 1)
            g.memset(ones[:, :], 1.0).then_inc(S["consts"], 1)
            g.memset(epsc[:, :], EPS).then_inc(S["consts"], 1)
            g.memset(edge_c[:, 0:1], -1.0).then_inc(S["consts"], 1)
            g.memset(edge_c[:, 1:2], -BIG).then_inc(S["consts"], 1)
            g.memset(below[:, :], -BIG).then_inc(S["consts"], 1)
            pool.wait_ge(S["consts"], 2)
            g.affine_select(out=ident[:, :], in_=ident[:, :], compare_op=ALU.not_equal, fill=1.0, base=0,
                            pattern=[[-1, P]], channel_multiplier=1).then_inc(S["consts"], 1)
            pool.wait_ge(S["consts"], 11)

            for dst, src, z in ((src_pad, a["src"], zpad[:, :]), (dst_pad, a["dst"], zpad[:, :]),
                                (w_pad, a["edge_weight"], zpad[:, :].bitcast(f32))):
                pool.dma_start(flat(dst)[0:E].rearrange("(p n) -> p n", p=125),
                               src.rearrange("(p n) -> p n", p=125)).then_inc(S["pads_in"], 16)
                pool.dma_start(flat(dst)[E:EPAD].rearrange("(p n) -> p n", p=1), z).then_inc(S["pads_in"], 16)
            pool.wait_ge(S["pads_in"], 6 * 16)
            pool.wait_ge(S["e0_ready"], 1)
            for dst, src in ((dst_r, dst_pad), (src_r, src_pad), (w_r, w_pad)):
                for k in range(TG):
                    pool.indirect_dma_start(dst[0:TP, k, :], None, flat(src).rearrange("(a n) -> a n", a=1),
                                            bass.IndirectOffsetOnAxis(e0_i[0:TP, k:k + 1], 1)
                                            ).then_inc(S["rows_gathered"], 16)
            for k in range(TG):
                with nc.allow_non_contiguous_dma(reason="one number per edge tile"):
                    pool.dma_start(nt_lin[k * TP:(k + 1) * TP].rearrange("(p n) -> p n", n=1),
                                   bk_i[0:TP, k:k + 1]).then_inc(S["prepared"], 16)
            pool.wait_ge(S["prepared"], NT_STORED)
            pool.dma_start(nt_row[:, :], nt_lin.rearrange("(a n) -> a n", a=1)).then_inc(S["prepared"], 16)
            pool.wait_ge(S["prepared"], NT_IN)
            pool.wait_ge(S["keys_ready"], 1)
            pool.dma_start(tiles_of(key_lin, 1), key1[0:TP]).then_inc(S["prepared"], 16)
            pool.dma_start(key_lin[0:1].rearrange("(a n) -> a n", a=1), edge_c[:, 0:1]).then_inc(S["prepared"], 16)
            pool.wait_ge(S["prepared"], KEY_STORED)
            pool.dma_start(prev[0:TP], tiles_of(key_lin, 0)).then_inc(S["prepared"], 16)
            pool.wait_ge(S["keys_ready"], 2)
            pool.wait_ge(S["prepared"], PREV_IN)
            pool.dma_start(tiles_of(loc_lin, 0), loc_b[0:TP]).then_inc(S["prepared"], 16)

            for k in range(4):
                pool.wait_ge(so_stored[k], 16 * len(range(k, NT, 4)))

            def gather_support(i, par):
                c = 2 * i + par
                pool.wait_ge(S["staged0"], 3 * c + 1)
                for j in range(CT):
                    ge_alone(pool, S["l0_mm"], CT * (c - 1) + j + 1)
                    pool.indirect_dma_start(G0[:, j, :], None, sup_tab,
                                            bass.IndirectOffsetOnAxis(SRC[:, par, j:j + 1], 0)
                                            ).then_inc(landed[j // 2], 16)

            each_chunk(pool, gather_support)

            pool.wait_ge(kv_stored[0], 16 * (NT // 2 + 1))
            pool.wait_ge(kv_stored[1], 16 * (NT // 2))

            def rows(i, par, k):
                c = 2 * i + par
                ge(pool, S["ag_done"], CT * (c - 1) + 4 * (k + 1))
                pool.wait_ge(S["ex_ready"], c + 1)
                j = par * CT + 4 * k
                g.tensor_tensor(R[:, k, :, 0:D].rearrange("p t (h d) -> p t h d", d=HD),
                                KV[:, j:j + 4, D:2 * D].rearrange("p t (h d) -> p t h d", d=HD),
                                EX[:, par, 4 * k:4 * k + 4, :].unsqueeze(3).to_broadcast([P, 4, H, HD]),
                                ALU.mult).then_inc(S["r_ready_2"], 1)

            def gather_kv(i, par):
                c = 2 * i + par
                later = not (isinstance(i, int) and i == 0)
                pool.wait_ge(S["staged_src"], c + 1)
                for j in range(CT):
                    if later and j % 4 == 0:
                        rows_done(pool, c - 2, j // 4)
                    pool.indirect_dma_start(KV[:, par * CT + j, :], None, kv_tab,
                                            bass.IndirectOffsetOnAxis(SRC[:, par, j:j + 1], 0)
                                            ).then_inc(landed[(par * CT + j) // 2], 16)
                    if later and j in (3, 7):
                        rows(i - 1, par, 2 + j // 4)

            gather_kv(0, 0)
            gather_kv(0, 1)
            pool.wait_ge(S["x2_stored"], 16)
            pool.wait_ge(S["ln_h"], 3 * NT)
            g.memset(ACC[:, :, :], 0.0).then_inc(S["acc_clear"], 1)
            gather_kv(1, 0)
            gather_kv(1, 1)
            with pool.Fori(2, C // 2) as i:
                gather_kv(i, 0)
                gather_kv(i, 1)
            for par in range(2):
                for k in (2, 3):
                    rows(C // 2 - 1, par, k)

            pool.wait_ge(S["fin_w"], 12 * 16)
            pool.wait_ge(S["den_ready"], 2)

            def attention(n, par, i):
                ge(pool, S["f_sa"], n - 1)
                g.tensor_tensor(fin["att"][:, par, :].rearrange("p (h d) -> p h d", d=HD),
                                ACC[:, bass.ds(n, 1), 0:D].rearrange("p a (h d) -> p (a h) d", d=HD),
                                RD[:, bass.ds(n, 1), :].rearrange("p a h -> p (a h)").unsqueeze(2)
                                .to_broadcast([P, H, HD]), ALU.mult).then_inc(S["f_att"], 1)
                pool.wait_ge(S["f_att"], 2 * n + 1)
                g.tensor_tensor(fin["att"][:, par, :], fin["att"][:, par, :], row["bs"][:, :], ALU.add
                                ).then_inc(S["f_att"], 1)

            def rows_and_bias(n, par, i):
                pool.wait_ge(S["f_h"], n + 1)
                ge(pool, S["f_y"], n - 1)
                g.tensor_tensor(fin["hb"][:, par, :], fin["h"][:, par, :], row["bo"][:, :], ALU.add
                                ).then_inc(S["f_hb"], 1)

            def z_and_bias(n, par, i):
                pool.wait_ge(S["f_z"], n + 1)
                ge(pool, S["f_y2"], n - 1)
                g.tensor_tensor(fin["zb"][:, par, :], f1["z"][:, :], row["b2"][:, :], ALU.add
                                ).then_inc(S["f_zb"], 1)

            def x_and_bias(n, par, i):
                pool.wait_ge(xo_in[par], 16 * (i + 1))
                g.tensor_tensor(fin["xo"][:, par, :], fin["xo"][:, par, :], row["be2"][:, :], ALU.add
                                ).then_inc(S["f_xb"], 1)

            each_step(pool, [(2, attention), (-1, x_and_bias), (2, rows_and_bias), (1, z_and_bias)])

        @block.scalar
        def _(act):
            A_ = nc.scalar.activation

            def node_acts(before, rows, queries):
                def deviations(k):
                    act.wait_ge(S["stats_ready"], 2 * (before // NT) + k + 1)
                    A_(SD[:, LN_PARTS[k]], MV[:, LN_PARTS[k], 1], ACT.Sqrt, bias=epsc[:, :]).then_inc(S["sd_ready"], 1)
                    act.wait_ge(S["ln_ready"], 4 * (before // NT) + 2 * (k + 1))

                def norm(n, par):
                    ge(act, S["ln_pt"], before + n - 1)
                    A_(Hn[:, par, :], node(rows, n), ACT.Relu, bias=NM[:, bass.ds(n, 1)],
                       scale=RS[:, bass.ds(n, 1)]).then_inc(S["ln_h"], 1)

                def first_bits(m, par):
                    act.wait_ge(S["ln_so"], before + m + 1)
                    A_(node(QHM, m)[:, 0:D], QF[:, par, :], ACT.Copy).then_inc(S["q_first"], 1)

                def second_bits(m, par):
                    act.wait_ge(S["q_left"], m + 1)
                    A_(node(QHM, m)[:, D:2 * D], QR[:, par, :], ACT.Copy).then_inc(S["q_second"], 1)

                def step(n, par, i):
                    if not (isinstance(n, int) and n == NT - 1):
                        norm(n + 1, 1 - par)
                    if not queries:
                        act.wait_ge(S["ln_pt"], before + n + 1)
                        ge(act, S["ln_mm"], before + n - 1)
                        A_(HT[:, par, :], ps[par][:, 0:D], ACT.Copy).then_inc(S["ln_ht"], 1)
                    if not queries and isinstance(n, int) and n == 1:
                        deviations(1)
                    if queries and not (isinstance(n, int) and n < 1):
                        first_bits(n - 1, 1 - par)
                    if queries and not (isinstance(n, int) and n < 2):
                        second_bits(n - 2, par)

                if not queries:
                    deviations(0)
                norm(0, 0)
                each_node_tile(act, step)
                if queries:
                    first_bits(NT - 1, 0)
                    second_bits(NT - 2, 1)
                    second_bits(NT - 1, 0)

            act.wait_ge(S["consts"], 11)
            node_acts(0, Xs, False)
            node_acts(NT, ACC[:, :, 0:D], False)
            node_acts(2 * NT, ACC[:, :, 0:D], True)

            def node_to_edge(i, par, k):
                G = G4 * (2 * i + par) + k
                if k == 0:
                    act.wait_ge(lb_in[par], 16 * (i + 1))
                ge(act, S["ot_ready"], G)
                A_(OB.rearrange("p t e -> p (t e)"), LB[:, par, 4 * P * k:4 * P * (k + 1)], ACT.Abs,
                   bias=minus_p[:, :]).then_inc(S["ob_ready"], 1)
                act.wait_ge(S["ob_ready"], G + 1)
                ge(act, S["qe_done"], 2 * (G - 1))
                A_(OT[:, k % 2], OB[:, :, :], ACT.Relu, bias=1.0, scale=-1.0).then_inc(S["ot_ready"], 1)

            def edge_to_node(i, par, k):
                G = G4 * (2 * i + par) + k
                ge(act, S["a1_ready"], G)
                if k == 0:
                    act.wait_ge(S["staged_loc"], 2 * i + par + 1)
                for t in range(4):
                    last = A_(AB[:, t, :], iota_j[:, :], ACT.Abs, bias=LOC[:, par, 4 * k + t:4 * k + t + 1])
                last.then_inc(S["ab_ready"], 1)
                act.wait_ge(S["ab_ready"], G + 1)
                ge(act, S["ag_done"], 4 * (G - 1))
                A_(A[:, k % 2], AB[:, :, :], ACT.Relu, bias=1.0, scale=-1.0).then_inc(S["a1_ready"], 1)

            def denominators(i, par, k):
                c = 2 * i + par
                G = G4 * c + k
                act.wait_ge(S["ex_ready"], c + 1)
                ge(act, S["ag_done"], CT * (c - 1) + 4 * (k + 1))
                A_(R[:, k, :, D:AW], EX[:, par, 4 * k:4 * k + 4, :], ACT.Copy).then_inc(S["rden_ready"], 1)

            def l1_step(i, par, has_c, p):
                c = 2 * i + par
                pi, pp = before(i, par)
                if has_c:
                    for k in range(0 if p == 0 else 1, 2):
                        node_to_edge(i, par, k)
                if p >= 2:
                    edge_to_node(i - 1, par, 3)
                    denominators(i - 1, par, 3)
                if has_c:
                    for k in range(2, G4):
                        node_to_edge(i, par, k)
                if p >= 1:
                    A_(LOC[:, pp, :], loc_e[:, bass.ds((c - 1) * CT, CT)], ACT.Copy, scale=-1.0
                       ).then_inc(S["staged_loc"], 1)
                    edge_to_node(pi, pp, 0)
                    if p >= 2:
                        act.wait_ge(S["c_diff"], 2 * (c - 1))
                        ge(act, S["cs_ready"], c - 2)
                        A_(c_s[:, pp:pp + 1], c_d[:, 2:3], ACT.Exp, scale=SCALE).then_inc(S["c_exp"], 1)
                    act.wait_ge(S["df_ready"], c)
                    ge(act, S["r_ready"], 2 * (c - 2))
                    ge(act, S["r_ready_2"], 2 * (c - 2))
                    A_(EX[:, pp], DF[:, :, :], ACT.Exp, scale=SCALE).then_inc(S["ex_ready"], 1)
                    denominators(pi, pp, 0)
                    edge_to_node(pi, pp, 1)
                    denominators(pi, pp, 1)
                if has_c and not (isinstance(i, int) and c == C - 1):
                    node_to_edge(i + par, 1 - par, 0)
                if p >= 1:
                    edge_to_node(pi, pp, 2)
                    denominators(pi, pp, 2)

            act.wait_ge(S["sel_ready"], 1)
            each_l1_step(act, l1_step)
            edge_to_node(C // 2 - 1, 1, 3)
            denominators(C // 2 - 1, 1, 3)

            def rows_of(n, par, i):
                act.wait_ge(x2_in[par], 16 * (i + 1))
                ge(act, S["f_pt"], n - 1)
                ge(act, S["f_hb"], n - 1)
                A_(fin["h"][:, par, :], fin["x2"][:, par, :], ACT.Relu, bias=NM[:, bass.ds(n, 1)],
                   scale=RS[:, bass.ds(n, 1)]).then_inc(S["f_h"], 1)

            def rows_across(n, par, i):
                act.wait_ge(S["f_pt"], n + 1)
                ge(act, S["f_skip"], n)
                A_(f1["hT"][:, :], ps[0][:, 0:D], ACT.Copy).then_inc(S["f_hT"], 1)

            def attention_across(n, par, i):
                act.wait_ge(S["f_sapt"], n + 1)
                ge(act, S["f_wo"], n)
                A_(f1["saT"][:, :], ps[2][:, 0:D], ACT.Copy).then_inc(S["f_saT"], 1)

            def deviation(n, par, i):
                act.wait_ge(S["f_st"], 2 * (n + 1))
                ge(act, S["f_t"], 2 * n)
                A_(fsd[:, 0:1], fmv[:, 0, 1:2], ACT.Sqrt, bias=epsc[:, :]).then_inc(S["f_sd"], 1)

            def z_across(n, par, i):
                act.wait_ge(S["f_zpt"], n + 1)
                ge(act, S["f_ff1"], 2 * (n - 1))
                A_(fin["zT"][:, par, :], ps[4][:, 0:D], ACT.Copy).then_inc(S["f_zT"], 1)

            def relus(part):
                def half(n, par, i):
                    act.wait_ge(S["f_ff1"], 2 * n + part + 1)
                    ge(act, S["f_ff2"], n)
                    for m in range(4 * part, 4 * part + 4):
                        last = A_(F1[:, m, :], ps[5 + part][:, m % 4 * P:(m % 4 + 1) * P], ACT.Relu,
                                  bias=b1c[:, m:m + 1])
                    last.then_inc(S["f_relu"], 1)
                return half

            def deviation2(n, par, i):
                act.wait_ge(S["f_st2"], 2 * (n + 1))
                ge(act, S["f_t2"], 2 * n)
                A_(fsd[:, 1:2], fmv[:, 1, 1:2], ACT.Sqrt, bias=epsc[:, :]).then_inc(S["f_sd2"], 1)

            act.wait_ge(S["fin_w"], 12 * 16)
            act.wait_ge(S["max_b"], 3 * C)
            each_step(act, [(-1, deviation2), (2, rows_across), (0, relus(0)), (3, rows_of),
                            (2, attention_across), (0, relus(1)), (1, z_across), (2, deviation)])

        @block.vector
        def _(dve):
            V = nc.vector
            chained = [0]

            def link(ins):
                chained[0] += 1
                ins.then_inc(S["chain"], 1)
                dve.wait_ge(S["chain"], chained[0])

            def layer_norm_stats(before, rows):
                for k, part in enumerate(LN_PARTS):
                    for n in range(part.start, part.stop):
                        V.bn_stats(ST[:, n, :], rows[:, n, :]).then_inc(S["stat"], 1)
                    dve.wait_ge(S["stat"], before * NT + part.stop)
                    for n in range(part.start, part.stop):
                        last = V.bn_aggr(MV[:, n, :], ST[:, n, :])
                    last.then_inc(S["stats_ready"], 1)
                    dve.wait_ge(S["sd_ready"], 2 * before + k + 1)
                    dve.wait_ge(S["stats_ready"], 2 * before + k + 1)
                    V.reciprocal(RS[:, part], SD[:, part]).then_inc(S["ln_ready"], 1)
                    dve.wait_ge(S["ln_ready"], 4 * before + 2 * k + 1)
                    V.scalar_tensor_tensor(NM[:, part], MV[:, part, 0], -1.0, RS[:, part], ALU.mult, ALU.mult
                                           ).then_inc(S["ln_ready"], 1)

            dve.wait_ge(S["consts"], 11)
            dve.wait_ge(S["dst_in"], 16)
            for b in range(NT):
                link(V.tensor_scalar(junk[0:125, :], dst_i[0:125, :], float(P * (b + 1)), None, ALU.is_lt,
                                     ALU.add, accum_out=cnt_p[0:125, b:b + 1]))
            V.tensor_scalar(minus_p[:, :], iota_p[:, :], -1.0, None, ALU.mult).then_inc(S["sel_ready"], 1)
            V.memset(TB[:, 0:1], 0.0)
            V.memset(OFF[:, 0:1], 0.0)
            V.tensor_reduce(sel_t[:, :], ident[:, :].rearrange("p (t h) -> p t h", h=H), AX.X, ALU.add
                            ).then_inc(S["sel_ready"], 1)
            V.tensor_reduce(sel_h[:, :], ident[:, :].rearrange("p (t h) -> p h t", h=H), AX.X, ALU.add
                            ).then_inc(S["sel_ready"], 1)
            V.tensor_copy(sel_hT[:, :, :], ident[0:H, 0:H].unsqueeze(1).to_broadcast([H, CT, H])
                          ).then_inc(S["sel_ready"], 1)
            dve.wait_ge(S["total"], 1)
            link(V.tensor_copy(OFF[:, 1:NT + 1], ps[4][:, 0:NT]))
            link(V.tensor_tensor(nb[:, :], OFF[:, 1:NT + 1], OFF[:, 0:NT], ALU.subtract))
            link(V.tensor_scalar(nti[:, :], nb[:, :], 1.0 / P, (P - 1.0) / P - 0.5 + 1.0 / 512, ALU.mult, ALU.add))
            link(V.tensor_copy(ntf[:, :], nti[:, :]))
            link(V.tensor_tensor_scan(TB[:, 1:NT + 1], ones[:, 0:NT], ntf[:, :], 0.0, ALU.mult, ALU.add))
            link(V.scalar_tensor_tensor(Dd[:, :], TB[:, 0:NT], -float(P), OFF[:, 0:NT], ALU.mult, ALU.add))
            link(V.tensor_tensor(dD[:, 0:NT - 1], Dd[:, 1:NT], Dd[:, 0:NT - 1], ALU.subtract))
            B = [P, TG, NT - 1]

            def over_tiles(v):
                return v.unsqueeze(1).to_broadcast(B)

            link(V.tensor_tensor(ge_, iota_t[:, :].unsqueeze(2).to_broadcast(B), over_tiles(TB[:, 1:NT]), ALU.is_ge))
            link(V.tensor_tensor(ge2, ge_, over_tiles(dD[:, 0:NT - 1]), ALU.mult))
            link(V.tensor_tensor(ge3, ge_, over_tiles(nb[:, 1:NT]), ALU.mult))
            link(V.tensor_reduce(s4["BK"][:, :], ge_, AX.X, ALU.add))
            link(V.tensor_reduce(s4["DD"][:, :], ge2, AX.X, ALU.add))
            link(V.tensor_reduce(s4["EE"][:, :], ge3, AX.X, ALU.add))
            link(V.scalar_tensor_tensor(s4["E0"][:, :], iota_t[:, :], float(P), s4["DD"][:, :], ALU.mult, ALU.add))
            link(V.scalar_tensor_tensor(s4["LEN"][:, :], s4["EE"][:, :], OFF[:, 1:2], s4["E0"][:, :],
                                        ALU.add, ALU.subtract))
            link(V.tensor_scalar(bk_i[:, :], s4["BK"][:, :], 1.0, None, ALU.mult))
            link(V.tensor_scalar(s4["B1"][:, :], s4["BK"][:, :], float(P), 1.0, ALU.mult, ALU.add))
            link(V.tensor_scalar(e0_i[:, :], s4["E0"][:, :], float(E), None, ALU.min))
            V.memset(junk[:, 0:1], 0.0).then_inc(S["e0_ready"], 1)
            dve.wait_ge(S["x_in"], 32)
            layer_norm_stats(0, Xs)
            def over_edges(v):
                return v[0:TP, :].unsqueeze(2).to_broadcast([TP, TG, P])

            link(V.tensor_tensor(live[0:TP], iota_j[0:TP, :].unsqueeze(1).to_broadcast([TP, TG, P]),
                                 over_edges(s4["LEN"]), ALU.is_lt))
            dve.wait_ge(S["rows_gathered"], 3 * TG * 16)
            V.scalar_tensor_tensor(key1[0:TP], dst_r[0:TP], 1.0, live[0:TP], ALU.add, ALU.mult
                                   ).then_inc(S["keys_ready"], 1)
            dve.wait_ge(S["keys_ready"], 1)
            link(V.tensor_tensor(loc_m[0:TP], key1[0:TP], over_edges(s4["B1"]), ALU.subtract))
            V.tensor_copy(loc_b[0:TP], loc_m[0:TP]).then_inc(S["keys_ready"], 1)
            V.tensor_copy(src_f[0:TP], src_r[0:TP]).then_inc(S["tr_in"], 1)

            def support(n, slot, i):
                dve.wait_ge(S["ln_mm"], n + 1)
                ge(dve, so_stored[slot], 16 * i)
                V.tensor_copy(SUP[:, slot, :], ps[2 + slot % 2][:, 0:D]).then_inc(S["ln_so"], 1)

            each_node_tile_in_fours(dve, support)
            dve.wait_ge(S["tr_out"], 1)
            V.tensor_copy(loc_e[:, :], ps[5][:, 0:T])
            V.tensor_copy(src_e[:, :], ps[6][:, 0:T])
            V.tensor_copy(w_e[:, :], ps[7][:, 0:T]).then_inc(S["edges_ready"], 1)
            dve.wait_ge(S["edges_ready"], 1)
            dve.wait_ge(S["b0_in"], 16)
            dve.wait_ge(S["prepared"], NT_IN)

            regs = [dve.alloc_register(f"dve_nt{k}") for k in range(4)]

            def node_tiles(first):
                dve.load(regs, nt_row[0:1, bass.ds(first, 4)])
                return [dve.snap(r, min_val=0, max_val=NT - 1) for r in regs]

            def stage0(i, par):
                c = 2 * i + par
                cols = bass.ds(c * CT, CT)
                V.tensor_copy(SRC[:, par, :], src_e[:, cols]).then_inc(S["staged0"], 1)
                V.tensor_copy(LOC[:, par, :], loc_e[:, cols]).then_inc(S["staged0"], 1)
                V.tensor_copy(WGT[:, par, :], w_e[:, cols]).then_inc(S["staged0"], 1)

            def weights(i, par, k):
                c = 2 * i + par
                ge(dve, S["l0_mm"], CT * c + 4 * (k - 1))
                for t in range(4):
                    j = 4 * k + t
                    last = V.tensor_scalar(A[:, k % 2, t, :], iota_j[:, :], LOC[:, par, j:j + 1],
                                           WGT[:, par, j:j + 1], ALU.is_equal, ALU.mult)
                last.then_inc(S["onehot0"], 1)

            def sums0(i, par):
                c = 2 * i + par
                dve.wait_ge(S["staged0"], 3 * c + 3)
                if not (isinstance(i, int) and i == C // 2 - 1 and par):
                    stage0(i + par, 1 - par)
                weights(i, par, 0)
                for k in range(G4):
                    if k + 1 < G4:
                        weights(i, par, k + 1)
                    nt = node_tiles(c * CT + 4 * k)
                    for t in range(4):
                        n = c * CT + 4 * k + t
                        dve.wait_ge(S["l0_mm"], n + 1)
                        ge(dve, S["l0_added"], n)
                        s_ = ACC[:, bass.ds(nt[t], 1), 0:D].rearrange("p a d -> p (a d)")
                        V.tensor_tensor(s_, ps[t][:, 0:D], s_, ALU.add).then_inc(S["l0_added"], 1)

            stage0(0, 0)
            V.tensor_tensor(ACC[:, :, 0:D], Xs, row["b0"][:, :].unsqueeze(1).to_broadcast([P, NT, D]), ALU.add
                            ).then_inc(S["acc_set"], 1)
            dve.wait_ge(S["acc_set"], 1)
            sums0(0, 0)
            dve.wait_ge(S["prepared"], PREV_IN)
            link(V.tensor_tensor(brk[0:TP], key1[0:TP], prev[0:TP], ALU.not_equal))
            V.tensor_scalar(brk[0:TP], brk[0:TP], -BIG, None, ALU.mult).then_inc(S["brk_ready"], 1)
            sums0(0, 1)
            dve.wait_ge(S["brk_ready"], 1)
            dve.wait_ge(S["breaks"], NEXT_IN)
            V.tensor_reduce(run2[0:TP, 0, :], brk[0:TP], AX.X, ALU.min)
            V.tensor_reduce(run2[0:TP, 1, :], brk_next[0:TP], AX.X, ALU.min).then_inc(S["next_ready"], 1)
            with dve.Fori(1, C // 2 - 1) as i:
                sums0(i, 0)
                sums0(i, 1)
            sums0(C // 2 - 1, 0)
            sums0(C // 2 - 1, 1)

            dve.wait_ge(S["l0_added"], T)
            layer_norm_stats(1, ACC[:, :, 0:D])
            dve.wait_ge(S["rows_in"], 6 * 16)

            def keys_and_values(n, par, i):
                dve.wait_ge(S["ln_mm"], NT + n + 1)
                ge(dve, kv_stored[par], 16 * i)
                V.tensor_tensor(SO[:, par, :], ps[4 + par][:, :], row_kv[:, :], ALU.add).then_inc(S["ln_so"], 1)

            each_node_tile(dve, keys_and_values)

            def stage_src(i, par):
                V.tensor_copy(SRC[:, par, :], src_e[:, bass.ds((2 * i + par) * CT, CT)]).then_inc(S["staged_src"], 1)

            stage_src(0, 0)
            stage_src(0, 1)

            def less_first(m, par):
                dve.wait_ge(S["q_first"], m + 1)
                ge(dve, S["q_ready"], m - 1)
                V.tensor_tensor(QR[:, par, :], QF[:, par, :], node(QHM, m)[:, 0:D], ALU.subtract
                                ).then_inc(S["q_left"], 1)

            def less_second(m, par):
                dve.wait_ge(S["q_second"], m + 1)
                V.tensor_tensor(node(QLO, m), QR[:, par, :], node(QHM, m)[:, D:2 * D], ALU.subtract
                                ).then_inc(S["q_ready"], 1)

            def queries(m, par):
                dve.wait_ge(S["ln_mm"], 2 * NT + m + 1)
                ge(dve, S["q_left"], m - 1)
                V.tensor_tensor(QF[:, par, :], ps[2 + par][:, 0:D], row["bq"][:, :], ALU.add).then_inc(S["ln_so"], 1)

            def query_step(n, par, i):
                dve.wait_ge(S["ln_pt"], 2 * NT + n + 1)
                dve.wait_ge(S["ln_mm"], 2 * NT + n - 1)
                V.tensor_copy(HT[:, par, :], ps[par][:, 0:D]).then_inc(S["ln_ht"], 1)
                for behind, part in ((1, queries), (2, less_first), (3, less_second)):
                    if not (isinstance(n, int) and n < behind):
                        part(n - behind, (par + behind) % 2)

            dve.wait_ge(S["breaks"], RUN_IN)
            each_node_tile(dve, query_step)
            queries(NT - 1, 0)
            less_first(NT - 2, 1)
            less_second(NT - 3, 0)
            less_first(NT - 1, 0)
            less_second(NT - 2, 1)
            less_second(NT - 1, 0)
            V.tensor_copy(run_br[:, :], run_b[:, ::-1]).then_inc(S["sel_ready"], 1)

            def products(i, par, u):
                U = CT // 2 * (2 * i + par) + u
                dve.wait_ge(S["qe_done"], U + 1)
                ge(dve, S["logit_pairs"], U - 1)
                dve.wait_ge(landed[par * CT // 2 + u], landed_before[par] + 32 * (i + 1))
                V.tensor_tensor(PR[u % 2], KV[:, par * CT + 2 * u:par * CT + 2 * u + 2, 0:D],
                                ps[u % 2][:, :].rearrange("p (t d) -> p t d", d=D), ALU.mult
                                ).then_inc(S["prod_done"], 1)

            def logits(i, par, u):
                dve.wait_ge(S["prod_done"], CT // 2 * (2 * i + par) + u + 1)
                V.tensor_reduce(L[:, par, 2 * u:2 * u + 2, :], PR[u % 2].rearrange(
                    "p t (h d) -> p t h d", d=HD), AX.X, ALU.add).then_inc(S["logit_pairs"], 1)

            def first_loc(i, par):
                dve.wait_ge(lb_in[par], 16 * (i + 1))
                ge(dve, S["cs_done"], 2 * i + par - 2)
                V.tensor_scalar(c_sel[:, par, :], iota_j[0:H, :], LB[0:H, par, 0:1], None, ALU.is_equal
                                ).then_inc(S["c_sel_r"], 1)

            def scan(out, breaks, values, initial, back):
                if back:
                    out, breaks, values = out[:, ::-1], breaks[:, ::-1], values[:, ::-1]
                return V.tensor_tensor_scan(out, breaks, values, initial, ALU.add, ALU.max)

            def forward_1(i, par, part):
                c = 2 * i + par
                if part == 0:
                    dve.wait_ge(brk_in[par], 16 * (i + 1))
                    dve.wait_ge(S["max_moved"], 6 * c + 1)
                    scan(F1s, BRK[:, par, 0:P], ps[2][:, 0:P], -BIG, False).then_inc(S["last_f"], 1)
                else:
                    dve.wait_ge(S["last_f"], 2 * c + 1)
                    V.tensor_scalar(ends[:, 0, :], sel_t[:, :], F1s[:, P - 1:P], None, ALU.mult
                                    ).then_inc(S["last_f"], 1)

            def forward_2(i, par, carried):
                c = 2 * i + par
                dve.wait_ge(S["max_moved"], 6 * c + 2)
                ge(dve, S["carry_f"], c)
                first = cf[:, 1 - par, CT - 1:CT] if carried else -BIG
                V.tensor_tensor_scan(cf[:, par, :], run_f[:, bass.ds(c * CT, CT)], ps[3][0:H, 128:128 + CT],
                                     first, ALU.add, ALU.max).then_inc(S["carry_f"], 1)

            def pick_start(k, at_, done, before_, part):
                if part == 0:
                    V.tensor_tensor(pick[:, k, :], ps[3][:, at_:at_ + CT], sel_t[:, :], ALU.mult).then_inc(done, 1)
                else:
                    dve.wait_ge(done, before_ + 1)
                    V.tensor_reduce(start[:, k:k + 1], pick[:, k, :], AX.X, ALU.add).then_inc(done, 1)

            def forward_3(i, par, part):
                c = 2 * i + par
                if part == 0:
                    dve.wait_ge(S["max_moved"], 6 * c + 3)
                if part < 2:
                    pick_start(0, 160, S["max_f"], 5 * c, part)
                    return
                dve.wait_ge(S["max_f"], 5 * c + part)
                if part == 2:
                    scan(F2s, BRK[:, par, 0:P], ps[2][:, 0:P], start[:, 0:1], False).then_inc(S["max_f"], 1)
                elif part == 3:
                    scan(B1s, BRK[:, par, P:2 * P], F2s, -BIG, True).then_inc(S["max_f"], 1)
                else:
                    V.tensor_scalar(ends[:, 1, :], sel_t[:, :], B1s[:, 0:1], None, ALU.mult).then_inc(S["max_f"], 1)

            def backward_2(i, par):
                c = 2 * i + par
                dve.wait_ge(S["max_moved"], 6 * c + 4)
                V.memset(cb[:, par, CT:CT + 1], -BIG)
                V.tensor_tensor_scan(cb[:, par, 0:CT][:, ::-1], run_br[:, bass.ds(T - (c + 1) * CT, CT)],
                                     ps[3][0:H, 192:192 + CT][:, ::-1], -BIG, ALU.add, ALU.max
                                     ).then_inc(S["carry_b"], 1)

            def backward_3(i, par, part):
                c = 2 * i + par
                if part == 0:
                    dve.wait_ge(S["max_moved"], 6 * c + 5)
                if part < 2:
                    pick_start(1, 224, S["max_b"], 3 * c, part)
                else:
                    dve.wait_ge(S["max_b"], 3 * c + 2)
                    scan(B2s, BRK[:, par, P:2 * P], F2s, start[:, 1:2], True).then_inc(S["max_b"], 1)

            def carry(i, par, part):
                c = 2 * i + par
                if part == 0:
                    dve.wait_ge(S["carry_b"], c + 1)
                    V.tensor_tensor(c_d[:, 0:1], cf[:, 1 - par, CT - 1:CT], cb[:, par, 0:1], ALU.subtract
                                    ).then_inc(S["c_diff"], 1)
                else:
                    dve.wait_ge(S["c_diff"], 2 * c - 1)
                    ge(dve, S["c_exp"], c - 1)
                    V.scalar_tensor_tensor(c_d[:, 2:3], BRK[0:H, par, 0:1], 0.0, c_d[:, 0:1], ALU.is_equal, ALU.mult
                                           ).then_inc(S["c_diff"], 1)

            def carry_diag(i, par):
                c = 2 * i + par
                dve.wait_ge(S["c_exp"], c)
                V.scalar_tensor_tensor(c_diag[:, par, :], ident[0:H, 0:H], c_s[:, par:par + 1], ident[0:H, 0:H],
                                       ALU.mult, ALU.subtract).then_inc(S["cs_ready"], 1)

            def minus_max(i, par):
                c = 2 * i + par
                dve.wait_ge(S["max_moved"], 6 * c + 6)
                ge(dve, S["ex_ready"], c)
                V.tensor_tensor(DF[:, :, :], L[:, par], ps[3][:, 0:P].rearrange("p (t h) -> p t h", h=H),
                                ALU.subtract).then_inc(S["df_ready"], 1)

            def rows(i, par, k):
                c = 2 * i + par
                ge(dve, S["ag_done"], CT * (c - 1) + 4 * (k + 1))
                dve.wait_ge(S["ex_ready"], c + 1)
                j = par * CT + 4 * k
                V.tensor_tensor(R[:, k, :, 0:D].rearrange("p t (h d) -> p t h d", d=HD),
                                KV[:, j:j + 4, D:2 * D].rearrange("p t (h d) -> p t h d", d=HD),
                                EX[:, par, 4 * k:4 * k + 4, :].unsqueeze(3).to_broadcast([P, 4, H, HD]),
                                ALU.mult).then_inc(S["r_ready"], 1)

            def rescale(i, par):
                c = 2 * i + par
                nt = node_tiles(c * CT)[0]
                dve.wait_ge(S["cs_done"], c)
                dve.wait_ge(S["ag_added"], CT * c)
                s_ = ACC[:, bass.ds(nt, 1), 0:D].rearrange("p a (h d) -> p (a h) d", d=HD)
                V.scalar_tensor_tensor(s_, ps[2][:, 256:256 + H].unsqueeze(2).to_broadcast([P, H, HD]), 1.0, s_,
                                       ALU.add, ALU.mult).then_inc(S["acc_scaled"], 1)
                d_ = ACC[:, bass.ds(nt, 1), D:AW].rearrange("p a h -> p (a h)")
                V.scalar_tensor_tensor(d_, ps[2][:, 256:256 + H], 1.0, d_, ALU.add, ALU.mult).then_inc(S["acc_scaled"], 1)

            def add(i, par, k, ts):
                c = 2 * i + par
                if ts[0] == 0 or (k, ts[0]) == (0, 2):
                    nt_of[:] = node_tiles(c * CT + 4 * k)
                if (k, ts[0]) == (0, 0):
                    ge(dve, S["acc_scaled"], 2 * c)
                for t in ts:
                    n = c * CT + 4 * k + t
                    dve.wait_ge(S["ag_done"], n + 1)
                    ge(dve, S["ag_added"], n)
                    s_ = ACC[:, bass.ds(nt_of[t], 1), :].rearrange("p a d -> p (a d)")
                    V.tensor_tensor(s_, ps[4 + t][:, 0:AW], s_, ALU.add).then_inc(S["ag_added"], 1)

            nt_of = [0] * 4

            def l1_step(i, par, has_c, p):
                pi, pp = before(i, par)

                def m(u):
                    if has_c:
                        products(i, par, u)

                def l(u):
                    if has_c:
                        logits(i, par, u)

                def a(k, *ts):
                    if p >= 2:
                        add(i - 1, par, k, ts)

                def y(f, *args):
                    if p >= 1:
                        f(pi, pp, *args)

                def z(f, *args):
                    if p >= 2:
                        f(pi, pp, *args)

                if has_c and not (isinstance(i, int) and 2 * i + par == C - 1):
                    if p >= 1:
                        stage_src(i + par, 1 - par)
                if p == 1:
                    dve.wait_ge(S["acc_clear"], 1)
                m(0), y(forward_1, 0), a(0, 2), y(forward_1, 1), l(0), a(0, 3)
                if has_c:
                    first_loc(i, par)
                y(forward_2, p >= 2), m(1), a(1, 0), y(forward_3, 0), l(1), y(forward_3, 1), a(1, 1)
                y(forward_3, 2), m(2), y(forward_3, 3), a(1, 2), y(forward_3, 4), l(2), a(1, 3)
                y(backward_2), m(3), a(2, 0), y(backward_3, 0), l(3), y(backward_3, 1), a(2, 1)
                y(backward_3, 2), z(carry, 0), m(4), z(carry, 1), a(2, 2), l(4), a(2, 3), y(minus_max)
                m(5), a(3, 0), y(rows, 0), z(carry_diag), a(3, 1), l(5), a(3, 2), y(rows, 1), a(3, 3)
                m(6), z(rescale), l(6), y(add, 0, [0]), m(7), y(add, 0, [1]), l(7)

            dve.wait_ge(S["sel_ready"], 5)
            each_l1_step(dve, l1_step)
            add(C // 2 - 1, 1, 0, [2, 3])
            for k in range(1, G4):
                add(C // 2 - 1, 1, k, range(4))

            def stats(k, src, ready, st, sd_used):
                def part(n, par, i):
                    dve.wait_ge(ready, n + 1)
                    ge(dve, sd_used, n)
                    V.bn_stats(fst[:, k, :], fin[src][:, par, :]).then_inc(st, 1)
                    ge_alone(dve, st, 2 * n + 1)
                    V.bn_aggr(fmv[:, k, :], fst[:, k, :]).then_inc(st, 1)
                return part

            def attention_sum(n, par, i):
                dve.wait_ge(S["f_skip"], n + 1)
                dve.wait_ge(S["f_att"], 2 * (n + 1))
                ge(dve, S["f_sapt"], n)
                V.tensor_tensor(f1["sa"][:, :], ps[1][:, 0:D], fin["att"][:, par, :], ALU.add
                                ).then_inc(S["f_sa"], 1)

            def residual(n, par, i):
                dve.wait_ge(S["f_wo"], n + 1)
                dve.wait_ge(S["f_hb"], n + 1)
                V.tensor_tensor(fin["y"][:, par, :], ps[3][:, 0:D], fin["hb"][:, par, :], ALU.add
                                ).then_inc(S["f_y"], 1)

            def residual2(n, par, i):
                dve.wait_ge(S["f_ff2"], n + 1)
                dve.wait_ge(S["f_zb"], n + 1)
                V.tensor_tensor(fin["y2"][:, par, :], ps[7][:, 0:D], fin["zb"][:, par, :], ALU.add
                                ).then_inc(S["f_y2"], 1)

            def norm1(n, par, i):
                dve.wait_ge(S["f_sd"], n + 1)
                V.reciprocal(frs[:, 0:1], fsd[:, 0:1]).then_inc(S["f_t"], 1)
                V.scalar_tensor_tensor(f1["t"][:, :], fin["y"][:, par, :], fmv[:, 0, 0:1], row["g1"][:, :],
                                       ALU.subtract, ALU.mult).then_inc(S["f_t"], 1)
                dve.wait_ge(S["f_t"], 2 * (n + 1))
                ge(dve, S["f_zpt"], n)
                ge(dve, S["f_zb"], n)
                V.scalar_tensor_tensor(f1["z"][:, :], f1["t"][:, :], frs[:, 0:1], row["be1"][:, :],
                                       ALU.mult, ALU.add).then_inc(S["f_z"], 1)

            def norm2(n, par, i):
                dve.wait_ge(S["f_sd2"], n + 1)
                V.reciprocal(frs[:, 1:2], fsd[:, 1:2]).then_inc(S["f_t2"], 1)
                V.scalar_tensor_tensor(f1["t2"][:, :], fin["y2"][:, par, :], fmv[:, 1, 0:1], row["g2"][:, :],
                                       ALU.subtract, ALU.mult).then_inc(S["f_t2"], 1)
                dve.wait_ge(S["f_t2"], 2 * (n + 1))
                dve.wait_ge(S["f_xb"], n + 1)
                ge(dve, out_stored[par], 16 * i)
                V.scalar_tensor_tensor(fin["out"][:, par, :], f1["t2"][:, :], frs[:, 1:2], fin["xo"][:, par, :],
                                       ALU.mult, ALU.add).then_inc(S["f_out"], 1)

            dve.wait_ge(S["ag_added"], T)
            V.tensor_scalar(RD[:, :, :], ACC[:, :, D:AW], 1e-16, None, ALU.add).then_inc(S["den_ready"], 1)
            dve.wait_ge(S["den_ready"], 1)
            V.reciprocal(RD[:, :, :], RD[:, :, :]).then_inc(S["den_ready"], 1)
            dve.wait_ge(S["fin_w"], 12 * 16)
            each_step(dve, [(-1, stats(1, "y2", S["f_y2"], S["f_st2"], S["f_sd2"])), (1, norm1),
                            (2, attention_sum), (-1, norm2), (2, residual),
                            (2, stats(0, "y", S["f_y"], S["f_st"], S["f_sd"])), (0, residual2)])

        @block.tensor
        def _(pe):
            mm, tr = nc.tensor.matmul, nc.tensor.transpose
            pe.wait_ge(S["consts"], 11)
            pe.wait_ge(S["chain"], NT)
            mm(ps[4][:, 0:NT], ones[0:125, :], cnt_p[0:125, :], start=True, stop=True).then_inc(S["total"], 1)

            def node_products(before, bank, w, width):
                def product(m, par):
                    pe.wait_ge(S["ln_ht"], before + m + 1)
                    ge(pe, S["ln_so"], before + m - 1)
                    for k in range(DK):
                        last = mm(ps[bank + par][:, 0:width], HT[:, par, k * P:(k + 1) * P], w[:, k, :],
                                  start=(k == 0), stop=(k == DK - 1))
                    last.then_inc(S["ln_mm"], 1)

                def step(n, par, i):
                    pe.wait_ge(S["ln_h"], before + n + 1)
                    ge(pe, S["ln_ht"], before + n - 1)
                    for k in range(DK):
                        last = tr(ps[par][:, k * P:(k + 1) * P], Hn[:, par, k * P:(k + 1) * P], ident[:, :])
                    last.then_inc(S["ln_pt"], 1)
                    if not (isinstance(n, int) and n == 0):
                        product(n - 1, 1 - par)

                each_node_tile(pe, step)
                product(NT - 1, 0)

            pe.wait_ge(S["w0_in"], 16)
            node_products(0, 2, W0, D)

            pe.wait_ge(S["tr_in"], 1)
            for bank, t_ in ((5, loc_m), (6, src_f), (7, w_r.bitcast(f32))):
                for k in range(TG):
                    last = tr(ps[bank][:, k * TP:(k + 1) * TP], t_[0:TP, k, :], ident[0:TP, 0:TP])
            last.then_inc(S["tr_out"], 1)

            pe.wait_ge(S["ln_so"], NT)

            def sums0(i, par):
                c = 2 * i + par
                for j in range(CT):
                    n = CT * c + j
                    if j % 4 == 0:
                        pe.wait_ge(S["onehot0"], G4 * c + j // 4 + 1)
                    if j % 2 == 0:
                        pe.wait_ge(landed[j // 2], 32 * (c + 1))
                    ge(pe, S["l0_added"], n - 3)
                    mm(ps[j % 4][:, 0:D], A[:, j // 4 % 2, j % 4, :], G0[:, j, :], start=True, stop=True
                       ).then_inc(S["l0_mm"], 1)

            each_chunk(pe, sums0)

            pe.wait_ge(S["rows_in"], 6 * 16)
            pe.wait_ge(S["l0_added"], T)
            node_products(NT, 4, WKV, 2 * D)
            node_products(2 * NT, 2, WQ, D)
            pe.wait_ge(S["q_ready"], NT)

            regs = [pe.alloc_register(f"pe_nt{k}") for k in range(4)]

            nt_of = [0] * 4

            def queries(i, par, u):
                c = 2 * i + par
                k = u // 2
                if u % 2 == 0:
                    pe.load(regs, nt_row[0:1, bass.ds(c * CT + 4 * k, 4)])
                    nt_of[:] = [pe.snap(r, min_val=0, max_val=NT - 1) for r in regs]
                    pe.wait_ge(S["ot_ready"], G4 * c + k + 1)
                ge(pe, S["prod_done"], CT // 2 * c + u - 1)
                for t in range(2):
                    e = 2 * (u % 2) + t
                    parts = (node(QHM, nt_of[e])[:, 0:D], node(QHM, nt_of[e])[:, D:2 * D], node(QLO, nt_of[e]))
                    for x, part in enumerate(parts):
                        last = mm(ps[u % 2][:, t * D:(t + 1) * D], OT[:, k % 2, e, :], part,
                                  start=(x == 0), stop=(x == 2))
                last.then_inc(S["qe_done"], 1)

            def logits_across(i, par):
                c = 2 * i + par
                pe.wait_ge(S["logit_pairs"], CT // 2 * (c + 1))
                ge(pe, S["max_f"], 5 * c - 2)
                ge(pe, S["acc_scaled"], 2 * (c - 1))
                tr(ps[2][:, 0:P], L[:, par].rearrange("p t h -> p (t h)"), ident[:, :]).then_inc(S["max_moved"], 1)

            def to_heads(k, ready, count):
                pe.wait_ge(ready, count)
                mm(ps[3][0:H, 128 + 64 * k:128 + 64 * k + CT], sel_h[:, :], ends[:, k, :], start=True, stop=True
                   ).then_inc(S["max_moved"], 1)

            def to_tiles(par, k, ready, count, carried):
                pe.wait_ge(ready, count)
                o_ = 160 + 64 * k
                sel = sel_hT[:, :, :].rearrange("a t h -> a (t h)")
                if k == 0:
                    mm(ps[3][:, o_ + 1:o_ + CT], sel, cf[:, par, 0:CT - 1], start=True, stop=True)
                    first = cf[:, 1 - par, CT - 1:CT] if carried else below[:, :]
                    mm(ps[3][:, o_:o_ + 1], sel, first, start=True, stop=True).then_inc(S["max_moved"], 1)
                else:
                    mm(ps[3][:, o_:o_ + CT], sel, cb[:, par, 1:CT + 1], start=True, stop=True).then_inc(S["max_moved"], 1)

            def max_by_edge(i, par):
                c = 2 * i + par
                pe.wait_ge(S["max_b"], 3 * c + 3)
                ge(pe, S["df_ready"], c)
                tr(ps[3][:, 0:P], B2s, ident[:, :]).then_inc(S["max_moved"], 1)

            def carry(i, par):
                c = 2 * i + par
                pe.wait_ge(S["cs_ready"], c)
                pe.wait_ge(S["c_sel_r"], c + 1)
                ge(pe, S["acc_scaled"], 2 * (c - 1))
                mm(ps[2][:, 256:256 + H], c_sel[:, par, :], c_diag[:, par, :], start=True, stop=True
                   ).then_inc(S["cs_done"], 1)

            def sums(i, par, k, ts):
                G = G4 * (2 * i + par) + k
                if ts[0] == 0:
                    pe.wait_ge(S["a1_ready"], G + 1)
                    pe.wait_ge(S["r_ready" if k < 2 else "r_ready_2"], 2 * (2 * i + par) + k % 2 + 1)
                    pe.wait_ge(S["rden_ready"], G + 1)
                for t in ts:
                    ge(pe, S["ag_added"], 4 * G + t - 3)
                    mm(ps[4 + t][:, 0:AW], A[:, k % 2, t, :], R[:, k, t, :], start=True, stop=True
                       ).then_inc(S["ag_done"], 1)

            def l1_step(i, par, has_c, p):
                c = 2 * i + par
                pi, pp = before(i, par)

                def q(u):
                    if has_c:
                        queries(i, par, u)

                def s(k, *ts):
                    if p >= 2:
                        sums(i - 1, par, k, ts)

                if p == 0:
                    q(0), q(1)
                if p >= 1:
                    to_heads(0, S["last_f"], 2 * c)
                s(1, 2)
                if p >= 1:
                    to_tiles(pp, 0, S["carry_f"], c, p >= 2)
                q(2), s(1, 3), q(3)
                if p >= 1:
                    to_heads(1, S["max_f"], 5 * c)
                s(2, 0)
                if p >= 1:
                    to_tiles(pp, 1, S["carry_b"], c, p >= 2)
                s(2, 1), q(4), s(2, 2), q(5), s(2, 3), s(3, 0)
                if p >= 1:
                    max_by_edge(pi, pp)
                s(3, 1), q(6), s(3, 2), q(7), s(3, 3)
                if p >= 2:
                    carry(pi, pp)
                if p >= 1:
                    sums(pi, pp, 0, range(4))
                has_next = has_c and not (isinstance(i, int) and c == C - 1)
                if has_next:
                    queries(i + par, 1 - par, 0)
                if p >= 1:
                    sums(pi, pp, 1, [0])
                if has_next:
                    queries(i + par, 1 - par, 1)
                if p >= 1:
                    sums(pi, pp, 1, [1])
                if has_c:
                    logits_across(i, par)

            each_l1_step(pe, l1_step)
            sums(C // 2 - 1, 1, 1, [2, 3])
            for k in (2, 3):
                sums(C // 2 - 1, 1, k, range(4))

            def across(bank, t_, s_):
                for k in range(DK):
                    last = tr(ps[bank][:, k * P:(k + 1) * P], t_[:, k * P:(k + 1) * P], ident[:, :])
                last.then_inc(s_, 1)

            def times(bank, tT, w, s_):
                for k in range(DK):
                    last = mm(ps[bank][:, 0:D], tT[:, k * P:(k + 1) * P], w[:, k, :], start=(k == 0), stop=(k == DK - 1))
                last.then_inc(s_, 1)

            def rows_across(n, par, i):
                pe.wait_ge(S["f_h"], n + 1)
                ge(pe, S["f_hT"], n)
                across(0, fin["h"][:, par, :], S["f_pt"])

            def skip(n, par, i):
                pe.wait_ge(S["f_hT"], n + 1)
                ge(pe, S["f_sa"], n)
                times(1, f1["hT"][:, :], WS, S["f_skip"])

            def attention_across(n, par, i):
                pe.wait_ge(S["f_sa"], n + 1)
                ge(pe, S["f_saT"], n)
                across(2, f1["sa"][:, :], S["f_sapt"])

            def output(n, par, i):
                pe.wait_ge(S["f_saT"], n + 1)
                ge(pe, S["f_y"], n)
                times(3, f1["saT"][:, :], WO, S["f_wo"])

            def z_across(n, par, i):
                pe.wait_ge(S["f_z"], n + 1)
                ge(pe, S["f_zT"], n)
                across(4, f1["z"][:, :], S["f_zpt"])

            def up(part):
                def half(n, par, i):
                    pe.wait_ge(S["f_zT"], n + 1)
                    ge(pe, S["f_relu"], 2 * (n - 1) + part + 1)
                    for m in range(4 * part, 4 * part + 4):
                        for k in range(DK):
                            last = mm(ps[5 + part][:, m % 4 * P:(m % 4 + 1) * P], W1[:, k, m * P:(m + 1) * P],
                                      fin["zT"][:, par, k * P:(k + 1) * P], start=(k == 0), stop=(k == DK - 1))
                    last.then_inc(S["f_ff1"], 1)
                return half

            def down(part):
                def half(n, par, i):
                    if part == 0:
                        ge(pe, S["f_y2"], n)
                    pe.wait_ge(S["f_relu"], 2 * n + part + 1)
                    for m in range(4 * part, 4 * part + 4):
                        last = mm(ps[7][:, 0:D], F1[:, m, :], W2[:, m, :], start=(m == 0), stop=(m == FK - 1))
                    if part:
                        last.then_inc(S["f_ff2"], 1)
                return half

            pe.wait_ge(S["fin_w"], 12 * 16)
            pe.wait_ge(S["ag_added"], T)
            each_step(pe, [(2, rows_across), (0, up(0)), (2, skip), (0, up(1)), (2, attention_across),
                           (1, z_across), (0, down(0)), (2, output), (0, down(1))])


def kernel(**inputs):
    import numpy as _np
    import concourse.bacc as _bacc
    from concourse import mybir as _mybir
    from concourse.bass_utils import run_bass_kernel_spmd as _run

    nc = _bacc.Bacc("TRN2", target_bir_lowering=False, num_devices=1)
    arrays, args = {}, {}
    for name, value in inputs.items():
        v = _np.ascontiguousarray(value)
        arrays[f"in_{name}"] = v
        args[name] = nc.dram_tensor(f"in_{name}", v.shape, _mybir.dt.from_np(v.dtype), kind="ExternalInput").ap()
    x = args["x"]
    out = nc.dram_tensor("out_x", x.shape, _mybir.dt.float32, kind="ExternalOutput").ap()
    gnn_two_layers(nc, args, out)
    r = _run(nc, [arrays], core_ids=[0])
    return r.results[0]["out_x"]
```
